# Optimizing a Trainium2 kernel written in Bass

```python
import numpy as np
import jax
import jax.numpy as jnp

def _softmax(x, axis=-1):
    return jax.nn.softmax(x, axis=axis)

def _gelu(x):
    return jax.nn.gelu(x, approximate=True)

def _silu(x):
    return jax.nn.silu(x)

def _sigmoid(x):
    return jax.nn.sigmoid(x)

def _layernorm(x, axis=-1, eps=1e-05):
    m = jnp.mean(x, axis=axis, keepdims=True)
    v = jnp.var(x, axis=axis, keepdims=True)
    return (x - m) / jnp.sqrt(v + eps)

def _scatter_add(tgt, idx, src, axis=0):
    return tgt.at[idx].add(src)

def _segment_sum(src, seg, n):
    return jax.ops.segment_sum(src, seg, n)
kernel_name = 'mk_gps_d2_gnn_r8_b282c4'

def setup_inputs(seed: int=0):
    np.random.seed(seed)
    _w = jnp.asarray

    def _rec_inputs():
        import jax
        import jax.numpy as jnp
        _gk = jax.random.key(seed)
        x = -6.415e-05 + 1 * jax.random.normal(jax.random.fold_in(_gk, 1), (1250, 1024), jnp.float32)
        src = jax.random.randint(jax.random.fold_in(_gk, 2), (40000,), 0, 1250, jnp.int32)
        dst = jnp.minimum((1250 * jax.random.uniform(jax.random.fold_in(_gk, 3), (40000,)) ** 2.0).astype(jnp.int32), 9999)
        _o = jnp.argsort(dst, stable=True)
        src = src[_o]
        dst = dst[_o]
        return (x, src, dst)
    x, src, dst = _rec_inputs()

    def _L0_gnn_setup():
        import jax, jax.numpy as jnp
        import numpy as np
        NEG_SLOPE = 0.1
        EPS = 1e-05
        key = jax.random.key(seed)
        k1, k2, k3, k4, k5 = jax.random.split(key, 5)
        N, E, DIN, DOUT = (1250, 20000, 1024, 1024)
        x = jax.random.normal(k1, (N, DIN), dtype=jnp.float32)
        W = jax.random.normal(k2, (DIN, DOUT), dtype=jnp.float32) * 0.02
        a = jax.random.normal(k3, (1, 2 * DOUT), dtype=jnp.float32) * 0.02
        src = jax.random.randint(k4, (E,), 0, N, dtype=jnp.int64)
        dst = jax.random.randint(k5, (E,), 0, N, dtype=jnp.int64)
        return {'x': x, 'W': W, 'a': a, 'src': src, 'dst': dst}
    _L0_gnn_all = _L0_gnn_setup()
    _L0_gnn_in = {k: v for k, v in _L0_gnn_all.items() if k in ('W', 'a')}
    del _L0_gnn_all

    def _L0_mix_setup():
        import math
        import jax, jax.numpy as jnp
        import numpy as np
        H = 1024
        NH = 16
        HD = H // NH
        FF = 512
        EPS = 1e-12

        def _lin(key, fan_in, fan_out):
            k1, k2 = jax.random.split(key)
            bound = 1.0 / math.sqrt(fan_in)
            W = jax.random.uniform(k1, (fan_in, fan_out), jnp.float32, -bound, bound)
            b = jax.random.uniform(k2, (fan_out,), jnp.float32, -bound, bound)
            return (W, b)

        def _layernorm(x, g, b):
            mu = jnp.mean(x, axis=-1, keepdims=True)
            var = jnp.mean((x - mu) ** 2, axis=-1, keepdims=True)
            return (x - mu) * jax.lax.rsqrt(var + EPS) * g + b

        def _gelu(x):
            return x * 0.5 * (1.0 + jax.lax.erf(x / jnp.sqrt(jnp.float32(2.0))))
        key = jax.random.key(seed)
        ks = jax.random.split(key, 8)
        x = jax.random.normal(ks[0], (4, 512, H), jnp.float32)
        Wq, bq = _lin(ks[1], H, H)
        Wk, bk = _lin(ks[2], H, H)
        Wv, bv = _lin(ks[3], H, H)
        Wo, bo = _lin(ks[4], H, H)
        W1, b1 = _lin(ks[5], H, FF)
        W2, b2 = _lin(ks[6], FF, H)
        g1 = jnp.ones((H,), jnp.float32)
        be1 = jnp.zeros((H,), jnp.float32)
        g2 = jnp.ones((H,), jnp.float32)
        be2 = jnp.zeros((H,), jnp.float32)
        return dict(x=x, Wq=Wq, bq=bq, Wk=Wk, bk=bk, Wv=Wv, bv=bv, Wo=Wo, bo=bo, g1=g1, be1=be1, W1=W1, b1=b1, W2=W2, b2=b2, g2=g2, be2=be2)
    _L0_mix_all = _L0_mix_setup()
    _L0_mix_in = {k: v for k, v in _L0_mix_all.items() if k in ('Wq', 'bq', 'Wk', 'bk', 'Wv', 'bv', 'Wo', 'bo', 'g1', 'be1', 'W1', 'b1', 'W2', 'b2', 'g2', 'be2')}
    del _L0_mix_all

    def _L0_ffn_setup():
        import jax, jax.numpy as jnp
        import numpy as np
        B, S, D, E, H = (2, 1024, 1024, 16, 256)
        TOP_K = 2
        TEMP = 1.0
        key = jax.random.key(seed)
        ks = jax.random.split(key, 4)
        sc_d = 1.0 / np.sqrt(D)
        sc_h = 1.0 / np.sqrt(H)
        return {'x': jax.random.normal(ks[0], (B, S, D), dtype=jnp.float32), 'Wr': jax.random.normal(ks[1], (D, E), dtype=jnp.float32) * sc_d, 'br': jnp.zeros((E,), dtype=jnp.float32), 'W1': jax.random.normal(ks[2], (E, D, H), dtype=jnp.float32) * sc_d, 'b1': jnp.zeros((E, H), dtype=jnp.float32), 'W2': jax.random.normal(ks[3], (E, H, D), dtype=jnp.float32) * sc_h, 'b2': jnp.zeros((E, D), dtype=jnp.float32)}
    _L0_ffn_all = _L0_ffn_setup()
    _L0_ffn_in = {k: v for k, v in _L0_ffn_all.items() if k in ('Wr', 'br', 'W1', 'b1', 'W2', 'b2')}
    del _L0_ffn_all

    def _L1_gnn_setup():
        import jax, jax.numpy as jnp
        import numpy as np
        N = 2500
        E = 40000
        IN = 1024
        HID = 256
        H = 4
        D = HID // H
        OUT = 1024
        EPS = 1e-06
        NEG_SLOPE = 0.2
        key = jax.random.key(seed)
        ks = jax.random.split(key, 8)
        x = jax.random.normal(ks[0], (N, IN), dtype=jnp.float32)
        edge_index = jax.random.randint(ks[1], (2, E), 0, N, dtype=jnp.int64)
        s = 0.02
        return {'x': x, 'edge_index': edge_index, 'rms_w': jnp.ones((IN,), dtype=jnp.float32), 'W_down': jax.random.normal(ks[2], (IN, HID), dtype=jnp.float32) * s, 'Wl': jax.random.normal(ks[3], (HID, HID), dtype=jnp.float32) * s, 'Wr': jax.random.normal(ks[4], (HID, HID), dtype=jnp.float32) * s, 'att': jax.random.normal(ks[5], (H, D), dtype=jnp.float32) * s, 'W_up': jax.random.normal(ks[6], (HID, OUT), dtype=jnp.float32) * s}
    _L1_gnn_all = _L1_gnn_setup()
    _L1_gnn_in = {k: v for k, v in _L1_gnn_all.items() if k in ('rms_w', 'W_down', 'Wl', 'Wr', 'att', 'W_up')}
    del _L1_gnn_all

    def _L1_mix_setup():
        import jax, jax.numpy as jnp
        import numpy as np
        DIM = 1024
        NUM_HEADS = 16
        HEAD_DIM = DIM // NUM_HEADS
        key = jax.random.key(seed)
        k1, k2, k3, k4 = jax.random.split(key, 4)
        x = jax.random.normal(k1, (4, 512, DIM), dtype=jnp.float32)
        W_qkv = jax.random.normal(k2, (DIM, 3 * DIM), dtype=jnp.float32) * DIM ** (-0.5)
        W_proj = jax.random.normal(k3, (DIM, DIM), dtype=jnp.float32) * DIM ** (-0.5)
        b_proj = jax.random.normal(k4, (DIM,), dtype=jnp.float32) * 0.01
        return {'x': x, 'W_qkv': W_qkv, 'W_proj': W_proj, 'b_proj': b_proj}
    _L1_mix_all = _L1_mix_setup()
    _L1_mix_in = {k: v for k, v in _L1_mix_all.items() if k in ('W_qkv', 'W_proj', 'b_proj')}
    del _L1_mix_all

    def _L1_ffn_setup():
        import jax, jax.numpy as jnp
        import numpy as np

        def _binarize(w):
            alpha = jax.lax.stop_gradient(jnp.mean(jnp.abs(w), axis=1, keepdims=True))
            bw = alpha * jnp.sign(w)
            return w + jax.lax.stop_gradient(bw - w)
        key = jax.random.key(seed)
        k1, k2, k3, k4, k5 = jax.random.split(key, 5)
        D, H = (1024, 512)
        x = jax.random.normal(k1, (64, 196, D), dtype=jnp.float32)
        w1 = jax.random.normal(k2, (H, D), dtype=jnp.float32) * 0.02
        b1 = jax.random.normal(k3, (H,), dtype=jnp.float32) * 0.02
        w2 = jax.random.normal(k4, (D, H), dtype=jnp.float32) * 0.02
        b2 = jax.random.normal(k5, (D,), dtype=jnp.float32) * 0.02
        return {'x': x, 'w1': w1, 'b1': b1, 'w2': w2, 'b2': b2}
    _L1_ffn_all = _L1_ffn_setup()
    _L1_ffn_in = {k: v for k, v in _L1_ffn_all.items() if k in ('w1', 'b1', 'w2', 'b2')}
    del _L1_ffn_all
    return {'x': x, 'src': src, 'dst': dst, 'L0_gnn_W': _L0_gnn_in['W'], 'L0_gnn_a': _L0_gnn_in['a'], 'L0_mix_Wq': _L0_mix_in['Wq'], 'L0_mix_bq': _L0_mix_in['bq'], 'L0_mix_Wk': _L0_mix_in['Wk'], 'L0_mix_bk': _L0_mix_in['bk'], 'L0_mix_Wv': _L0_mix_in['Wv'], 'L0_mix_bv': _L0_mix_in['bv'], 'L0_mix_Wo': _L0_mix_in['Wo'], 'L0_mix_bo': _L0_mix_in['bo'], 'L0_mix_g1': _L0_mix_in['g1'], 'L0_mix_be1': _L0_mix_in['be1'], 'L0_mix_W1': _L0_mix_in['W1'], 'L0_mix_b1': _L0_mix_in['b1'], 'L0_mix_W2': _L0_mix_in['W2'], 'L0_mix_b2': _L0_mix_in['b2'], 'L0_mix_g2': _L0_mix_in['g2'], 'L0_mix_be2': _L0_mix_in['be2'], 'L0_ffn_Wr': _L0_ffn_in['Wr'], 'L0_ffn_br': _L0_ffn_in['br'], 'L0_ffn_W1': _L0_ffn_in['W1'], 'L0_ffn_b1': _L0_ffn_in['b1'], 'L0_ffn_W2': _L0_ffn_in['W2'], 'L0_ffn_b2': _L0_ffn_in['b2'], 'L1_gnn_rms_w': _L1_gnn_in['rms_w'], 'L1_gnn_W_down': _L1_gnn_in['W_down'], 'L1_gnn_Wl': _L1_gnn_in['Wl'], 'L1_gnn_Wr': _L1_gnn_in['Wr'], 'L1_gnn_att': _L1_gnn_in['att'], 'L1_gnn_W_up': _L1_gnn_in['W_up'], 'L1_mix_W_qkv': _L1_mix_in['W_qkv'], 'L1_mix_W_proj': _L1_mix_in['W_proj'], 'L1_mix_b_proj': _L1_mix_in['b_proj'], 'L1_ffn_w1': _L1_ffn_in['w1'], 'L1_ffn_b1': _L1_ffn_in['b1'], 'L1_ffn_w2': _L1_ffn_in['w2'], 'L1_ffn_b2': _L1_ffn_in['b2']}

def reference(x, src, dst, L0_gnn_W, L0_gnn_a, L0_mix_Wq, L0_mix_bq, L0_mix_Wk, L0_mix_bk, L0_mix_Wv, L0_mix_bv, L0_mix_Wo, L0_mix_bo, L0_mix_g1, L0_mix_be1, L0_mix_W1, L0_mix_b1, L0_mix_W2, L0_mix_b2, L0_mix_g2, L0_mix_be2, L0_ffn_Wr, L0_ffn_br, L0_ffn_W1, L0_ffn_b1, L0_ffn_W2, L0_ffn_b2, L1_gnn_rms_w, L1_gnn_W_down, L1_gnn_Wl, L1_gnn_Wr, L1_gnn_att, L1_gnn_W_up, L1_mix_W_qkv, L1_mix_W_proj, L1_mix_b_proj, L1_ffn_w1, L1_ffn_b1, L1_ffn_w2, L1_ffn_b2):
    import jax
    import jax.numpy as jnp

    def _L0_gnn_ref(x, W, a, src, dst):
        import jax, jax.numpy as jnp
        import numpy as np
        NEG_SLOPE = 0.1
        EPS = 1e-05
        N = x.shape[0]
        d = W.shape[1]
        h = x @ W
        a_l, a_r = (a[0, :d], a[0, d:])
        al = h @ a_l
        ar = h @ a_r
        e = jnp.exp(-jax.nn.leaky_relu(al[src] + ar[dst], negative_slope=NEG_SLOPE))
        rowsum = jax.ops.segment_sum(e, src, num_segments=N)
        h_prime = jax.ops.segment_sum(e[:, None] * h[dst], src, num_segments=N)
        h_prime = h_prime / (rowsum[:, None] + EPS)
        return jax.nn.elu(h_prime)

    def _L0_mix_ref(x, Wq, bq, Wk, bk, Wv, bv, Wo, bo, g1, be1, W1, b1, W2, b2, g2, be2):
        import math
        import jax, jax.numpy as jnp
        import numpy as np
        H = 1024
        NH = 16
        HD = H // NH
        FF = 512
        EPS = 1e-12

        def _lin(key, fan_in, fan_out):
            k1, k2 = jax.random.split(key)
            bound = 1.0 / math.sqrt(fan_in)
            W = jax.random.uniform(k1, (fan_in, fan_out), jnp.float32, -bound, bound)
            b = jax.random.uniform(k2, (fan_out,), jnp.float32, -bound, bound)
            return (W, b)

        def _layernorm(x, g, b):
            mu = jnp.mean(x, axis=-1, keepdims=True)
            var = jnp.mean((x - mu) ** 2, axis=-1, keepdims=True)
            return (x - mu) * jax.lax.rsqrt(var + EPS) * g + b

        def _gelu(x):
            return x * 0.5 * (1.0 + jax.lax.erf(x / jnp.sqrt(jnp.float32(2.0))))
        B, S, _ = x.shape

        def heads(W, b):
            return (x @ W + b).reshape(B, S, NH, HD).transpose(0, 2, 1, 3)
        q, k, v = (heads(Wq, bq), heads(Wk, bk), heads(Wv, bv))
        eq = jax.nn.elu(q)
        ek = jax.nn.elu(k)
        qn = eq / jnp.linalg.norm(eq, axis=-1, keepdims=True)
        kn = ek / jnp.linalg.norm(ek, axis=-1, keepdims=True)
        kv = jnp.einsum('bhsd,bhse->bhde', kn, v)
        ctx = jnp.einsum('bhsd,bhde->bhse', qn, kv) / jnp.float32(math.sqrt(HD))
        ctx = ctx.transpose(0, 2, 1, 3).reshape(B, S, H)
        attn_out = _layernorm(ctx @ Wo + bo + x, g1, be1)
        h = _gelu(attn_out @ W1 + b1)
        out = _layernorm(h @ W2 + b2 + attn_out, g2, be2)
        return out

    def _L0_ffn_ref(x, Wr, br, W1, b1, W2, b2):
        import jax, jax.numpy as jnp
        import numpy as np
        B, S, D, E, H = (2, 1024, 1024, 16, 256)
        TOP_K = 2
        TEMP = 1.0
        token_shape = x.shape[:-1]
        d = x.shape[-1]
        xt = x.reshape(-1, d)
        T = xt.shape[0]
        logits = (xt @ Wr + br) / TEMP
        probs = jax.nn.softmax(logits, axis=-1)
        w, idx = jax.lax.top_k(probs, TOP_K)
        w = w / jnp.clip(jnp.sum(w, axis=-1, keepdims=True), 1e-09)
        comb = jnp.zeros((T, E), dtype=xt.dtype)
        comb = comb.at[jnp.arange(T)[:, None], idx].add(w)
        h = jax.nn.gelu(jnp.einsum('td,edh->teh', xt, W1) + b1, approximate=False)
        o = jnp.einsum('teh,eho->teo', h, W2) + b2
        y = jnp.einsum('teo,te->to', o, comb)
        y = xt + y
        return y.reshape(*token_shape, d)

    def _L1_gnn_ref(x, edge_index, rms_w, W_down, Wl, Wr, att, W_up):
        import jax, jax.numpy as jnp
        import numpy as np
        N = 2500
        E = 40000
        IN = 1024
        HID = 256
        H = 4
        D = HID // H
        OUT = 1024
        EPS = 1e-06
        NEG_SLOPE = 0.2
        n = x.shape[0]
        ms = jnp.mean(jnp.square(x), axis=-1, keepdims=True)
        x = x * jax.lax.rsqrt(ms + EPS) * rms_w
        x = x @ W_down
        loop = jnp.arange(n, dtype=edge_index.dtype)
        src = jnp.concatenate([edge_index[0], loop])
        dst = jnp.concatenate([edge_index[1], loop])
        xl = (x @ Wl).reshape(n, H, D)
        xr = (x @ Wr).reshape(n, H, D)
        msg = xl[src] + xr[dst]
        act = jnp.where(msg > 0, msg, NEG_SLOPE * msg)
        e = jnp.einsum('ehd,hd->eh', act, att)
        m = jax.ops.segment_max(e, dst, num_segments=n)
        p = jnp.exp(e - m[dst])
        denom = jax.ops.segment_sum(p, dst, num_segments=n)
        alpha = p / (denom[dst] + 1e-16)
        out = jax.ops.segment_sum(alpha[..., None] * xl[src], dst, num_segments=n)
        out = out.reshape(n, HID)
        return out @ W_up

    def _L1_mix_ref(x, W_qkv, W_proj, b_proj):
        import jax, jax.numpy as jnp
        import numpy as np
        DIM = 1024
        NUM_HEADS = 16
        HEAD_DIM = DIM // NUM_HEADS
        B, N, C = x.shape
        H, D = (NUM_HEADS, HEAD_DIM)
        qkv = (x @ W_qkv).reshape(B, N, 3, H, D)
        qkv = jnp.transpose(qkv, (2, 0, 3, 1, 4))
        q, k, v = (qkv[0], qkv[1], qkv[2])
        q = jax.nn.elu(q) + 1.0
        k = jax.nn.elu(k) + 1.0
        kv = jnp.einsum('bhnd,bhne->bhde', k, v)
        z = 1.0 / (jnp.einsum('bhnd,bhd->bhn', q, k.sum(axis=2)) + 1e-06)
        out = jnp.einsum('bhnd,bhde->bhne', q, kv) * z[..., None]
        out = jnp.transpose(out, (0, 2, 1, 3)).reshape(B, N, C)
        return out @ W_proj + b_proj

    def _L1_ffn_ref(x, w1, b1, w2, b2):
        import jax, jax.numpy as jnp
        import numpy as np

        def _binarize(w):
            alpha = jax.lax.stop_gradient(jnp.mean(jnp.abs(w), axis=1, keepdims=True))
            bw = alpha * jnp.sign(w)
            return w + jax.lax.stop_gradient(bw - w)
        bw1 = _binarize(w1)
        h = jnp.einsum('bsd,hd->bsh', x, bw1) + b1
        h = jax.nn.gelu(h, approximate=False)
        bw2 = _binarize(w2)
        out = jnp.einsum('bsh,dh->bsd', h, bw2) + b2
        return out
    edge_index = jnp.stack([src, dst])
    xn = _layernorm(x, axis=-1)
    x = x + _L0_gnn_ref(xn, L0_gnn_W, L0_gnn_a, src, dst) + _L0_mix_ref(xn[None], L0_mix_Wq, L0_mix_bq, L0_mix_Wk, L0_mix_bk, L0_mix_Wv, L0_mix_bv, L0_mix_Wo, L0_mix_bo, L0_mix_g1, L0_mix_be1, L0_mix_W1, L0_mix_b1, L0_mix_W2, L0_mix_b2, L0_mix_g2, L0_mix_be2)[0]
    x = x + _L0_ffn_ref(_layernorm(x, axis=-1)[None], L0_ffn_Wr, L0_ffn_br, L0_ffn_W1, L0_ffn_b1, L0_ffn_W2, L0_ffn_b2)[0]
    xn = _layernorm(x, axis=-1)
    x = x + _L1_gnn_ref(xn, edge_index, L1_gnn_rms_w, L1_gnn_W_down, L1_gnn_Wl, L1_gnn_Wr, L1_gnn_att, L1_gnn_W_up) + _L1_mix_ref(xn[None], L1_mix_W_qkv, L1_mix_W_proj, L1_mix_b_proj)[0]
    x = x + _L1_ffn_ref(_layernorm(x, axis=-1)[None], L1_ffn_w1, L1_ffn_b1, L1_ffn_w2, L1_ffn_b2)[0]
    return x

_drawn_inputs = setup_inputs


def setup_inputs(seed=0):
    import zlib

    import numpy as np

    out = dict(_drawn_inputs(seed))
    spreads = {'L0_mix_g1': (1.0, 0.2),
     'L0_mix_be1': (0.0, 0.1),
     'L0_mix_g2': (1.0, 0.2),
     'L0_mix_be2': (0.0, 0.1),
     'L0_ffn_br': (0.0, 0.1),
     'L0_ffn_b1': (0.0, 0.484),
     'L0_ffn_b2': (0.0, 0.328),
     'L1_gnn_rms_w': (1.0, 0.6)}
    factors = {'L0_gnn_a': 2.793,
     'L0_mix_bq': 5.808,
     'L0_mix_bk': 6.34,
     'L0_mix_bo': 3.708,
     'L0_mix_b1': 8.0,
     'L0_mix_b2': 2.863,
     'L1_gnn_W_down': 8.0,
     'L1_gnn_Wl': 8.0,
     'L1_gnn_Wr': 8.0,
     'L1_gnn_att': 8.0,
     'L1_gnn_W_up': 8.0,
     'L1_mix_b_proj': 200.0,
     'L1_ffn_b1': 64.0,
     'L1_ffn_b2': 64.0,
     'L1_mix_W_qkv': 8.0,
     'L1_mix_W_proj': 8.0,
     'L1_ffn_w1': 8.0,
     'L1_ffn_w2': 8.0}
    for name, (base, spread) in spreads.items():
        noise = np.random.default_rng([zlib.crc32(name.encode()), seed]).standard_normal(out[name].shape)
        drawn = base * np.exp(spread * noise) if base else spread * noise
        out[name] = jnp.asarray(drawn.astype(out[name].dtype))
    for name, factor in factors.items():
        out[name] = (out[name] * factor).astype(out[name].dtype)
    return out
```

```python
from contextlib import ExitStack

import concourse.bass as bass
from concourse import mybir

F32 = mybir.dt.float32
F16 = mybir.dt.float16
BF16 = mybir.dt.bfloat16
I32 = mybir.dt.int32
U32 = mybir.dt.uint32
ALU = mybir.AluOpType
ACT = mybir.ActivationFunctionType
AX = mybir.AxisListType
ds = bass.ds

N = 1250
P = 125
NT = N // P
D = 1024
KD = D // 128
CW = 256
NC = D // CW
E = 40000
SUB = 8
BE = SUB * P
NB = E // BE
HB = SUB // 2
FCH = [(0, 500), (500, 500), (1000, 250)]
NEXP = 16
EH = 256
HID = 256
GH = 4
GD = HID // GH
BIG = 1e30
COLS = {"L0_mix_bq": (0, 8), "L0_mix_b1": (8, 4), "L0_ffn_b1": (12, 32), "L1_ffn_b1": (44, 4),
        "L1_gnn_rms_w": (48, 8), "L1_gnn_att": (56, 2)}


class Steps:

    def __init__(self, eng, sem, turn=None, per=0, base=0):
        self.eng, self.sem, self.n, self.turn, self.per, self.base = eng, sem, 0, turn, per, base

    def value(self):
        return self.base + self.n if self.turn is None else self.turn * self.per + self.base + self.n

    def link(self, ins):
        self.n += 1
        ins.then_inc(self.sem, 1)
        self.eng.wait_ge(self.sem, self.value())

    def end(self):
        assert self.turn is None or self.n == self.per, (self.n, self.per)


def build(nc, A, out, stop=99):
    with ExitStack() as ctx:
        def sb(name, shape, dt=F32):
            return ctx.enter_context(nc.sbuf_tensor(name, shape, dt))

        phase_sems = []

        def sem(name):
            phase_sems.append(nc.alloc_semaphore(name=name))
            return phase_sems[-1]

        def stream_sem(name):
            return nc.alloc_semaphore(name=name)

        def recycle():
            nc.clear_and_free_semaphores(list(phase_sems))
            phase_sems.clear()
            nc.all_engine_barrier()

        def scratch(name, shape, dt=F32):
            return nc.dram_tensor(name, shape, dt, kind="Internal").ap()

        featA = sb("featA", [128, KD, N])
        bigB = sb("bigB", [128, NT * D])
        bigC = sb("bigC", [128, NT * N])
        ring = sb("ring", [128, 2, 10, CW])
        stage1 = sb("stage1", [128, NT * CW])
        stage2 = sb("stage2", [128, NT * CW])
        stage3 = sb("stage3", [128, NT * CW])
        stage4 = sb("stage4", [128, NT * CW])
        gatT = stage4[:, 0:2 * N].rearrange("p (k n) -> p k n", k=2)
        tokB = bigB[0:P, 0:NT * D].rearrange("p (t n) -> p t n", t=NT)
        tokC = bigC[0:P, 0:NT * D].rearrange("p (t n) -> p t n", t=NT)
        featB = bigB[:, 0:KD * N].rearrange("p (k n) -> p k n", k=KD)
        ident = sb("ident", [128, 128])
        ident16 = sb("ident16", [128, 128], BF16)
        ones = sb("ones", [128, 128])
        blocks = sb("blocks", [128, 128])
        iota_i = bigC[0:P, NT * N // 2:NT * N // 2 + N].bitcast(I32)
        iota16 = sb("iota16", [P, N], F16)
        src_i = sb("src_i", [P, NB * SUB], I32)
        dst_i = sb("dst_i", [P, NB * SUB], I32)
        src_f = sb("src_f", [P, NB * SUB])
        dst_f = sb("dst_f", [P, NB * SUB])
        table = sb("table", [1, 4, NT], I32)
        small = sb("small", [128, 256])
        bcol = sb("bcol", [128, 64])
        comb = sb("comb", [P, NT, NEXP])[:, :, :]
        bank = [ctx.enter_context(nc.psum_tensor(f"bank{i}", [128, 512], F32)) for i in range(8)]

        XR = scratch("XR", (N, D))
        XN = scratch("XN", (N, D))
        XL = scratch("XL", (N, HID))
        ptile = lambda ap: ap.rearrange("(t p) n -> p t n", p=P)

        slots = []

        def chunked(w, n, cw=CW):
            v = w.rearrange("(k p) n -> p k n", p=128)
            for c in range(n):
                slots.append([(slice(0, v.shape[1]), v[:, :, c * cw:(c + 1) * cw])])

        w_full = [stream_sem("w_full0"), stream_sem("w_full1")]
        w_used = stream_sem("w_used")
        loaded = [0]
        took = [0]

        def ring_k(i, nk, cw):
            return ring[:, i].rearrange("p k n -> p (k n)")[:, 0:nk * cw].rearrange("p (k n) -> p k n", k=nk)

        def load_slots(sp, upto):
            while loaded[0] < min(upto, len(slots)):
                s = loaded[0]
                if s >= 2:
                    sp.wait_ge(w_used, s - 1)
                parts = slots[s]
                for kk, v in parts:
                    nk, cw = v.shape[1], v.shape[2]
                    dst = ring[:, s % 2, kk, :] if cw == CW else ring_k(s % 2, nk, cw)
                    sp.dma_start(dst, v).then_inc(w_full[s % 2], 16)
                fulls[s % 2].append((fulls[s % 2][-1] if fulls[s % 2] else 0) + 16 * len(parts))
                loaded[0] += 1

        fulls = [[], []]

        def full_value(s):
            return sum(16 * len(slots[q]) for q in range(s % 2, s + 1, 2))

        chunked(A["L0_gnn_W"], NC)
        q0 = [A[f"L0_mix_W{x}"].rearrange("(k p) n -> p k n", p=128) for x in "qkv"]
        for c in range(NC):
            for w in q0:
                slots.append([(slice(0, KD), w[:, :, c * CW:(c + 1) * CW])])
        chunked(A["L0_mix_Wo"], NC)
        chunked(A["L0_mix_W1"], 2)
        chunked(A["L0_mix_W2"], 2, 512)
        for e in range(NEXP):
            slots.append([(slice(0, KD), A["L0_ffn_W1"][e].rearrange("(k p) n -> p k n", p=128))])
            slots.append([(slice(0, 2), A["L0_ffn_W2"][e].rearrange("(k p) n -> p k n", p=128))])
        chunked(A["L1_gnn_W_down"], 1)
        wl = A["L1_gnn_Wl"].rearrange("(k p) n -> p k n", p=128)
        wr = A["L1_gnn_Wr"].rearrange("(k p) n -> p k n", p=128)
        slots.append([(slice(0, 2), wl), (slice(2, 4), wr)])
        qkv = A["L1_mix_W_qkv"].rearrange("(k p) n -> p k n", p=128)
        for c in range(NC):
            for j in range(3):
                slots.append([(slice(0, KD), qkv[:, :, j * D + c * CW:j * D + (c + 1) * CW])])
        wp = A["L1_mix_W_proj"].rearrange("(k p) n -> p k n", p=128)
        wu = A["L1_gnn_W_up"].rearrange("(k p) n -> p k n", p=128)
        for c in range(NC):
            slots.append([(slice(0, KD), wp[:, :, c * CW:(c + 1) * CW]),
                          (slice(KD, KD + 2), wu[:, :, c * CW:(c + 1) * CW])])

        def take(n):
            s = took[0]
            took[0] += n
            return s

        def w_wait(eng, s, turn=None, per=0):
            eng.wait_ge(w_full[s % 2], full_value(s) if turn is None else turn * per + full_value(s))


        idle = stream_sem("idle")

        def hold(eng):
            eng.sem_inc(idle, 1)

        def row_bc(v, n):
            return v.rearrange("(o n) -> o n", o=1).to_broadcast([P, n])

        def phase_start():
            s_bc = sem("columns_in")
            s_ld, s_c, s_t, s_x, s_p = sem("edges_in"), sem("consts"), sem("start_dve"), sem("start_pe"), sem("start_pool")
            dw = stage1[0:NB, 0:BE].bitcast(I32)
            dwf = stage2[0:NB, 0:BE]
            mm = small[0:NB, 0:2]
            row = small[0:1, 16:16 + 2 * NB]
            big = bigC[0:1, 0:8 * NT * NB].rearrange("p (a t b) -> p a t b", a=8, t=NT)
            with nc.Block() as block:
                @block.sync
                def _(sp):
                    for v, t in ((A["src"], src_i), (A["dst"], dst_i)):
                        sp.dma_start(t[:, :].rearrange("p (b g) -> p b g", g=SUB),
                                     v.rearrange("(b p g) -> p b g", p=P, g=SUB)).then_inc(s_ld, 16)
                    sp.dma_start(dw, A["dst"].rearrange("(b e) -> b e", b=NB)).then_inc(s_ld, 16)
                    for name, (at, n) in COLS.items():
                        sp.dma_start(bcol[:, at:at + n], A[name]).then_inc(s_bc, 16)
                    load_slots(sp, 2)
                    sp.wait_ge(s_bc, 16 * len(COLS))

                @block.gpsimd
                def _(pool):
                    nc.gpsimd.iota(iota_i[:], pattern=[[1, N]], base=0, channel_multiplier=0).then_inc(s_p, 1)
                    nc.gpsimd.memset(ones[:], 1.0).then_inc(s_p, 1)
                    pool.wait_ge(s_p, 2)
                    nc.gpsimd.affine_select(out=ident[:], in_=ones[:], compare_op=ALU.is_equal, fill=0.0, base=0,
                                            pattern=[[-1, 128]], channel_multiplier=1).then_inc(s_p, 1)
                    nc.gpsimd.memset(blocks[:], 0.0).then_inc(s_p, 1)
                    pool.wait_ge(s_p, 4)
                    nc.gpsimd.memset(blocks[0:64, 0:64], 1.0).then_inc(s_p, 1)
                    nc.gpsimd.memset(blocks[64:128, 64:128], 1.0).then_inc(s_p, 1)

                @block.tensor
                def _(pe):
                    pe.wait_ge(s_p, 6)
                    pe.wait_ge(s_t, 1)
                    for i in range(2):
                        last = nc.tensor.transpose(bank[0][0:1, i * NB:(i + 1) * NB], mm[:, i:i + 1], ident[0:NB, 0:NB])
                    last.then_inc(s_x, 1)

                @block.vector
                def _(dve):
                    st = Steps(dve, s_c)
                    dve.wait_ge(s_ld, 48)
                    nc.vector.tensor_copy(src_f[:], src_i[:])
                    nc.vector.tensor_copy(dst_f[:], dst_i[:])
                    st.link(nc.vector.tensor_copy(dwf, dw))
                    nc.vector.tensor_reduce(mm[:, 0:1], dwf, AX.X, ALU.max)
                    nc.vector.tensor_reduce(mm[:, 1:2], dwf, AX.X, ALU.min).then_inc(s_t, 1)
                    dve.wait_ge(s_p, 3)
                    nc.vector.tensor_copy(ident16[:], ident[:])
                    st.link(nc.vector.tensor_copy(iota16[:], iota_i[:]))
                    dve.wait_ge(s_x, 1)
                    st.link(nc.vector.tensor_copy(row, bank[0][0:1, 0:2 * NB]))
                    tile_at = iota16[0:1, 0:N:P].rearrange("p (t o) -> p t o", o=1).to_broadcast([1, NT, NB])
                    b_at = iota16[0:1, 0:NB].rearrange("p (o b) -> p o b", o=1).to_broadcast([1, NT, NB])
                    rows = row.rearrange("p (a o b) -> p a o b", a=2, o=1)
                    bmax, bmin = (rows[:, a].to_broadcast([1, NT, NB]) for a in range(2))
                    st.link(nc.vector.tensor_tensor(big[:, 0], bmax, tile_at, ALU.is_lt))
                    st.link(nc.vector.scalar_tensor_tensor(out=big[:, 1], in0=big[:, 0], scalar=1000.0, in1=b_at,
                                                           op0=ALU.mult, op1=ALU.add))
                    st.link(nc.vector.scalar_tensor_tensor(out=big[:, 2], in0=bmin, scalar=float(P), in1=tile_at,
                                                           op0=ALU.subtract, op1=ALU.is_lt))
                    st.link(nc.vector.scalar_tensor_tensor(out=big[:, 3], in0=b_at, scalar=1.0, in1=big[:, 2],
                                                           op0=ALU.add, op1=ALU.mult))
                    lo, hi, cnt, base = (small[0:1, 128 + 16 * i:128 + 16 * i + NT] for i in range(4))
                    st.link(nc.vector.tensor_reduce(lo, big[:, 1], AX.X, ALU.min))
                    st.link(nc.vector.tensor_reduce(hi, big[:, 3], AX.X, ALU.max))
                    st.link(nc.vector.tensor_scalar(lo, lo, float(NB - 1), None, ALU.min))
                    st.link(nc.vector.tensor_tensor(cnt, hi, lo, ALU.subtract))
                    st.link(nc.vector.tensor_scalar(cnt, cnt, 1.0, None, ALU.max))
                    st.link(nc.vector.memset(base[:, 0:1], 0.0))
                    for t in range(1, NT):
                        st.link(nc.vector.tensor_tensor(base[:, t:t + 1], base[:, t - 1:t], cnt[:, t - 1:t], ALU.add))
                    nc.vector.tensor_copy(table[:, 0], lo)
                    nc.vector.tensor_copy(table[:, 1], cnt)
                    nc.vector.tensor_copy(table[:, 2], base)

        def phase_norm(name, load=None, gain=None, add=None, keep=None, keep_sum=None, turn=True, store=None,
                       store_src=None, rms=None, eps=1e-5, tok=None):
            tok = tokC if tok is None else tok
            s_in = [sem(f"{name}_in{i}") for i in range(2)]
            s_ad = [sem(f"{name}_add{i}") for i in range(2)]
            s_st = [sem(f"{name}_stored{i}") for i in range(2)]
            s_row, s_va, s_sd, s_y, s_tr, s_ev, s_own = (sem(f"{name}_" + x) for x in
                                                         ("rows", "var", "sd", "y", "turned", "evac", "own"))
            xin = stage1[0:P, 0:2 * D].rearrange("p (i n) -> p i n", i=2)
            y = stage2[0:P, 0:2 * D].rearrange("p (i n) -> p i n", i=2)
            rows = stage3[0:P, 0:2 * D].rearrange("p (i n) -> p i n", i=2)
            ain = xin
            stores = [(store, y)] if store is not None else [(store_src, xin)] if store_src is not None else []
            with nc.Block() as block:
                @block.sync
                def _(sp):
                    if gain is not None:
                        for i in range(2):
                            sp.dma_start(rows[:, i], row_bc(gain[i], D)).then_inc(s_row, 16)
                    for t in range(NT + 2):
                        i = t % 2
                        if t >= 2:
                            sp.wait_ge(s_y, t - 1)
                            if store is not None:
                                sp.dma_start(store[(t - 2) * P:(t - 1) * P, :], y[:, i]).then_inc(s_st[i], 16)
                            if store_src is not None:
                                sp.dma_start(store_src[(t - 2) * P:(t - 1) * P, :],
                                             tok[:, t - 2]).then_inc(s_st[i], 16)
                        if t < NT and load is not None:
                            sp.dma_start(xin[:, i], load[t * P:(t + 1) * P, :]).then_inc(s_in[i], 16)
                        if t < NT and add is not None:
                            sp.dma_start(ain[:, i], add[t * P:(t + 1) * P, :]).then_inc(s_ad[i], 16)
                    load_slots(sp, took[0] + 2)
                    if store is not None or store_src is not None:
                        for i in range(2):
                            sp.wait_ge(s_st[i], 16 * NT // 2 + (16 if store is not None else 0))

                @block.vector
                def _(dve):
                    if store is not None:
                        for i in range(2):
                            dve.sem_inc(idle, 1)
                    per = 2 * (4 + (2 if gain is not None else 0) + (1 if rms is not None else 0)
                               + (1 if add is not None else 0) + (1 if keep or keep_sum else 0))
                    if gain is not None:
                        dve.wait_ge(s_row, 32)
                    with dve.Fori(0, NT // 2) as tt:
                        st = Steps(dve, s_own, tt, per)
                        for i in range(2):
                            t = tt * 2 + i
                            sm = small[0:P, 32 * i:32 * i + 32]
                            if load is not None:
                                dve.wait_ge(s_in[i], tt * 16 + 16)
                                x = xin[:, i]
                                x0, x1 = xin[:, i, 0:512], xin[:, i, 512:D]
                            else:
                                x = tok[:, ds(t, 1), :].rearrange("p o n -> p (o n)")
                                x0 = tok[:, ds(t, 1), 0:512].rearrange("p o n -> p (o n)")
                                x1 = tok[:, ds(t, 1), 512:D].rearrange("p o n -> p (o n)")
                            nc.vector.bn_stats(sm[:, 0:6], x0)
                            st.link(nc.vector.bn_stats(sm[:, 6:12], x1))
                            hold(dve)
                            st.link(nc.vector.bn_aggr(sm[:, 12:14], sm[:, 0:12]))
                            nc.vector.tensor_scalar(sm[:, 14:15], sm[:, 13:14], eps, None, ALU.add).then_inc(s_va, 1)
                            dve.wait_ge(s_sd, t + 1)
                            st.link(nc.vector.reciprocal(sm[:, 16:17], sm[:, 15:16]))
                            if turn:
                                dve.wait_ge(s_tr, t * 2 + 1)
                            if store is not None:
                                dve.wait_ge(s_st[i], tt * 16 + 16)
                            st.link(nc.vector.tensor_scalar(y[:, i], x, sm[:, 12:13], sm[:, 16:17],
                                                            ALU.subtract, ALU.mult))
                            if gain is not None:
                                st.link(nc.vector.tensor_tensor(y[:, i], y[:, i], rows[:, 0], ALU.mult))
                                st.link(nc.vector.tensor_tensor(y[:, i], y[:, i], rows[:, 1], ALU.add))
                            if add is not None:
                                dve.wait_ge(s_ad[i], tt * 16 + 16)
                                st.link(nc.vector.tensor_tensor(y[:, i], y[:, i], ain[:, i], ALU.add))
                            if rms is not None:
                                st.link(nc.vector.scalar_tensor_tensor(
                                    out=xin[:, i], in0=y[:, i], scalar=1.0, in1=y[:, i], op0=ALU.mult, op1=ALU.mult,
                                    accum_out=small[0:P, ds(t + rms, 1)]))
                            if keep:
                                hold(dve)
                                st.link(nc.vector.tensor_copy(tokC[:, ds(t, 1), :].rearrange("p o n -> p (o n)"),
                                                              y[:, i]))
                            elif keep_sum:
                                st.link(nc.vector.tensor_tensor(tokB[:, ds(t, 1), :].rearrange("p o n -> p (o n)"),
                                                                x, y[:, i], ALU.add))
                            nc.vector.sem_inc(s_y, 1)
                        st.end()

                @block.scalar
                def _(act):
                    if turn:
                        act.sem_inc(s_tr, 4)
                    if store is not None:
                        for i in range(2):
                            act.sem_inc(s_st[i], 16)
                    act.sem_inc(s_ev, 4)
                    with act.Fori(0, NT // 2) as tt:
                        for i in range(2):
                            t = tt * 2 + i
                            sm = small[0:P, 32 * i:32 * i + 32]
                            act.wait_ge(s_va, t + 1)
                            nc.scalar.sqrt(sm[:, 15:16], sm[:, 14:15]).then_inc(s_sd, 1)
                            if turn:
                                for h in range(2):
                                    act.wait_ge(s_tr, t * 2 + h + 5)
                                    nc.scalar.copy(
                                        featA[:, 4 * h:4 * h + 4, ds(t * P, P)],
                                        bank[2 * i + h][:, 0:4 * P].rearrange("p (k n) -> p k n", k=4)).then_inc(s_ev, 1)

                if turn:
                    @block.tensor
                    def _(pe):
                        with pe.Fori(0, NT // 2) as tt:
                            for i in range(2):
                                pe.wait_ge(s_y, tt * 2 + i + 1)
                                for k in range(KD):
                                    if k % 4 == 0:
                                        pe.wait_ge(s_ev, (tt * 2 + i) * 2 + k // 4 + 1)
                                    m = nc.tensor.transpose(bank[2 * i + k // 4][:, (k % 4) * P:(k % 4 + 1) * P],
                                                            y[:, i, k * 128:(k + 1) * 128], ident[0:P, 0:P])
                                    if k % 4 == 3:
                                        m.then_inc(s_tr, 1)

        def pe_tok(pe, s0, lhs, nk, s_mm, s_free, turns=NC // 2, cw=CW, rhs_more=None):
            with pe.Fori(0, turns) as tt:
                for i in range(2):
                    w_wait(pe, s0 + i, tt, 16 * len(slots[s0 + i]))
                    w = ring_k((s0 + i) % 2, nk, cw)
                    for t in range(NT):
                        u = i * NT + t
                        pe.wait_ge(s_free, tt * 2 * NT + u + 1)
                        for k in range(nk):
                            m = nc.tensor.matmul(bank[u % 4][0:P, 0:cw], lhs(k, t), w[:, k, :],
                                                 start=(k == 0), stop=(k == nk - 1))
                        m.then_inc(s_mm, 1)
                    pe.wait_ge(s_mm, tt * 2 * NT + (i + 1) * NT)
                    pe.sem_inc(w_used, 1)

        def phase_h0():
            s_mm, s_free, s_a, s_own = sem("h0_mm"), sem("h0_free"), sem("h0_a"), sem("h0_own")
            s0 = take(NC)
            al, ar = small[0:P, 128:128 + NT], small[0:P, 144:144 + NT]
            arow = stage3[0:P, 0:2 * D].rearrange("p (i n) -> p i n", i=2)
            junk = stage1[0:P, 0:D]
            with nc.Block() as block:
                @block.sync
                def _(sp):
                    sp.dma_start(arow, A["L0_gnn_a"].rearrange("o (i n) -> o i n", i=2)
                                 .to_broadcast([P, 2, D])).then_inc(s_a, 16)
                    load_slots(sp, s0 + NC + 2)

                @block.tensor
                def _(pe):
                    pe_tok(pe, s0, lambda k, t: featA[:, k, t * P:(t + 1) * P], KD, s_mm, s_free)

                @block.scalar
                def _(act):
                    act.sem_inc(s_free, 4)
                    with act.Fori(0, NC // 2) as tt:
                        for i in range(2):
                            for t in range(NT):
                                u = i * NT + t
                                act.wait_ge(s_mm, tt * 2 * NT + u + 1)
                                nc.scalar.copy(tokB[:, t, ds((tt * 2 + i) * CW, CW)],
                                               bank[u % 4][0:P, 0:CW]).then_inc(s_free, 1)

                @block.vector
                def _(dve):
                    st = Steps(dve, s_own)
                    dve.wait_ge(s_a, 16)
                    for t in range(NT):
                        dve.wait_ge(s_free, 4 + (NC - 1) * NT + t + 1)
                        for i, dst in ((0, al), (1, ar)):
                            st.link(nc.vector.tensor_tensor_reduce(junk, tokB[:, t, :], arow[:, i], 1.0, 0.0,
                                                                   ALU.mult, ALU.add, dst[:, t:t + 1]))

        def batches(eng, d):
            return [eng.value_load(table[0:1, i, ds(d, 1)], min_val=0, max_val=(NB - 1, NB, NB * NT)[i])
                    for i in range(3)]

        def batch(lo, r):
            return nc.s_assert_within(lo + r, 0, NB - 1, skip_runtime_bounds_check_because="the table keeps "
                                      "first <= NB - 1 and first + count <= NB")

        def phase_edges0():
            s_dg, s_al, s_alb, s_z, s_ez, s_c, s_free, s_oh, s_used, s_own = (sem("e0_" + x) for x in (
                "diag", "al", "alb", "z", "expz", "count", "free", "onehot", "used", "own"))
            al, ar = small[0:P, 128:128 + NT], small[0:P, 144:144 + NT]
            ohs = stage1[0:P, :].bitcast(F16)[:, 0:HB * N].rearrange("p (q n) -> p q n", q=HB)
            ohd = stage2[0:P, :].bitcast(F16)[:, 0:SUB * P].rearrange("p (q n) -> p q n", q=SUB)
            z = stage2[0:P, SUB * P // 2:SUB * P // 2 + N]
            alb = stage3[0:P, 0:N]
            zero16 = gatT[0:P, 0, 0:P // 2 + 1].bitcast(F16)[:, 0:P]
            diag = gatT[0:P, 1, 0:N].rearrange("p (t n) -> p t n", t=NT)
            emat = bigC[0:P, 0:NT * N].rearrange("p (t n) -> p t n", t=NT)
            with nc.Block() as block:
                @block.vector
                def _(dve):
                    nc.vector.memset(zero16, 0.0)
                    nc.vector.tensor_tensor(diag, ident[0:P, 0:P].rearrange("p (o n) -> p o n", o=1)
                                            .to_broadcast([P, NT, P]),
                                            al.rearrange("p (t o) -> p t o", o=1).to_broadcast([P, NT, P]),
                                            ALU.mult).then_inc(s_dg, 1)
                    dve.wait_ge(s_alb, 3)
                    dve.sem_inc(s_free, 2)
                    with dve.Fori(0, NT) as d:
                        lo, cnt, base = batches(dve, d)
                        st = Steps(dve, s_own, d, 1)
                        dve.wait_ge(s_free, d + 2)
                        st.link(nc.vector.tensor_scalar(z, alb, ar[:, ds(d, 1)], None, ALU.add))
                        nc.vector.scalar_tensor_tensor(out=z, in0=z, scalar=0.1, in1=z, op0=ALU.mult,
                                                       op1=ALU.max).then_inc(s_z, 1)
                        st.end()
                        with dve.Fori(0, cnt) as r:
                            for q in range(SUB):
                                u = (base + r) * SUB + q
                                j = batch(lo, r) * SUB + q
                                dve.wait_ge(s_used, u + 1)
                                if q % HB == 0:
                                    nc.vector.tensor_tensor(
                                        ohd[:, q:q + HB, :],
                                        iota16[:, ds(d * P, P)].rearrange("p (o n) -> p o n", o=1).to_broadcast([P, HB, P]),
                                        dst_f[:, ds(j, HB)].rearrange("p (q o) -> p q o", o=1).to_broadcast([P, HB, P]),
                                        ALU.is_equal)
                                nc.vector.tensor_scalar(ohs[:, q % HB, :], iota16[:], src_f[:, ds(j, 1)], None,
                                                        ALU.is_equal).then_inc(s_oh, 1)
                        dve.wait_ge(s_ez, d + 1)
                        dve.wait_ge(s_c, d + 1)
                        for ch, (a, w) in enumerate(FCH):
                            m = nc.vector.tensor_tensor(emat[:, ds(d, 1), a:a + w].rearrange("p o n -> p (o n)"),
                                                        bank[ch][0:P, 0:w], z[:, a:a + w], ALU.mult)
                        m.then_inc(s_free, 1)

                @block.scalar
                def _(act):
                    act.wait_ge(s_al, 1)
                    for ch, (a, w) in enumerate(FCH):
                        nc.scalar.copy(alb[:, a:a + w], bank[5 + ch][0:P, 0:w]).then_inc(s_alb, 1)
                    with act.Fori(0, NT) as d:
                        act.wait_ge(s_z, d + 1)
                        nc.scalar.activation(z, z, ACT.Exp, scale=-1.0).then_inc(s_ez, 1)

                @block.tensor
                def _(pe):
                    pe.wait_ge(s_dg, 1)
                    for t in range(NT):
                        m = nc.tensor.matmul(bank[5 + t // 4][0:P, (t % 4) * P:(t % 4 + 1) * P], ones[0:P, 0:P],
                                             diag[:, t, :], start=True, stop=True)
                    m.then_inc(s_al, 1)
                    pe.sem_inc(s_used, HB)
                    with pe.Fori(0, NT) as d:
                        lo, cnt, base = batches(pe, d)
                        pe.wait_ge(s_free, d + 2)
                        for ch, (a, w) in enumerate(FCH):
                            nc.tensor.matmul(bank[ch][0:P, 0:w], zero16, iota16[:, a:a + w], start=True, stop=False,
                                             skip_group_check=True)
                        with pe.Fori(0, cnt) as r:
                            for q in range(SUB):
                                pe.wait_ge(s_oh, (base + r) * SUB + q + 1)
                                for ch, (a, w) in enumerate(FCH):
                                    m = nc.tensor.matmul(bank[ch][0:P, 0:w], ohd[:, q, :], ohs[:, q % HB, a:a + w],
                                                         start=False, stop=False, skip_group_check=True)
                                m.then_inc(s_used, 1)
                        for ch, (a, w) in enumerate(FCH):
                            m = nc.tensor.matmul(bank[ch][0:P, 0:w], zero16, iota16[:, a:a + w], start=False,
                                                 stop=True, skip_group_check=True)
                        m.then_inc(s_c, 1)

        def phase_agg0():
            s_rs, s_rr, s_mm, s_free, s_m, s_e, s_own, s_ch = (sem("a0_" + x) for x in (
                "rowsum", "recip", "mm", "free", "min", "exp", "own", "chunk"))
            s_x = [sem(f"a0_x{i}") for i in range(2)]
            s_st = [sem(f"a0_stored{i}") for i in range(2)]
            emat = bigC[0:P, 0:NT * N].rearrange("p (t n) -> p t n", t=NT)
            rs = small[0:P, 160:160 + NT]
            xch = [s_[0:P, :].rearrange("p (t n) -> p t n", t=NT) for s_ in (stage1, stage2)]
            low = stage3[0:P, :]
            hp = stage4[0:P, :]
            xv, rv = ptile(A["x"]), ptile(XR)
            with nc.Block() as block:
                @block.sync
                def _(sp):
                    for c in range(NC + 2):
                        if c >= 2:
                            sp.wait_ge(s_ch, c)
                            sp.dma_start(rv[:, :, (c - 2) * CW:(c - 1) * CW], xch[c % 2]).then_inc(s_st[c % 2], 16)
                            sp.wait_ge(s_st[c % 2], 16 * (c // 2))
                        if c < NC:
                            sp.dma_start(xch[c % 2], xv[:, :, c * CW:(c + 1) * CW]).then_inc(s_x[c % 2], 16)

                @block.tensor
                def _(pe):
                    for t in range(NT):
                        for d in range(NT):
                            m = nc.tensor.matmul(bank[7][0:P, t:t + 1], emat[:, d, t * P:(t + 1) * P], ones[0:P, 0:1],
                                                 start=(d == 0), stop=(d == NT - 1))
                    m.then_inc(s_rs, 1)
                    with pe.Fori(0, NC // 2) as cc:
                        for u in range(2 * NT):
                            t = u % NT
                            pe.wait_ge(s_free, cc * 2 * NT + u + 1)
                            for d in range(NT):
                                m = nc.tensor.matmul(bank[u % 4][0:P, 0:CW], emat[:, d, t * P:(t + 1) * P],
                                                     tokB[:, d, ds((cc * 2 + u // NT) * CW, CW)],
                                                     start=(d == 0), stop=(d == NT - 1))
                            m.then_inc(s_mm, 1)

                @block.vector
                def _(dve):
                    st = Steps(dve, s_own)
                    dve.wait_ge(s_rs, 1)
                    st.link(nc.vector.tensor_scalar(rs, bank[7][0:P, 0:NT], 1e-5, None, ALU.add))
                    st.link(nc.vector.reciprocal(rs, rs))
                    nc.vector.sem_inc(s_rr, 1)
                    with dve.Fori(0, NC // 2) as cc:
                        st = Steps(dve, s_own, cc, 4, base=2)
                        for c in range(2):
                            dve.wait_ge(s_free, (cc * 2 + c) * NT + NT + 4)
                            nc.vector.tensor_scalar(low, hp, 0.0, None, ALU.min).then_inc(s_m, 1)
                            dve.wait_ge(s_e, cc * 2 + c + 1)
                            st.link(nc.vector.scalar_tensor_tensor(out=hp, in0=low, scalar=-1.0, in1=hp,
                                                                   op0=ALU.add, op1=ALU.max))
                            dve.wait_ge(s_x[c], cc * 16 + 16)
                            xc = xch[c].rearrange("p t n -> p (t n)")
                            st.link(nc.vector.tensor_tensor(xc, xc, hp, ALU.add))
                            nc.vector.sem_inc(s_ch, 1)
                        st.end()

                @block.scalar
                def _(act):
                    act.wait_ge(s_rr, 1)
                    act.sem_inc(s_free, 4)
                    act.sem_inc(s_ch, 1)
                    with act.Fori(0, NC // 2) as cc:
                        for c in range(2):
                            act.wait_ge(s_ch, cc * 2 + c + 1)
                            for t in range(NT):
                                u = c * NT + t
                                act.wait_ge(s_mm, cc * 2 * NT + u + 1)
                                nc.scalar.activation(hp[:, t * CW:(t + 1) * CW], bank[u % 4][0:P, 0:CW], ACT.Copy,
                                                     scale=rs[:, t:t + 1]).then_inc(s_free, 1)
                            act.wait_ge(s_m, cc * 2 + c + 1)
                            nc.scalar.activation(low, low, ACT.Exp).then_inc(s_e, 1)

        def phase_mix(name, normed):
            (s_row, s_q, s_qe, s_mq, s_eq, s_q2, s_n, s_ne, s_t, s_te, s_mk, s_ek, s_k2, s_kn, s_kr, s_kv, s_kve,
             s_cx, s_ce, s_own) = (sem(f"{name}_" + x) for x in (
                 "rows", "q", "qevac", "qmin", "qexp", "qsq", "norm", "normevac", "tok", "tokevac", "kmin", "kexp",
                 "ksq", "knorm", "kvin", "kv", "kvevac", "ctx", "ctxevac", "own"))
            s0 = take(3 * NC)
            qt = bigC[:, 0:2 * N].rearrange("p (m n) -> p m n", m=2)
            qv = bigC[:, 2 * N:4 * N].rearrange("p (m n) -> p m n", m=2)
            qt_all, qv_all = bigC[:, 0:2 * N], bigC[:, 2 * N:4 * N]
            tk = bigC[0:P, 4 * N:4 * N + NT * CW]
            kc, vc = stage1[0:P, :], stage2[0:P, :]
            kv = stage3[:, 0:512].rearrange("p (j n) -> p j n", j=4)
            n2, kn, rk = (small[0:P, 0 + 64 * i:40 + 64 * i] for i in range(3))
            rows = stage4[0:P, 0:2 * D].rearrange("p (i n) -> p i n", i=2)
            units = [(m, ch, a, w) for m in range(2) for ch, (a, w) in enumerate(FCH)]
            NU = len(units)

            with nc.Block() as block:
                @block.sync
                def _(sp):
                    if normed:
                        sp.dma_start(rows[:, 0], row_bc(A["L0_mix_bk"], D)).then_inc(s_row, 16)
                        sp.dma_start(rows[:, 1], row_bc(A["L0_mix_bv"], D)).then_inc(s_row, 16)
                    load_slots(sp, s0 + 3 * NC + 2)

                @block.tensor
                def _(pe):
                    pe.sem_inc(s_ce, 1)
                    with pe.Fori(0, NC // 2) as cc:
                        for i in range(2):
                            c = cc * 2 + i

                            def slot(j):
                                s = s0 + 3 * i + j
                                w_wait(pe, s, cc, 48)
                                return ring_k(s % 2, KD, CW)

                            w = slot(0)
                            for j, (m, ch, a, wd) in enumerate(units):
                                if j < 3:
                                    pe.wait_ge(s_ce, c * NU + 1)
                                else:
                                    pe.wait_ge(s_qe, c * NU + j - 2)
                                for k in range(KD):
                                    x = nc.tensor.matmul(bank[4 + ch][:, 0:wd], w[:, k, m * 128:(m + 1) * 128],
                                                         featA[:, k, a:a + wd], start=(k == 0), stop=(k == KD - 1))
                                x.then_inc(s_q, 1)
                            pe.wait_ge(s_q, c * NU + NU)
                            pe.sem_inc(w_used, 1)

                            def tok(j):
                                w = slot(1 + j)
                                for t in range(NT):
                                    u = j * NT + t
                                    pe.wait_ge(s_te, c * 2 * NT + u + 1)
                                    for k in range(KD):
                                        x = nc.tensor.matmul(bank[u % 4][0:P, 0:CW], featA[:, k, t * P:(t + 1) * P],
                                                             w[:, k, :], start=(k == 0), stop=(k == KD - 1))
                                    x.then_inc(s_t, 1)
                                pe.wait_ge(s_t, c * 2 * NT + (j + 1) * NT)
                                pe.sem_inc(w_used, 1)

                            def scales(lhs):
                                for j, (m, ch, a, wd) in enumerate(units):
                                    if j < 3:
                                        pe.wait_ge(s_qe, c * NU + 4 + j)
                                    else:
                                        pe.wait_ge(s_ne, c * NU + j - 2)
                                    rhs = qv if normed else qt
                                    nc.tensor.matmul(bank[4 + ch][:, 0:wd], lhs(m), rhs[:, m, a:a + wd], start=True,
                                                     stop=True).then_inc(s_n, 1)

                            tok(0)
                            if normed:
                                pe.wait_ge(s_q2, c + 1)
                                scales(lambda m: blocks[:, :])
                            tok(1)
                            pe.wait_ge(s_kr, c + 1)
                            for m in range(2):
                                for what in range(1 if normed else 2):
                                    for t in range(NT):
                                        col = t * CW + m * 128
                                        x = nc.tensor.matmul(
                                            bank[7][:, (2 * m + what) * 128:(2 * m + what + 1) * 128],
                                            kc[:, col:col + 128], ones[0:P, :] if what else vc[:, col:col + 128],
                                            start=(t == 0), stop=(t == NT - 1))
                            x.then_inc(s_kv, 1)
                            pe.wait_ge(s_kve, c + 1)
                            if not normed:
                                scales(lambda m: kv[:, 2 * m + 1, :])
                            for j, (m, ch, a, wd) in enumerate(units):
                                if j < 3:
                                    pe.wait_ge(s_ne, c * NU + 4 + j)
                                else:
                                    pe.wait_ge(s_ce, c * NU + j - 1)
                                nc.tensor.matmul(bank[4 + ch][:, 0:wd], kv[:, 2 * m, :], qt[:, m, a:a + wd],
                                                 start=True, stop=True).then_inc(s_cx, 1)

                @block.scalar
                def _(act):
                    act.sem_inc(s_te, 4)
                    with act.Fori(0, NC // 2) as cc:
                        for i in range(2):
                            c = cc * 2 + i
                            for j, (m, ch, a, wd) in enumerate(units):
                                act.wait_ge(s_q, c * NU + j + 1)
                                if normed:
                                    hold(act)
                                    nc.scalar.activation(qt[:, m, a:a + wd], bank[4 + ch][:, 0:wd], ACT.Identity,
                                                         bias=bcol[:, ds(c * 2 + m, 1)]).then_inc(s_qe, 1)
                                else:
                                    nc.scalar.copy(qt[:, m, a:a + wd], bank[4 + ch][:, 0:wd]).then_inc(s_qe, 1)
                            act.wait_ge(s_mq, c + 1)
                            nc.scalar.activation(qv_all, qv_all, ACT.Exp).then_inc(s_eq, 1)

                            def evac(j, dst):
                                for t in range(NT):
                                    u = j * NT + t
                                    act.wait_ge(s_t, c * 2 * NT + u + 1)
                                    nc.scalar.copy(dst[:, t * CW:(t + 1) * CW], bank[u % 4][0:P, 0:CW]).then_inc(s_te, 1)

                            evac(0, kc)
                            act.wait_ge(s_mk, c + 1)
                            nc.scalar.activation(tk, tk, ACT.Exp).then_inc(s_ek, 1)
                            if normed:
                                for j, (m, ch, a, wd) in enumerate(units):
                                    act.wait_ge(s_n, c * NU + j + 1)
                                    nc.scalar.sqrt(qv[:, m, a:a + wd], bank[4 + ch][:, 0:wd]).then_inc(s_ne, 1)
                            evac(1, vc)
                            if normed:
                                act.wait_ge(s_k2, c + 1)
                                nc.scalar.sqrt(kn, n2).then_inc(s_kn, 1)

                @block.vector
                def _(dve):
                    if normed:
                        dve.wait_ge(s_row, 32)
                    with dve.Fori(0, NC // 2) as cc:
                        st = Steps(dve, s_own, cc, 16 if normed else 6)
                        for i in range(2):
                            c = cc * 2 + i

                            def row(j):
                                return rows[:, j, ds(c * CW, CW)].rearrange("p (o n) -> p o n", o=1).to_broadcast([P, NT, CW])

                            def by_tile(v):
                                return v.rearrange("p (t n) -> p t n", t=NT)

                            dve.wait_ge(s_ce, c * NU + 1)
                            dve.wait_ge(s_qe, c * NU + NU)
                            nc.vector.tensor_scalar(qv_all, qt_all, 0.0, None, ALU.min).then_inc(s_mq, 1)
                            dve.wait_ge(s_eq, c + 1)
                            if normed:
                                st.link(nc.vector.scalar_tensor_tensor(out=qt_all, in0=qv_all, scalar=-1.0, in1=qt_all,
                                                                       op0=ALU.add, op1=ALU.max))
                                nc.vector.tensor_tensor(qv_all, qt_all, qt_all, ALU.mult).then_inc(s_q2, 1)
                            else:
                                st.link(nc.vector.scalar_tensor_tensor(out=qt_all, in0=qt_all, scalar=1.0, in1=qv_all,
                                                                       op0=ALU.add, op1=ALU.max))
                            dve.wait_ge(s_te, c * 2 * NT + NT + 4)
                            if normed:
                                st.link(nc.vector.tensor_tensor(by_tile(kc), by_tile(kc), row(0), ALU.add))
                            nc.vector.tensor_scalar(tk, kc, 0.0, None, ALU.min).then_inc(s_mk, 1)
                            dve.wait_ge(s_ek, c + 1)
                            if normed:
                                st.link(nc.vector.scalar_tensor_tensor(out=kc, in0=tk, scalar=-1.0, in1=kc,
                                                                       op0=ALU.add, op1=ALU.max))
                                st.link(nc.vector.tensor_tensor(tk, kc, kc, ALU.mult))
                                nc.vector.tensor_reduce(n2, tk.rearrange("p (h n) -> p h n", n=64), AX.X,
                                                        ALU.add).then_inc(s_k2, 1)
                                dve.wait_ge(s_ne, c * NU + NU)
                                st.link(nc.vector.reciprocal(qv_all, qv_all))
                                dve.wait_ge(s_kn, c + 1)
                                st.link(nc.vector.reciprocal(rk, kn))
                                kh = kc.rearrange("p (h n) -> p h n", n=64)
                                st.link(nc.vector.tensor_tensor(kh, kh, rk.rearrange("p (h o) -> p h o", o=1)
                                                                .to_broadcast([P, 4 * NT, 64]), ALU.mult))
                                st.link(nc.vector.tensor_tensor(by_tile(vc), by_tile(vc), row(1), ALU.add))
                            else:
                                st.link(nc.vector.scalar_tensor_tensor(out=kc, in0=kc, scalar=1.0, in1=tk,
                                                                       op0=ALU.add, op1=ALU.max))
                                dve.wait_ge(s_te, c * 2 * NT + 2 * NT + 4)
                            nc.vector.sem_inc(s_kr, 1)
                            dve.wait_ge(s_kv, c + 1)
                            b7 = bank[7][:, :].rearrange("p (j n) -> p j n", j=4)
                            mask = blocks[:, :].rearrange("p (o n) -> p o n", o=1)
                            if normed:
                                nc.vector.scalar_tensor_tensor(out=kv[:, 0:4:2, :], in0=b7[:, 0:4:2, :], scalar=0.125,
                                                               in1=mask.to_broadcast([128, 2, 128]), op0=ALU.mult,
                                                               op1=ALU.mult).then_inc(s_kve, 1)
                            else:
                                nc.vector.tensor_tensor(kv, b7, mask.to_broadcast([128, 4, 128]),
                                                        ALU.mult).then_inc(s_kve, 1)
                                for j, (m, ch, a, wd) in enumerate(units):
                                    dve.wait_ge(s_n, c * NU + j + 1)
                                    nc.vector.tensor_scalar(qv[:, m, a:a + wd], bank[4 + ch][:, 0:wd], 1e-6, None,
                                                            ALU.add).then_inc(s_ne, 1)
                                dve.wait_ge(s_ne, c * NU + NU)
                                st.link(nc.vector.reciprocal(qv_all, qv_all))
                            for j, (m, ch, a, wd) in enumerate(units):
                                dve.wait_ge(s_cx, c * NU + j + 1)
                                dst = featB[:, ds(c * 2 + m, 1), a:a + wd].rearrange("p o n -> p (o n)")
                                nc.vector.tensor_tensor(dst, bank[4 + ch][:, 0:wd], qv[:, m, a:a + wd],
                                                        ALU.mult).then_inc(s_ce, 1)
                        st.end()

        def phase_out(name, lhs, nk, bias, residual):
            s_mm, s_free, s_b, s_own, s_ch = (sem(f"{name}_" + x) for x in ("mm", "free", "bias", "own", "chunk"))
            s_r = [sem(f"{name}_res{i}") for i in range(2)]
            s0 = take(NC)
            res = [x[0:P, :].rearrange("p (t n) -> p t n", t=NT) for x in (stage1, stage2)]
            brow = stage3[0:P, 0:D]
            rv = ptile(residual)
            with nc.Block() as block:
                @block.sync
                def _(sp):
                    sp.dma_start(brow, row_bc(bias, D)).then_inc(s_b, 16)
                    for c in range(NC):
                        if c >= 2:
                            sp.wait_ge(s_ch, c - 1)
                        sp.dma_start(res[c % 2], rv[:, :, c * CW:(c + 1) * CW]).then_inc(s_r[c % 2], 16)
                    load_slots(sp, s0 + NC + 2)

                @block.tensor
                def _(pe):
                    pe_tok(pe, s0, lhs, nk, s_mm, s_free)

                @block.scalar
                def _(act):
                    act.sem_inc(s_free, 4)
                    with act.Fori(0, NC // 2) as tt:
                        for i in range(2):
                            for t in range(NT):
                                u = i * NT + t
                                act.wait_ge(s_mm, tt * 2 * NT + u + 1)
                                nc.scalar.copy(tokC[:, t, ds((tt * 2 + i) * CW, CW)],
                                               bank[u % 4][0:P, 0:CW]).then_inc(s_free, 1)

                @block.vector
                def _(dve):
                    dve.wait_ge(s_b, 16)
                    for c in range(NC):
                        chunk = tokC[:, :, c * CW:(c + 1) * CW]
                        dve.wait_ge(s_r[c % 2], 16 * (c // 2) + 16)
                        dve.wait_ge(s_free, 4 + (c + 1) * NT)
                        nc.vector.tensor_tensor(chunk, chunk, res[c % 2], ALU.add).then_inc(s_ch, 1)
                        dve.wait_ge(s_ch, c + 1)
                        nc.vector.tensor_tensor(chunk, chunk, brow[:, c * CW:(c + 1) * CW]
                                                .rearrange("p (o n) -> p o n", o=1).to_broadcast([P, NT, CW]), ALU.add)

        def phase_up(name, weights, bias_at):
            s_mm, s_ev = sem(f"{name}_mm"), sem(f"{name}_gelu")
            s0 = take(2) if weights is None else 0
            with nc.Block() as block:
                if weights is None:
                    @block.sync
                    def _(sp):
                        load_slots(sp, s0 + 4)

                @block.tensor
                def _(pe):
                    for m in range(4):
                        if weights is None:
                            w_wait(pe, s0 + m // 2)
                            w = ring_k((s0 + m // 2) % 2, KD, CW)[:, :, (m % 2) * 128:(m % 2 + 1) * 128]
                        else:
                            w = weights(m)
                        for ch, (a, wd) in enumerate(FCH):
                            if m:
                                pe.wait_ge(s_ev, 3 * m + ch - 2)
                            for k in range(KD):
                                x = nc.tensor.matmul(bank[4 + ch][:, 0:wd], w[:, k, :], featA[:, k, a:a + wd],
                                                     start=(k == 0), stop=(k == KD - 1))
                            x.then_inc(s_mm, 1)
                        if weights is None and m % 2:
                            pe.wait_ge(s_mm, 3 * m + 3)
                            pe.sem_inc(w_used, 1)

                @block.scalar
                def _(act):
                    for m in range(4):
                        for ch, (a, wd) in enumerate(FCH):
                            act.wait_ge(s_mm, 3 * m + ch + 1)
                            nc.scalar.activation(featB[:, m, a:a + wd], bank[4 + ch][:, 0:wd], ACT.Gelu,
                                                 bias=bcol[:, bias_at + m:bias_at + m + 1]).then_inc(s_ev, 1)

        def phase_down(name, weights, bias, dram=None):
            s_mm, s_free, s_b, s_ch, s_st = (sem(f"{name}_" + x) for x in ("mm", "free", "bias", "chunk", "stored"))
            s0 = take(2) if weights is None else 0
            brow = stage3[0:P, 0:D]
            with nc.Block() as block:
                @block.sync
                def _(sp):
                    sp.dma_start(brow, row_bc(bias, D)).then_inc(s_b, 16)
                    if weights is None:
                        load_slots(sp, s0 + 4)
                    if dram is not None:
                        for c in range(2):
                            sp.wait_ge(s_ch, c + 1)
                            sp.dma_start(ptile(dram)[:, :, c * 512:(c + 1) * 512],
                                         tokC[:, :, c * 512:(c + 1) * 512]).then_inc(s_st, 16)
                        sp.wait_ge(s_st, 32)

                @block.tensor
                def _(pe):
                    for c in range(2):
                        if weights is None:
                            w_wait(pe, s0 + c)
                            w = ring_k((s0 + c) % 2, 4, 512)
                        else:
                            w = weights(c)
                        for t in range(NT):
                            u = c * NT + t
                            if u >= 4:
                                pe.wait_ge(s_free, u - 3)
                            for k in range(4):
                                m = nc.tensor.matmul(bank[u % 4][0:P, :], featB[:, k, t * P:(t + 1) * P], w[:, k, :],
                                                     start=(k == 0), stop=(k == 3))
                            m.then_inc(s_mm, 1)
                        if weights is None:
                            pe.wait_ge(s_mm, c * NT + NT)
                            pe.sem_inc(w_used, 1)

                @block.vector
                def _(dve):
                    dve.wait_ge(s_b, 16)
                    for c in range(2):
                        for t in range(NT):
                            u = c * NT + t
                            part = tokC[:, t, c * 512:(c + 1) * 512]
                            dve.wait_ge(s_mm, u + 1)
                            nc.vector.tensor_tensor(part, bank[u % 4][0:P, :], part, ALU.add).then_inc(s_free, 1)
                        dve.wait_ge(s_free, c * NT + NT)
                        part = tokC[:, :, c * 512:(c + 1) * 512]
                        nc.vector.tensor_tensor(part, part, brow[:, c * 512:(c + 1) * 512]
                                                .rearrange("p (o n) -> p o n", o=1).to_broadcast([P, NT, 512]),
                                                ALU.add).then_inc(s_ch, 1)

        def phase_route():
            s_ld, s_lg, s_own, s_e, s_ex, s_ct, s_cs, s_bm, s_be, s_r = (sem("rt_" + x) for x in (
                "in", "logits", "own", "comb", "exp", "turned", "turnedevac", "b2", "b2evac", "rows"))
            wr = stage1[:, 0:KD * NEXP].rearrange("p (k n) -> p k n", k=KD)
            b2 = stage2[0:NEXP, 0:D]
            br = stage3[0:P, 0:NEXP]
            combT = stage4[0:NEXP, 0:N]
            work = stage3[0:P, 256:256 + 8 * NT * NEXP].rearrange("p (a t n) -> p a t n", a=8, t=NT)
            lg, ex, eq = work[:, 0], work[:, 1], work[:, 2]
            mx, sm, ws = (small[0:P, 64 + 16 * i:64 + 16 * i + NT] for i in range(3))
            top = work[:, 3, :, 0:8]
            top_at = work[:, 4, :, 0:8].bitcast(U32)
            atf = work[:, 5, :, 0:8]
            col = lambda v, n: v.rearrange("p (t o) -> p t o", o=1).to_broadcast([P, NT, n])
            with nc.Block() as block:
                @block.sync
                def _(sp):
                    sp.dma_start(wr, A["L0_ffn_Wr"].rearrange("(k p) n -> p k n", p=128)).then_inc(s_ld, 16)
                    sp.dma_start(b2, A["L0_ffn_b2"]).then_inc(s_r, 16)
                    sp.dma_start(br, row_bc(A["L0_ffn_br"], NEXP)).then_inc(s_r, 16)

                @block.tensor
                def _(pe):
                    pe.wait_ge(s_ld, 16)
                    for t in range(NT):
                        for k in range(KD):
                            m = nc.tensor.matmul(bank[0][0:P, t * NEXP:(t + 1) * NEXP], featA[:, k, t * P:(t + 1) * P],
                                                 wr[:, k, :], start=(k == 0), stop=(k == KD - 1))
                    m.then_inc(s_lg, 1)
                    pe.wait_ge(s_e, 1)
                    for t in range(NT):
                        m = nc.tensor.transpose(bank[4 + t // 4][0:NEXP, (t % 4) * P:(t % 4 + 1) * P], comb[:, t, :],
                                                ident[0:P, 0:P])
                    m.then_inc(s_ct, 1)
                    pe.wait_ge(s_cs, 3)
                    pe.wait_ge(s_r, 32)
                    for u in range(2 * NT):
                        if u >= 4:
                            pe.wait_ge(s_be, u - 3)
                        nc.tensor.matmul(bank[u % 4][0:P, :], combT[:, (u // 2) * P:(u // 2 + 1) * P],
                                         b2[:, (u % 2) * 512:(u % 2 + 1) * 512], start=True,
                                         stop=True).then_inc(s_bm, 1)

                @block.scalar
                def _(act):
                    act.wait_ge(s_ex, 1)
                    nc.scalar.activation(ex, lg, ACT.Exp).then_inc(s_ex, 1)
                    act.wait_ge(s_ct, 1)
                    for ch, (a, w) in enumerate(FCH):
                        nc.scalar.copy(combT[:, a:a + w], bank[4 + ch][0:NEXP, 0:w]).then_inc(s_cs, 1)

                @block.vector
                def _(dve):
                    st = Steps(dve, s_own)
                    dve.wait_ge(s_r, 32)
                    dve.wait_ge(s_lg, 1)
                    st.link(nc.vector.tensor_tensor(lg, bank[0][0:P, 0:NT * NEXP].rearrange("p (t n) -> p t n", t=NT),
                                                    br.rearrange("p (o n) -> p o n", o=1).to_broadcast([P, NT, NEXP]),
                                                    ALU.add))
                    st.link(nc.vector.tensor_reduce(mx, lg, AX.X, ALU.max))
                    nc.vector.tensor_tensor(lg, lg, col(mx, NEXP), ALU.subtract).then_inc(s_ex, 1)
                    dve.wait_ge(s_ex, 2)
                    st.link(nc.vector.tensor_reduce(sm, ex, AX.X, ALU.add))
                    st.link(nc.vector.reciprocal(sm, sm))
                    st.link(nc.vector.tensor_tensor(ex, ex, col(sm, NEXP), ALU.mult))
                    for t in range(NT):
                        last = nc.vector.max(top[:, t, :], ex[:, t, :])
                    st.link(last)
                    for t in range(NT):
                        last = nc.vector.max_index(top_at[:, t, :], top[:, t, :], ex[:, t, :])
                    st.link(last)
                    st.link(nc.vector.tensor_copy(atf, top_at))
                    st.link(nc.vector.tensor_reduce(ws, top[:, :, 0:2], AX.X, ALU.add))
                    st.link(nc.vector.tensor_scalar(ws, ws, 1e-9, None, ALU.max))
                    st.link(nc.vector.reciprocal(ws, ws))
                    st.link(nc.vector.tensor_tensor(top[:, :, 0:2], top[:, :, 0:2], col(ws, 2), ALU.mult))
                    iota = iota16[:, 0:NEXP].rearrange("p (o n) -> p o n", o=1).to_broadcast([P, NT, NEXP])
                    for i in range(2):
                        st.link(nc.vector.tensor_tensor(eq, iota, atf[:, :, i:i + 1].to_broadcast([P, NT, NEXP]),
                                                        ALU.is_equal))
                        st.link(nc.vector.tensor_tensor(eq if i else comb, eq,
                                                        top[:, :, i:i + 1].to_broadcast([P, NT, NEXP]), ALU.mult))
                    nc.vector.tensor_tensor(comb, comb, eq, ALU.add).then_inc(s_e, 1)
                    for u in range(2 * NT):
                        dve.wait_ge(s_bm, u + 1)
                        part = tokB[:, u // 2, (u % 2) * 512:(u % 2 + 1) * 512]
                        nc.vector.tensor_tensor(part, bank[u % 4][0:P, :], part, ALU.add).then_inc(s_be, 1)

        def phase_moe():
            s_f, s_ge, s_tm, s_ae = (sem("moe_" + x) for x in ("up", "gelu", "down", "added"))
            s0 = take(2 * NEXP)
            ht = stage1[:, 0:2 * N].rearrange("p (m n) -> p m n", m=2)
            units = [(m, ch, a, w) for m in range(2) for ch, (a, w) in enumerate(FCH)]
            with nc.Block() as block:
                @block.sync
                def _(sp):
                    load_slots(sp, s0 + 2 * NEXP + 2)

                @block.tensor
                def _(pe):
                    with pe.Fori(0, NEXP) as e:
                        w_wait(pe, s0, e, 16)
                        w = ring_k(s0 % 2, KD, EH)
                        for j, (m, ch, a, wd) in enumerate(units):
                            pe.wait_ge(s_ge, e * 6 + j + 1)
                            for k in range(KD):
                                x = nc.tensor.matmul(bank[4 + ch][:, 0:wd], w[:, k, m * 128:(m + 1) * 128],
                                                     featA[:, k, a:a + wd], start=(k == 0), stop=(k == KD - 1))
                            x.then_inc(s_f, 1)
                        pe.wait_ge(s_f, e * 6 + 6)
                        pe.sem_inc(w_used, 1)
                        w_wait(pe, s0 + 1, e, 16)
                        w = ring_k((s0 + 1) % 2, 2, D)
                        pe.wait_ge(s_ge, e * 6 + 6 + 3)
                        for t in range(NT):
                            for n in range(2):
                                u = t * 2 + n
                                pe.wait_ge(s_ae, e * 2 * NT + u + 1)
                                for k in range(2):
                                    x = nc.tensor.matmul(bank[u % 4][0:P, :], ht[:, k, t * P:(t + 1) * P],
                                                         w[:, k, n * 512:(n + 1) * 512], start=(k == 0), stop=(k == 1))
                                x.then_inc(s_tm, 1)
                        pe.wait_ge(s_tm, (e + 1) * 2 * NT)
                        pe.sem_inc(w_used, 1)

                @block.scalar
                def _(act):
                    act.sem_inc(s_ge, 3)
                    with act.Fori(0, NEXP) as e:
                        for j, (m, ch, a, wd) in enumerate(units):
                            act.wait_ge(s_f, e * 6 + j + 1)
                            hold(act)
                            nc.scalar.activation(ht[:, m, a:a + wd], bank[4 + ch][:, 0:wd], ACT.Gelu,
                                                 bias=bcol[:, ds(e * 2 + 12 + m, 1)]).then_inc(s_ge, 1)

                @block.vector
                def _(dve):
                    dve.sem_inc(s_ae, 4)
                    flat = comb.rearrange("p t n -> p (t n)")
                    with dve.Fori(0, NEXP) as e:
                        for u in range(2 * NT):
                            t, n = divmod(u, 2)
                            part = tokB[:, t, n * 512:(n + 1) * 512]
                            dve.wait_ge(s_tm, e * 2 * NT + u + 1)
                            nc.vector.scalar_tensor_tensor(out=part, in0=bank[u % 4][0:P, :],
                                                           scalar=flat[:, ds(e + t * NEXP, 1)], in1=part,
                                                           op0=ALU.mult, op1=ALU.add).then_inc(s_ae, 1)

        xlr = bigC[0:P, 0:NT * 2 * HID].rearrange("p (t n) -> p t n", t=NT)
        self_score = small[0:P, 208:208 + NT * GH].rearrange("p (t h) -> p t h", t=NT)

        def phase_gat_in():
            (s_own, s_rq, s_sq, s_w, s_mm, s_ev, s_tr, s_te, s_lr, s_le, s_st, s_at) = (sem("gi_" + x) for x in (
                "own", "sumsq", "sqrt", "scaled", "mm", "evac", "turned", "turnedevac", "lr", "lrevac", "stored", "att"))
            s0 = take(2)
            rq = small[0:P, 160:160 + NT]
            xd = stage1[0:P, :].rearrange("p (t n) -> p t n", t=NT)
            xdT = stage2[:, 0:2 * N].rearrange("p (k n) -> p k n", k=2)
            att = stage3[0:P, 0:HID]
            zs = bigC[0:P, 2 * D * 3:2 * D * 3 + NT * HID]
            with nc.Block() as block:
                @block.sync
                def _(sp):
                    sp.dma_start(att, A["L1_gnn_att_row"].rearrange("(o n) -> o n", o=1)
                                 .to_broadcast([P, HID])).then_inc(s_at, 16)
                    load_slots(sp, s0 + 2)
                    sp.wait_ge(s_le, NT)
                    sp.dma_start(ptile(XL), xlr[:, :, 0:HID]).then_inc(s_st, 16)
                    load_slots(sp, s0 + 4)
                    sp.wait_ge(s_st, 16)

                @block.vector
                def _(dve):
                    st = Steps(dve, s_own)
                    nc.vector.tensor_scalar(rq, rq, 1.0 / D, 1e-6, ALU.mult, ALU.add).then_inc(s_rq, 1)
                    w_wait(dve, s0)
                    w = ring_k(s0 % 2, KD, CW)
                    gains = bcol[:, 48:48 + KD].rearrange("p (k o) -> p k o", o=1).to_broadcast([128, KD, CW])
                    nc.vector.tensor_tensor(w, w, gains, ALU.mult).then_inc(s_w, 1)
                    dve.wait_ge(s_sq, 1)
                    nc.vector.reciprocal(rq, rq).then_inc(s_rq, 1)
                    for t in range(NT):
                        dve.wait_ge(s_tr, t + 1)
                        nc.vector.tensor_copy(xdT[:, :, t * P:(t + 1) * P],
                                              bank[4 + t % 2][:, 0:2 * P].rearrange("p (k n) -> p k n", k=2)
                                              ).then_inc(s_te, 1)
                    dve.wait_ge(s_le, NT)
                    dve.wait_ge(s_at, 16)
                    zt = zs.rearrange("p (t n) -> p t n", t=NT)
                    st.link(nc.vector.tensor_tensor(zt, xlr[:, :, 0:HID], xlr[:, :, HID:2 * HID], ALU.add))
                    st.link(nc.vector.scalar_tensor_tensor(out=zs, in0=zs, scalar=0.2, in1=zs, op0=ALU.mult,
                                                           op1=ALU.max))
                    st.link(nc.vector.tensor_tensor(zt, zt, att.rearrange("p (o n) -> p o n", o=1)
                                                    .to_broadcast([P, NT, HID]), ALU.mult))
                    nc.vector.tensor_reduce(self_score.rearrange("p t h -> p (t h)"),
                                            zs.rearrange("p (h n) -> p h n", n=GD), AX.X, ALU.add)

                @block.scalar
                def _(act):
                    act.wait_ge(s_rq, 1)
                    nc.scalar.sqrt(rq, rq).then_inc(s_sq, 1)
                    act.wait_ge(s_rq, 2)
                    for t in range(NT):
                        act.wait_ge(s_mm, t + 1)
                        nc.scalar.activation(xd[:, t, :], bank[t % 4][0:P, 0:CW], ACT.Copy,
                                             scale=rq[:, t:t + 1]).then_inc(s_ev, 1)
                    for t in range(NT):
                        act.wait_ge(s_lr, t + 1)
                        nc.scalar.copy(xlr[:, t, :], bank[t % 4][0:P, :]).then_inc(s_le, 1)

                @block.tensor
                def _(pe):
                    pe.wait_ge(s_w, 1)
                    w = ring_k(s0 % 2, KD, CW)
                    for t in range(NT):
                        if t >= 4:
                            pe.wait_ge(s_ev, t - 3)
                        for k in range(KD):
                            m = nc.tensor.matmul(bank[t % 4][0:P, 0:CW], featA[:, k, t * P:(t + 1) * P], w[:, k, :],
                                                 start=(k == 0), stop=(k == KD - 1))
                        m.then_inc(s_mm, 1)
                    pe.wait_ge(s_mm, NT)
                    pe.sem_inc(w_used, 1)
                    for t in range(NT):
                        pe.wait_ge(s_ev, t + 1)
                        if t >= 2:
                            pe.wait_ge(s_te, t - 1)
                        for k in range(2):
                            m = nc.tensor.transpose(bank[4 + t % 2][:, k * P:(k + 1) * P], xd[:, t, k * 128:(k + 1) * 128],
                                                    ident[0:P, 0:P])
                        m.then_inc(s_tr, 1)
                    w_wait(pe, s0 + 1)
                    w = ring_k((s0 + 1) % 2, 4, HID)
                    for t in range(NT):
                        pe.wait_ge(s_te, t + 1)
                        if t >= 4:
                            pe.wait_ge(s_le, t - 3)
                        for side in range(2):
                            for k in range(2):
                                m = nc.tensor.matmul(bank[t % 4][0:P, side * HID:(side + 1) * HID],
                                                     xdT[:, k, t * P:(t + 1) * P], w[:, 2 * side + k, :],
                                                     start=(k == 0), stop=(k == 1))
                        m.then_inc(s_lr, 1)
                    pe.wait_ge(s_lr, NT)
                    pe.sem_inc(w_used, 1)

        def phase_gat():
            (s_d, s_g0, s_g1, s_oh, s_oht, s_ohc, s_z, s_zt, s_e, s_sp, s_spt, s_spc, s_bc, s_tm, s_mn, s_sc, s_me,
             s_x, s_p, s_r, s_ag, s_acc, s_own, s_dn, s_idx) = (sem("g_" + x) for x in (
                 "tile", "gather0", "gather1", "onehot", "onehotT", "onehotTcopy", "z", "leaky", "score", "parts",
                 "partsT", "partsTcopy", "rows", "tilemax", "newmax", "rescale", "maxback", "shifted", "p", "rhs",
                 "agg", "acc", "own", "tiledone", "idx"))
            s_idx2, s_fin, s_rl = sem("g_inner"), sem("g_final"), sem("g_relu")
            s_g = [s_g0, s_g1]
            pos = [2 * D * 3]

            def inC(n, parts=P):
                a = pos[0]
                pos[0] += n
                assert pos[0] <= NT * N
                return bigC[0:parts, a:a + n]

            xg = stage1[0:P, 0:2 * HB * HID].rearrange("p (h g n) -> p h g n", h=2, g=HB)
            zt = stage2[:, 0:2 * 2 * 500].rearrange("p (h k n) -> p h k n", h=2, k=2)
            junk = stage3[0:P, 0:1000].rearrange("p (h n) -> p h n", h=2)
            neg = stage3[0:P, 1000:2000].rearrange("p (h n) -> p h n", h=2)
            oh = inC(1000).rearrange("p (h g n) -> p h g n", h=2, g=HB)
            oht = inC(1000).rearrange("p (h n) -> p h n", h=2)
            rhs = inC(2 * HB * (HID + GH)).rearrange("p (h g n) -> p h g n", h=2, g=HB)
            xrd = inC(HID)
            acc = inC(HID + GH)
            spt = inC(500, 12).bitcast(BF16).rearrange("p (h n) -> p h n", h=2)
            sel = inC(250, 12).bitcast(BF16).rearrange("p (h n) -> p h n", h=GH)
            attm = inC(2 * GH, 128).rearrange("p (k h) -> p k h", k=2)
            sp = inC(2 * HB * 12 // 2).bitcast(BF16).rearrange("p (h g n) -> p h g n", h=2, g=HB)
            tiny = inC(256)
            es, r1, r2, xs = (tiny[:, 32 * i:32 * i + 32].rearrange("p (h g n) -> p h g n", h=2, g=HB)
                              for i in range(4))
            m_ = tiny[:, 128:132]
            mn5 = tiny[:, 132:142].rearrange("p (h n) -> p h n", h=2)
            tm = tiny[:, 142:150].rearrange("p (h n) -> p h n", h=2)
            dm = tiny[:, 150:158].rearrange("p (h n) -> p h n", h=2)
            out_ = tiny[:, 158:166].rearrange("p (h g) -> p h g", h=2)
            rden = tiny[:, 166:170]
            idx = tiny[:, 170:178].bitcast(I32).rearrange("p (h g) -> p h g", h=2)
            gout = bigB[0:P, 0:NT * HID].rearrange("p (t n) -> p t n", t=NT)
            by_head = lambda v: v.rearrange("p (h n) -> p h n", n=GD)
            ov = lambda v, n: v.rearrange("p (h o) -> p h o", o=1).to_broadcast([P, v.shape[1], n])
            small_bank = [bank[6], bank[7]]

            with nc.Block() as block:
                @block.gpsimd
                def _(pool):
                    with pool.Fori(0, NT) as d:
                        lo, cnt, base = batches(pool, d)
                        with pool.Fori(0, cnt) as r:
                            for h in range(2):
                                pool.wait_ge(s_r, ((base + r) * 2 + h + 1))
                                hold(pool)
                                nc.gpsimd.tensor_copy(idx[:, h, :], src_i[:, ds(batch(lo, r) * SUB + h * HB, HB)]
                                                      ).then_inc(s_idx, 1)
                                pool.wait_ge(s_idx, (base + r) * 2 + h + 1)
                                hold(pool)
                                for g in range(HB):
                                    nc.gpsimd.indirect_dma_start(
                                        out=xg[:, h, g, :], out_offset=None, in_=XL,
                                        in_offset=bass.IndirectOffsetOnAxis(ap=idx[:, h, g:g + 1].bitcast(U32), axis=0),
                                        ).then_inc(s_g[h], 16)

                @block.tensor
                def _(pe):
                    pe.wait_ge(s_d, 1)
                    with pe.Fori(0, NT) as d:
                        lo, cnt, base = batches(pe, d)
                        pe.wait_ge(s_d, d + 2)
                        hold(pe)
                        with pe.Fori(0, cnt) as r:
                            step = base + r
                            n = lambda h: step * 2 + h + 1
                            for h in range(2):
                                pe.wait_ge(s_oh, n(h))
                                for g in range(HB):
                                    m = nc.tensor.transpose(bank[h][0:P, g * P:(g + 1) * P], oh[:, h, g, :],
                                                            ident[0:P, 0:P])
                                m.then_inc(s_oht, 1)
                            for h in range(2):
                                pe.wait_ge(s_ohc, n(h))
                                pe.wait_ge(s_g[h], step * 64 + 64)
                                for k in range(2):
                                    b = bank[2 + 2 * h + k]
                                    nc.tensor.matmul(b[:, 0:500], xrd[:, k * 128:(k + 1) * 128], oht[:, h, :],
                                                     start=True, stop=False, skip_group_check=True)
                                    for g in range(HB):
                                        m = nc.tensor.matmul(b[:, g * P:(g + 1) * P], xg[:, h, g, k * 128:(k + 1) * 128],
                                                             ident[0:P, 0:P], start=False, stop=(g == HB - 1),
                                                             skip_group_check=True)
                                m.then_inc(s_z, 1)
                            for h in range(2):
                                pe.wait_ge(s_zt, n(h))
                                for g in range(HB):
                                    for k in range(2):
                                        m = nc.tensor.matmul(small_bank[h][0:P, g * GH:(g + 1) * GH],
                                                             zt[:, h, k, g * P:(g + 1) * P], attm[:, k, :],
                                                             start=(k == 0), stop=(k == 1))
                                m.then_inc(s_e, 1)
                            for h in range(2):
                                pe.wait_ge(s_sp, n(h))
                                hold(pe)
                                for g in range(HB):
                                    m = nc.tensor.transpose(
                                        small_bank[h][0:12, 64:64 + 250].bitcast(BF16)[:, g * P:(g + 1) * P] if P % 2 == 0
                                        else small_bank[h][0:12, 64:64 + 256].bitcast(BF16)[:, g * 128:g * 128 + P],
                                        sp[:, h, g, :], ident16[0:P, 0:P])
                                m.then_inc(s_spt, 1)
                            for h in range(2):
                                pe.wait_ge(s_spc, n(h))
                                for hd in range(GH):
                                    u = h * GH + hd
                                    if u >= 6:
                                        pe.wait_ge(s_tm, step * 8 + u - 5)
                                    hold(pe)
                                    nc.tensor.matmul(bank[u % 6][0:P, 0:500], sel[:, hd, :], spt[:, h, :],
                                                     start=True, stop=True).then_inc(s_bc, 1)
                            for h in range(2):
                                pe.wait_ge(s_mn, n(h))
                                for g in range(HB):
                                    m = nc.tensor.matmul(small_bank[h][0:P, 320 + g * 5:325 + g * 5],
                                                         oht[:, h, g * P:(g + 1) * P], mn5[:, h, :], start=True,
                                                         stop=True)
                                m.then_inc(s_me, 1)
                                pe.wait_ge(s_r, n(h) + 2)
                                for g in range(HB):
                                    m = nc.tensor.matmul(small_bank[h][0:P, 0:HID + GH], oh[:, h, g, :], rhs[:, h, g, :],
                                                         start=(g == 0), stop=(g == HB - 1))
                                m.then_inc(s_ag, 1)
                    pe.wait_ge(s_dn, NT)
                    for t in range(NT):
                        for k in range(2):
                            c = t * 2 + k
                            m = nc.tensor.transpose(bank[c // 4][:, (c % 4) * P:(c % 4 + 1) * P],
                                                    gout[:, t, k * 128:(k + 1) * 128], ident[0:P, 0:P])
                    m.then_inc(s_dn, 1)

                @block.scalar
                def _(act):
                    act.sem_inc(s_acc, 2)
                    with act.Fori(0, NT) as d:
                        lo, cnt, base = batches(act, d)
                        with act.Fori(0, cnt) as r:
                            step = base + r
                            n = lambda h: step * 2 + h + 1
                            for h in range(2):
                                act.wait_ge(s_oht, n(h))
                                nc.scalar.copy(oht[:, h, :], bank[h][0:P, 0:500]).then_inc(s_ohc, 1)
                            for h in range(2):
                                act.wait_ge(s_z, n(h))
                                for k in range(2):
                                    m = nc.scalar.activation(zt[:, h, k, :], bank[2 + 2 * h + k][:, 0:500], ACT.Relu,
                                                             scale=0.8)
                                m.then_inc(s_rl, 1)
                            for h in range(2):
                                act.wait_ge(s_spt, n(h))
                                nc.scalar.copy(spt[:, h, :].rearrange("p (g n) -> p g n", g=HB),
                                               small_bank[h][0:12, 64:64 + 256].bitcast(BF16)
                                               .rearrange("p (g n) -> p g n", g=HB)[:, :, 0:P]).then_inc(s_spc, 1)
                            for h in range(2):
                                act.wait_ge(s_mn, n(h))
                                nc.scalar.activation(dm[:, h, :], dm[:, h, :], ACT.Exp).then_inc(s_sc, 1)
                                act.wait_ge(s_x, n(h))
                                nc.scalar.activation(rhs[:, h, :, HID:HID + GH], xs[:, h], ACT.Exp).then_inc(s_p, 1)
                    act.wait_ge(s_dn, NT + 1)
                    for t in range(NT):
                        c = t * 2
                        nc.scalar.copy(gatT[:, :, t * P:(t + 1) * P],
                                       bank[c // 4][:, (c % 4) * P:(c % 4 + 2) * P].rearrange("p (k n) -> p k n", k=2))

                @block.vector
                def _(dve):
                    nc.vector.memset(attm, 0.0)
                    st = Steps(dve, s_own)
                    t12 = tiny[0:12, 180:184]
                    st.link(nc.vector.tensor_tensor(t12, ident[0:12, 0:4], ident[0:12, 4:8], ALU.add))
                    st.link(nc.vector.tensor_tensor(t12, t12, ident[0:12, 8:12], ALU.add))
                    nc.vector.tensor_copy(sel, t12.rearrange("p (h o) -> p h o", o=1).to_broadcast([12, GH, P]))
                    for k in range(2):
                        for i in range(2):
                            nc.vector.tensor_tensor(attm[:, k, 2 * k + i:2 * k + i + 1], bcol[:, 56 + k:57 + k],
                                                    blocks[:, 64 * i:64 * i + 1], ALU.mult)
                    st.link(nc.vector.memset(mn5, 1.0))
                    nc.vector.sem_inc(s_d, 1)
                    dve.sem_inc(s_r, 2)
                    with dve.Fori(0, NT) as d:
                        lo, cnt, base = batches(dve, d)
                        row = lambda a, b: xlr[:, ds(d, 1), a:b].rearrange("p o n -> p (o n)")
                        nc.vector.tensor_copy(xrd, row(HID, 2 * HID))
                        nc.vector.tensor_copy(acc[:, 0:HID], row(0, HID))
                        nc.vector.memset(acc[:, HID:HID + GH], 1.0)
                        nc.vector.tensor_copy(m_, self_score[:, ds(d, 1), :].rearrange("p o h -> p (o h)")
                                              ).then_inc(s_d, 1)
                        dve.wait_ge(s_d, d + 2)
                        hold(dve)
                        with dve.Fori(0, cnt) as r:
                            step = base + r
                            st = Steps(dve, s_idx2, step, 22)
                            n = lambda h: step * 2 + h + 1
                            for h in range(2):
                                dve.wait_ge(s_acc, n(h))
                                nc.vector.tensor_tensor(
                                    oh[:, h], iota16[:, ds(d * P, P)].rearrange("p (o n) -> p o n", o=1)
                                    .to_broadcast([P, HB, P]),
                                    dst_f[:, ds(batch(lo, r) * SUB + h * HB, HB)].rearrange("p (q o) -> p q o", o=1)
                                    .to_broadcast([P, HB, P]), ALU.is_equal).then_inc(s_oh, 1)
                            for h in range(2):
                                dve.wait_ge(s_ohc, n(h))
                                nc.vector.tensor_scalar(neg[:, h, :], oht[:, h, :], 1.0, BIG, ALU.subtract, ALU.mult)
                            for h in range(2):
                                dve.wait_ge(s_rl, n(h))
                                for k in range(2):
                                    x = nc.vector.scalar_tensor_tensor(
                                        out=zt[:, h, k, :], in0=bank[2 + 2 * h + k][:, 0:500], scalar=0.2,
                                        in1=zt[:, h, k, :], op0=ALU.mult, op1=ALU.add)
                                x.then_inc(s_zt, 1)
                            for h in range(2):
                                dve.wait_ge(s_e, n(h))
                                b = small_bank[h][0:P, 0:HB * GH].rearrange("p (g n) -> p g n", g=HB)
                                part = lambda i: sp[:, h, :, i * GH:(i + 1) * GH]
                                st.link(nc.vector.tensor_copy(es[:, h], b))
                                st.link(nc.vector.tensor_copy(part(0), es[:, h]))
                                st.link(nc.vector.tensor_tensor(r1[:, h], es[:, h], part(0), ALU.subtract))
                                st.link(nc.vector.tensor_copy(part(1), r1[:, h]))
                                st.link(nc.vector.tensor_tensor(r2[:, h], r1[:, h], part(1), ALU.subtract))
                                nc.vector.tensor_copy(part(2), r2[:, h]).then_inc(s_sp, 1)
                            for h in range(2):
                                for hd in range(GH):
                                    u = h * GH + hd
                                    dve.wait_ge(s_bc, step * 8 + u + 1)
                                    if u >= 1:
                                        dve.wait_ge(s_tm, step * 8 + u)
                                    hold(dve)
                                    nc.vector.tensor_tensor_reduce(junk[:, 0, :], bank[u % 6][0:P, 0:500], neg[:, h, :],
                                                                   1.0, -BIG, ALU.add, ALU.max,
                                                                   tm[:, h, hd:hd + 1]).then_inc(s_tm, 1)
                            for h in range(2):
                                if h == 0:
                                    dve.wait_ge(s_tm, step * 8 + 4)
                                else:
                                    dve.wait_ge(s_tm, step * 8 + 8)
                                st.link(nc.vector.tensor_tensor(mn5[:, h, 0:GH], m_, tm[:, h, :], ALU.max))
                                st.link(nc.vector.tensor_tensor(dm[:, h, :], m_, mn5[:, h, 0:GH], ALU.subtract))
                                nc.vector.tensor_copy(m_, mn5[:, h, 0:GH]).then_inc(s_mn, 1)
                                dve.wait_ge(s_mn, n(h))
                            for h in range(2):
                                dve.wait_ge(s_me, n(h))
                                me = small_bank[h][0:P, 320:320 + 5 * HB].rearrange("p (g n) -> p g n", g=HB)
                                oo = out_[:, h, :].rearrange("p (g o) -> p g o", o=1)
                                st.link(nc.vector.tensor_tensor(xs[:, h], es[:, h], me[:, :, 0:GH], ALU.subtract))
                                st.link(nc.vector.tensor_scalar(oo, me[:, :, GH:GH + 1], 1.0, BIG, ALU.subtract,
                                                                ALU.mult))
                                nc.vector.tensor_tensor(xs[:, h], xs[:, h], oo.to_broadcast([P, HB, GH]),
                                                        ALU.add).then_inc(s_x, 1)
                                dve.wait_ge(s_p, n(h))
                                for g in range(HB):
                                    x = nc.vector.tensor_tensor(
                                        by_head(rhs[:, h, g, 0:HID]), by_head(xg[:, h, g, :]),
                                        ov(rhs[:, h, g, HID:HID + GH], GD), ALU.mult)
                                x.then_inc(s_r, 1)
                                dve.wait_ge(s_sc, n(h))
                                st.link(nc.vector.tensor_tensor(by_head(acc[:, 0:HID]), by_head(acc[:, 0:HID]),
                                                                ov(dm[:, h, :], GD), ALU.mult))
                                st.link(nc.vector.tensor_tensor(acc[:, HID:HID + GH], acc[:, HID:HID + GH], dm[:, h, :],
                                                                ALU.mult))
                                dve.wait_ge(s_ag, n(h))
                                nc.vector.tensor_tensor(acc, acc, small_bank[h][0:P, 0:HID + GH], ALU.add
                                                        ).then_inc(s_acc, 1)
                                dve.wait_ge(s_acc, n(h) + 2)
                            st.end()
                        so2 = Steps(dve, s_fin, d, 2)
                        so2.link(nc.vector.tensor_scalar(rden, acc[:, HID:HID + GH], 1e-16, None, ALU.add))
                        so2.link(nc.vector.reciprocal(rden, rden))
                        nc.vector.tensor_tensor(gout[:, ds(d, 1), :].rearrange("p o (h n) -> p (o h) n", h=GH),
                                                by_head(acc[:, 0:HID]), ov(rden, GD), ALU.mult).then_inc(s_dn, 1)
                        dve.wait_ge(s_dn, d + 1)

        w1T = bigB[:, 5120:5120 + KD * 512].rearrange("p (k n) -> p k n", k=KD)
        w2T = ring[:, :].rearrange("p i k n -> p (i k n)")[:, 0:4 * D].rearrange("p (k n) -> p k n", k=4)

        def phase_binarize():
            s_ab, s_sg, s_own, s_tr, s_ev = (sem("bw_" + x) for x in ("abs", "sign", "own", "turned", "evac"))
            s_trb = sem("bw_banks")
            s_ld = [sem(f"bw_in{i}") for i in range(2)]
            pieces = [(A["L1_ffn_w1"], j, D, w1T) for j in range(4)] + [(A["L1_ffn_w2"], j, 512, w2T) for j in range(8)]
            wn = [x[:, 0:D] for x in (stage1, stage2)]
            sg = stage3[:, 0:2 * D].rearrange("p (i n) -> p i n", i=2)
            def evac(dve, q):
                src, j, n, dst = pieces[q]
                for b in range(n // 512):
                    dve.wait_ge(s_trb, sum(p[2] // 512 for p in pieces[:q]) + b + 1)
                    nc.vector.tensor_copy(dst[:, 4 * b:4 * b + 4, j * 128:(j + 1) * 128],
                                          bank[2 * (q % 2) + b][:, :].rearrange("p (k n) -> p k n", k=4)
                                          ).then_inc(s_ev, 1)

            with nc.Block() as block:
                @block.sync
                def _(sp):
                    for q, (src, j, n, _) in enumerate(pieces):
                        if q >= 2:
                            sp.wait_ge(s_tr, q - 1)
                        sp.dma_start(wn[q % 2][:, 0:n], src[j * 128:(j + 1) * 128, :]).then_inc(s_ld[q % 2], 16)

                @block.scalar
                def _(act):
                    for q, (src, j, n, dst) in enumerate(pieces):
                        act.wait_ge(s_ld[q % 2], 16 * (q // 2) + 16)
                        if q >= 2:
                            act.wait_ge(s_ab, q - 1)
                        nc.scalar.sign(sg[:, q % 2, 0:n], wn[q % 2][:, 0:n]).then_inc(s_sg, 1)

                @block.vector
                def _(dve):
                    st = Steps(dve, s_own)
                    for q, (src, j, n, dst) in enumerate(pieces):
                        w, s = wn[q % 2][:, 0:n], sg[:, q % 2, 0:n]
                        mean = small[:, 250:251]
                        dve.wait_ge(s_ld[q % 2], 16 * (q // 2) + 16)
                        st.link(nc.vector.tensor_reduce(mean, w, AX.X, ALU.add, apply_absolute_value=True))
                        st.link(nc.vector.tensor_scalar(mean, mean, 1.0 / n, None, ALU.mult))
                        dve.wait_ge(s_sg, q + 1)
                        st.link(nc.vector.scalar_tensor_tensor(out=s, in0=s, scalar=mean, in1=w, op0=ALU.mult,
                                                               op1=ALU.subtract))
                        nc.vector.tensor_tensor(w, w, s, ALU.add).then_inc(s_ab, 1)
                        dve.wait_ge(s_ab, q + 1)
                        if q:
                            evac(dve, q - 1)
                    evac(dve, len(pieces) - 1)

                @block.tensor
                def _(pe):
                    for q, (src, j, n, dst) in enumerate(pieces):
                        pe.wait_ge(s_ab, q + 1)
                        if q >= 2:
                            pe.wait_ge(s_ev, sum(p[2] // 512 for p in pieces[:q - 1]))
                        for k in range(n // 128):
                            m = nc.tensor.transpose(bank[2 * (q % 2) + k // 4][:, (k % 4) * 128:(k % 4 + 1) * 128],
                                                    wn[q % 2][:, k * 128:(k + 1) * 128], ident[:, :])
                            if k % 4 == 3:
                                m.then_inc(s_trb, 1)
                        pe.wait_ge(s_trb, sum(p[2] // 512 for p in pieces[:q + 1]))
                        pe.sem_inc(s_tr, 1)

        phase_start()
        if stop >= 1:
            phase_norm("n0", load=A["x"], store=XN)
        if stop >= 2:
            phase_h0()
        if stop >= 3:
            phase_edges0()
        if stop >= 4:
            phase_agg0()
        if stop >= 5:
            phase_mix("m0", True)
        if stop >= 6:
            phase_out("o0", lambda k, t: featB[:, k, t * P:(t + 1) * P], KD, A["L0_mix_bo"], XN)
        if stop >= 7:
            phase_norm("na", gain=(A["L0_mix_g1"], A["L0_mix_be1"]), keep=True, eps=1e-12)
        if stop >= 8:
            phase_up("u0", None, COLS["L0_mix_b1"][0])
        if stop >= 9:
            phase_down("d0", None, A["L0_mix_b2"])
        if stop >= 10:
            phase_norm("nb", gain=(A["L0_mix_g2"], A["L0_mix_be2"]), add=XR, keep=True, turn=False, eps=1e-12)
        if stop >= 11:
            phase_norm("n1", keep_sum=True)
        if stop >= 12:
            phase_route()
        if stop >= 13:
            phase_moe()
            recycle()
        if stop >= 14:
            phase_norm("n2", tok=tokB, store_src=XR, rms=160)
        if stop >= 15:
            phase_gat_in()
        if stop >= 16:
            phase_gat()
        if stop >= 17:
            phase_mix("m1", False)
        if stop >= 18:
            phase_out("o1", lambda k, t: (featB if k < KD else gatT)[:, k % KD, t * P:(t + 1) * P], KD + 2,
                      A["L1_mix_b_proj"], XR)
        if stop >= 19:
            phase_norm("n3")
            phase_binarize()
            phase_up("u1", lambda m: w1T[:, :, m * 128:(m + 1) * 128], COLS["L1_ffn_b1"][0])
        if stop >= 20:
            phase_down("d1", lambda c: w2T[:, :, c * 512:(c + 1) * 512], A["L1_ffn_b2"], dram=out)
        if stop < 20:
            with nc.Block() as block:
                @block.sync
                def _(sp):
                    for i in range(2):
                        if fulls[i]:
                            sp.wait_ge(w_full[i], fulls[i][-1])


def kernel(**inputs):
    import numpy as _np
    import concourse.bacc as _bacc
    from concourse import mybir as _mybir
    from concourse.bass_utils import run_bass_kernel_spmd as _run

    nc = _bacc.Bacc("TRN2", target_bir_lowering=False, num_devices=1)
    given = {name: _np.asarray(a) for name, a in inputs.items()}
    given["L1_gnn_att_row"] = given["L1_gnn_att"].reshape(-1)
    arrays, aps = {}, {}
    for name, a in given.items():
        if name in COLS:
            a = a.reshape(-1, 128).T
        a = _np.ascontiguousarray(a)
        arrays[f"in_{name}"] = a
        aps[name] = nc.dram_tensor(f"in_{name}", a.shape, _mybir.dt.from_np(a.dtype), kind="ExternalInput").ap()
    out = nc.dram_tensor("out", (N, D), F32, kind="ExternalOutput").ap()
    build(nc, aps, out)
    return _run(nc, [arrays], core_ids=[0]).results[0]["out"]
```

```python
from contextlib import ExitStack

import concourse.bass as bass
from concourse import mybir

F32 = mybir.dt.float32
F32R = mybir.dt.float32r
F16 = mybir.dt.float16
BF16 = mybir.dt.bfloat16
I32 = mybir.dt.int32
U32 = mybir.dt.uint32
ALU = mybir.AluOpType
ACT = mybir.ActivationFunctionType
AX = mybir.AxisListType
ds = bass.ds

N = 1250
P = 125
NT = N // P
D = 1024
KD = D // 128
CW = 256
NC = D // CW
E = 40000
SUB = 8
BE = SUB * P
NB = E // BE
HB = SUB // 2
FCH = [(0, 500), (500, 500), (1000, 250)]
RCH = [(0, 418), (418, 416), (834, 416)]
NEXP = 16
EH = 256
HID = 256
GH = 4
GD = HID // GH
BIG = 1e30
COLS = {"L0_mix_bq": (0, 8), "L0_mix_b1": (8, 4), "L0_ffn_b1": (12, 32), "L1_ffn_b1": (44, 4),
        "L1_gnn_rms_w": (48, 8), "L1_gnn_att": (56, 2)}


class Steps:

    def __init__(self, eng, sem, turn=None, per=0, base=0):
        self.eng, self.sem, self.n, self.turn, self.per, self.base = eng, sem, 0, turn, per, base

    def value(self):
        return self.base + self.n if self.turn is None else self.turn * self.per + self.base + self.n

    def link(self, ins):
        self.n += 1
        ins.then_inc(self.sem, 1)
        self.eng.wait_ge(self.sem, self.value())

    def end(self):
        assert self.turn is None or self.n == self.per, (self.n, self.per)


def build(nc, A, out, stop=99):
    with ExitStack() as ctx:
        def sb(name, shape, dt=F32):
            return ctx.enter_context(nc.sbuf_tensor(name, shape, dt))

        phase_sems = []

        def sem(name):
            phase_sems.append(nc.alloc_semaphore(name=name))
            return phase_sems[-1]

        def stream_sem(name):
            return nc.alloc_semaphore(name=name)

        def recycle():
            nc.clear_and_free_semaphores(list(phase_sems))
            phase_sems.clear()
            nc.all_engine_barrier()

        def scratch(name, shape, dt=F32):
            return nc.dram_tensor(name, shape, dt, kind="Internal").ap()

        shapes = [("featA", [128, KD, N]),
                  ("bigB", [128, NT * D]),
                  ("bigC", [128, NT * N]),
                  ("ring", [128, 2, 10, CW])] + [
                  (f"stage{i}", [128, NT * CW]) for i in range(1, 5)]
        with ExitStack() as rounded:
            featA_r, bigB_r, bigC_r, ring_r, *stage_r = [
                rounded.enter_context(nc.sbuf_tensor(name + "_r", shape, F32R)) for name, shape in shapes]
        featA, bigB, bigC, ring, stage1, stage2, stage3, stage4 = [sb(name, shape) for name, shape in shapes]
        gatT = stage4[:, 0:2 * N].rearrange("p (k n) -> p k n", k=2)
        tokB = bigB[0:P, 0:NT * D].rearrange("p (t n) -> p t n", t=NT)
        tokC = bigC[0:P, 0:NT * D].rearrange("p (t n) -> p t n", t=NT)
        featB = bigB[:, 0:KD * N].rearrange("p (k n) -> p k n", k=KD)
        ident = sb("ident", [128, 128])
        ident16 = sb("ident16", [128, 128], BF16)
        ones = sb("ones", [128, 128])
        ids_i = sb("ids_i", [P, NT], I32)[:, :]
        ids = sb("ids", [P, NT])[:, :]
        blocks = sb("blocks", [128, 128])
        iota_i = bigC[0:P, NT * N // 2:NT * N // 2 + N].bitcast(I32)
        iota16 = sb("iota16", [P, N], F16)
        edge_i = sb("edge_i", [P, 2, NB * SUB], I32)
        src_i, dst_i = edge_i[:, 0, :], edge_i[:, 1, :]
        src_f = sb("src_f", [P, NB * SUB])
        dst_f = sb("dst_f", [P, NB * SUB])
        scores = sb("scores", [P, NB * SUB * GH])
        table = sb("table", [1, 4, NT], I32)
        small = sb("small", [128, 256])
        bcol = sb("bcol", [128, 64])
        edge_ix = sb("edge_ix", [P, 4, 2, HB], I32)
        attrow = sb("attrow", [P, HID])
        comb = sb("comb", [P, NT, NEXP])[:, :, :]
        bank = [ctx.enter_context(nc.psum_tensor(f"bank{i}", [128, 512], F32)) for i in range(8)]

        XR = scratch("XR", (N, D))
        XN = scratch("XN", (N, D))
        XL = scratch("XL", (N, HID))
        XRD = scratch("XRD", (N, HID))
        DR = scratch("DR", (NB + 1, BE), F16)
        ptile = lambda ap: ap.rearrange("(t p) n -> p t n", p=P)

        slots = []

        def chunked(w, n, cw=CW):
            v = w.rearrange("(k p) n -> p k n", p=128)
            for c in range(n):
                slots.append([(slice(0, v.shape[1]), v[:, :, c * cw:(c + 1) * cw])])

        w_full = [stream_sem("w_full0"), stream_sem("w_full1")]
        w_used = stream_sem("w_used")
        loaded = [0]
        took = [0]

        def ring_k(i, nk, cw, ring=ring):
            return ring[:, i].rearrange("p k n -> p (k n)")[:, 0:nk * cw].rearrange("p (k n) -> p k n", k=nk)

        def load_slots(sp, upto):
            while loaded[0] < min(upto, len(slots)):
                s = loaded[0]
                if s >= 2:
                    sp.wait_ge(w_used, s - 1)
                parts = slots[s]
                for kk, v in parts:
                    nk, cw = v.shape[1], v.shape[2]
                    dst = ring[:, s % 2, kk, :] if cw == CW else ring_k(s % 2, nk, cw)
                    sp.dma_start(dst, v).then_inc(w_full[s % 2], 16)
                fulls[s % 2].append((fulls[s % 2][-1] if fulls[s % 2] else 0) + 16 * len(parts))
                loaded[0] += 1

        fulls = [[], []]

        def full_value(s):
            return sum(16 * len(slots[q]) for q in range(s % 2, s + 1, 2))

        chunked(A["L0_gnn_W"], NC)
        q0 = [A[f"L0_mix_W{x}"].rearrange("(k p) n -> p k n", p=128) for x in "qkv"]
        for c in range(NC):
            for w in q0:
                slots.append([(slice(0, KD), w[:, :, c * CW:(c + 1) * CW])])
        chunked(A["L0_mix_Wo"], NC)
        chunked(A["L0_mix_W1"], 2)
        chunked(A["L0_mix_W2"], 2, 512)
        for e in range(NEXP):
            slots.append([(slice(0, KD), A["L0_ffn_W1"][e].rearrange("(k p) n -> p k n", p=128))])
            slots.append([(slice(0, 2), A["L0_ffn_W2"][e].rearrange("(k p) n -> p k n", p=128))])
        chunked(A["L1_gnn_W_down"], 1)
        wl = A["L1_gnn_Wl"].rearrange("(k p) n -> p k n", p=128)
        wr = A["L1_gnn_Wr"].rearrange("(k p) n -> p k n", p=128)
        slots.append([(slice(0, 2), wl), (slice(2, 4), wr)])
        qkv = A["L1_mix_W_qkv"].rearrange("(k p) n -> p k n", p=128)
        for c in range(NC):
            for j in range(3):
                slots.append([(slice(0, KD), qkv[:, :, j * D + c * CW:j * D + (c + 1) * CW])])
        wp = A["L1_mix_W_proj"].rearrange("(k p) n -> p k n", p=128)
        wu = A["L1_gnn_W_up"].rearrange("(k p) n -> p k n", p=128)
        for c in range(NC):
            slots.append([(slice(0, KD), wp[:, :, c * CW:(c + 1) * CW]),
                          (slice(KD, KD + 2), wu[:, :, c * CW:(c + 1) * CW])])

        def take(n):
            s = took[0]
            took[0] += n
            return s

        def w_wait(eng, s, turn=None, per=0):
            eng.wait_ge(w_full[s % 2], full_value(s) if turn is None else turn * per + full_value(s))


        idle = stream_sem("idle")

        def hold(eng):
            eng.sem_inc(idle, 1)

        def row_bc(v, n):
            return v.rearrange("(o n) -> o n", o=1).to_broadcast([P, n])

        def phase_start():
            s_bc = sem("columns_in")
            s_ld, s_c, s_t, s_x, s_p = sem("edges_in"), sem("consts"), sem("start_dve"), sem("start_pe"), sem("start_pool")
            dw = stage1[0:NB, 0:BE].bitcast(I32)
            dwf = stage2[0:NB, 0:BE]
            dw16 = stage3[0:NB, 0:BE // 2].bitcast(F16)
            s_dr = sem("rows_stored")
            mm = small[0:NB, 0:2]
            row = small[0:1, 16:16 + 2 * NB]
            big = bigC[0:1, 0:8 * NT * NB].rearrange("p (a t b) -> p a t b", a=8, t=NT)
            with nc.Block() as block:
                @block.sync
                def _(sp):
                    for v, t in ((A["src"], src_i), (A["dst"], dst_i)):
                        sp.dma_start(t.rearrange("p (b g) -> p b g", g=SUB),
                                     v.rearrange("(b p g) -> p b g", p=P, g=SUB)).then_inc(s_ld, 16)
                    sp.dma_start(dw, A["dst"].rearrange("(b e) -> b e", b=NB)).then_inc(s_ld, 16)
                    for name, (at, n) in COLS.items():
                        sp.dma_start(bcol[:, at:at + n], A[name]).then_inc(s_bc, 16)
                    load_slots(sp, 2)
                    sp.wait_ge(s_bc, 16 * len(COLS))
                    sp.wait_ge(s_dr, 1)
                    sp.dma_start(DR[0:NB, :], dw16).then_inc(s_dr, 16)
                    sp.wait_ge(s_dr, 17)

                @block.gpsimd
                def _(pool):
                    nc.gpsimd.iota(iota_i[:], pattern=[[1, N]], base=0, channel_multiplier=0).then_inc(s_p, 1)
                    nc.gpsimd.iota(ids_i, pattern=[[P, NT]], base=0, channel_multiplier=1)
                    nc.gpsimd.memset(ones[:], 1.0).then_inc(s_p, 1)
                    pool.wait_ge(s_p, 2)
                    nc.gpsimd.affine_select(out=ident[:], in_=ones[:], compare_op=ALU.is_equal, fill=0.0, base=0,
                                            pattern=[[-1, 128]], channel_multiplier=1).then_inc(s_p, 1)
                    nc.gpsimd.memset(blocks[:], 0.0).then_inc(s_p, 1)
                    pool.wait_ge(s_p, 4)
                    nc.gpsimd.memset(blocks[0:64, 0:64], 1.0).then_inc(s_p, 1)
                    nc.gpsimd.memset(blocks[64:128, 64:128], 1.0).then_inc(s_p, 1)

                @block.tensor
                def _(pe):
                    pe.wait_ge(s_p, 6)
                    pe.wait_ge(s_t, 1)
                    for i in range(2):
                        last = nc.tensor.transpose(bank[0][0:1, i * NB:(i + 1) * NB], mm[:, i:i + 1], ident[0:NB, 0:NB])
                    last.then_inc(s_x, 1)

                @block.vector
                def _(dve):
                    st = Steps(dve, s_c)
                    dve.wait_ge(s_ld, 48)
                    nc.vector.tensor_copy(src_f[:], src_i)
                    nc.vector.tensor_copy(dst_f[:], dst_i)
                    nc.vector.tensor_copy(dw16, dw).then_inc(s_dr, 1)
                    st.link(nc.vector.tensor_copy(dwf, dw))
                    nc.vector.tensor_reduce(mm[:, 0:1], dwf, AX.X, ALU.max)
                    nc.vector.tensor_reduce(mm[:, 1:2], dwf, AX.X, ALU.min).then_inc(s_t, 1)
                    dve.wait_ge(s_p, 3)
                    nc.vector.tensor_copy(ident16[:], ident[:])
                    nc.vector.tensor_copy(ids, ids_i)
                    st.link(nc.vector.tensor_copy(iota16[:], iota_i[:]))
                    dve.wait_ge(s_x, 1)
                    st.link(nc.vector.tensor_copy(row, bank[0][0:1, 0:2 * NB]))
                    tile_at = iota16[0:1, 0:N:P].rearrange("p (t o) -> p t o", o=1).to_broadcast([1, NT, NB])
                    b_at = iota16[0:1, 0:NB].rearrange("p (o b) -> p o b", o=1).to_broadcast([1, NT, NB])
                    rows = row.rearrange("p (a o b) -> p a o b", a=2, o=1)
                    bmax, bmin = (rows[:, a].to_broadcast([1, NT, NB]) for a in range(2))
                    st.link(nc.vector.tensor_tensor(big[:, 0], bmax, tile_at, ALU.is_lt))
                    st.link(nc.vector.scalar_tensor_tensor(out=big[:, 1], in0=big[:, 0], scalar=1000.0, in1=b_at,
                                                           op0=ALU.mult, op1=ALU.add))
                    st.link(nc.vector.scalar_tensor_tensor(out=big[:, 2], in0=bmin, scalar=float(P), in1=tile_at,
                                                           op0=ALU.subtract, op1=ALU.is_lt))
                    st.link(nc.vector.scalar_tensor_tensor(out=big[:, 3], in0=b_at, scalar=1.0, in1=big[:, 2],
                                                           op0=ALU.add, op1=ALU.mult))
                    lo, hi, cnt, base = (small[0:1, 128 + 16 * i:128 + 16 * i + NT] for i in range(4))
                    st.link(nc.vector.tensor_reduce(lo, big[:, 1], AX.X, ALU.min))
                    st.link(nc.vector.tensor_reduce(hi, big[:, 3], AX.X, ALU.max))
                    st.link(nc.vector.tensor_scalar(lo, lo, float(NB - 1), None, ALU.min))
                    st.link(nc.vector.tensor_tensor(cnt, hi, lo, ALU.subtract))
                    st.link(nc.vector.tensor_scalar(cnt, cnt, 1.0, None, ALU.max))
                    st.link(nc.vector.memset(base[:, 0:1], 0.0))
                    for t in range(1, NT):
                        st.link(nc.vector.tensor_tensor(base[:, t:t + 1], base[:, t - 1:t], cnt[:, t - 1:t], ALU.add))
                    nc.vector.tensor_copy(table[:, 0], lo)
                    nc.vector.tensor_copy(table[:, 1], cnt)
                    nc.vector.tensor_copy(table[:, 2], base)

        def phase_norm(name, load=None, gain=None, add=None, keep=None, keep_sum=None, turn=True, store=None,
                       store_src=None, rms=None, eps=1e-5, tok=None):
            tok = tokC if tok is None else tok
            s_in = [sem(f"{name}_in{i}") for i in range(2)]
            s_ad = [sem(f"{name}_add{i}") for i in range(2)]
            s_st = [sem(f"{name}_stored{i}") for i in range(2)]
            s_row, s_va, s_sd, s_y, s_tr, s_ev, s_own = (sem(f"{name}_" + x) for x in
                                                         ("rows", "var", "sd", "y", "turned", "evac", "own"))
            xin = stage1[0:P, 0:2 * D].rearrange("p (i n) -> p i n", i=2)
            y = stage2[0:P, 0:2 * D].rearrange("p (i n) -> p i n", i=2)
            rows = stage3[0:P, 0:2 * D].rearrange("p (i n) -> p i n", i=2)
            ain = xin
            stores = [(store, y)] if store is not None else [(store_src, xin)] if store_src is not None else []
            with nc.Block() as block:
                @block.sync
                def _(sp):
                    if gain is not None:
                        for i in range(2):
                            sp.dma_start(rows[:, i], row_bc(gain[i], D)).then_inc(s_row, 16)
                    for t in range(NT + 2):
                        i = t % 2
                        if t >= 2:
                            sp.wait_ge(s_y, t - 1)
                            if store is not None:
                                sp.dma_start(store[(t - 2) * P:(t - 1) * P, :], y[:, i]).then_inc(s_st[i], 16)
                            if store_src is not None:
                                sp.dma_start(store_src[(t - 2) * P:(t - 1) * P, :],
                                             tok[:, t - 2]).then_inc(s_st[i], 16)
                        if t < NT and load is not None:
                            sp.dma_start(xin[:, i], load[t * P:(t + 1) * P, :]).then_inc(s_in[i], 16)
                        if t < NT and add is not None:
                            sp.dma_start(ain[:, i], add[t * P:(t + 1) * P, :]).then_inc(s_ad[i], 16)
                    load_slots(sp, took[0] + 2)
                    if store is not None or store_src is not None:
                        for i in range(2):
                            sp.wait_ge(s_st[i], 16 * NT // 2 + (16 if store is not None else 0))

                @block.vector
                def _(dve):
                    if store is not None:
                        for i in range(2):
                            dve.sem_inc(idle, 1)
                    per = 2 * (4 + (2 if gain is not None else 0) + (1 if rms is not None else 0)
                               + (1 if add is not None else 0) + (1 if keep or keep_sum else 0))
                    if gain is not None:
                        dve.wait_ge(s_row, 32)
                    with dve.Fori(0, NT // 2) as tt:
                        st = Steps(dve, s_own, tt, per)
                        for i in range(2):
                            t = tt * 2 + i
                            sm = small[0:P, 32 * i:32 * i + 32]
                            if load is not None:
                                dve.wait_ge(s_in[i], tt * 16 + 16)
                                x = xin[:, i]
                                x0, x1 = xin[:, i, 0:512], xin[:, i, 512:D]
                            else:
                                x = tok[:, ds(t, 1), :].rearrange("p o n -> p (o n)")
                                x0 = tok[:, ds(t, 1), 0:512].rearrange("p o n -> p (o n)")
                                x1 = tok[:, ds(t, 1), 512:D].rearrange("p o n -> p (o n)")
                            nc.vector.bn_stats(sm[:, 0:6], x0)
                            st.link(nc.vector.bn_stats(sm[:, 6:12], x1))
                            hold(dve)
                            st.link(nc.vector.bn_aggr(sm[:, 12:14], sm[:, 0:12]))
                            nc.vector.tensor_scalar(sm[:, 14:15], sm[:, 13:14], eps, None, ALU.add).then_inc(s_va, 1)
                            dve.wait_ge(s_sd, t + 1)
                            st.link(nc.vector.reciprocal(sm[:, 16:17], sm[:, 15:16]))
                            if turn:
                                dve.wait_ge(s_tr, t * 2 + 1)
                            if store is not None:
                                dve.wait_ge(s_st[i], tt * 16 + 16)
                            st.link(nc.vector.tensor_scalar(y[:, i], x, sm[:, 12:13], sm[:, 16:17],
                                                            ALU.subtract, ALU.mult))
                            if gain is not None:
                                st.link(nc.vector.tensor_tensor(y[:, i], y[:, i], rows[:, 0], ALU.mult))
                                st.link(nc.vector.tensor_tensor(y[:, i], y[:, i], rows[:, 1], ALU.add))
                            if add is not None:
                                dve.wait_ge(s_ad[i], tt * 16 + 16)
                                st.link(nc.vector.tensor_tensor(y[:, i], y[:, i], ain[:, i], ALU.add))
                            if rms is not None:
                                st.link(nc.vector.scalar_tensor_tensor(
                                    out=xin[:, i], in0=y[:, i], scalar=1.0, in1=y[:, i], op0=ALU.mult, op1=ALU.mult,
                                    accum_out=small[0:P, ds(t + rms, 1)]))
                            if keep:
                                hold(dve)
                                st.link(nc.vector.tensor_copy(tokC[:, ds(t, 1), :].rearrange("p o n -> p (o n)"),
                                                              y[:, i]))
                            elif keep_sum:
                                st.link(nc.vector.tensor_tensor(tokB[:, ds(t, 1), :].rearrange("p o n -> p (o n)"),
                                                                x, y[:, i], ALU.add))
                            nc.vector.sem_inc(s_y, 1)
                        st.end()

                @block.scalar
                def _(act):
                    if turn:
                        act.sem_inc(s_tr, 4)
                    if store is not None:
                        for i in range(2):
                            act.sem_inc(s_st[i], 16)
                    act.sem_inc(s_ev, 4)
                    with act.Fori(0, NT // 2) as tt:
                        for i in range(2):
                            t = tt * 2 + i
                            sm = small[0:P, 32 * i:32 * i + 32]
                            act.wait_ge(s_va, t + 1)
                            nc.scalar.sqrt(sm[:, 15:16], sm[:, 14:15]).then_inc(s_sd, 1)
                            if turn:
                                for h in range(2):
                                    act.wait_ge(s_tr, t * 2 + h + 5)
                                    nc.scalar.copy(
                                        featA[:, 4 * h:4 * h + 4, ds(t * P, P)],
                                        bank[2 * i + h][:, 0:4 * P].rearrange("p (k n) -> p k n", k=4)).then_inc(s_ev, 1)

                if turn:
                    @block.tensor
                    def _(pe):
                        with pe.Fori(0, NT // 2) as tt:
                            for i in range(2):
                                pe.wait_ge(s_y, tt * 2 + i + 1)
                                for k in range(KD):
                                    if k % 4 == 0:
                                        pe.wait_ge(s_ev, (tt * 2 + i) * 2 + k // 4 + 1)
                                    m = nc.tensor.transpose(bank[2 * i + k // 4][:, (k % 4) * P:(k % 4 + 1) * P],
                                                            y[:, i, k * 128:(k + 1) * 128], ident[0:P, 0:P])
                                    if k % 4 == 3:
                                        m.then_inc(s_tr, 1)

        def pe_tok(pe, s0, lhs, nk, s_mm, s_free, turns=NC // 2, cw=CW, rhs_more=None):
            with pe.Fori(0, turns) as tt:
                for i in range(2):
                    w_wait(pe, s0 + i, tt, 16 * len(slots[s0 + i]))
                    w = ring_k((s0 + i) % 2, nk, cw)
                    for t in range(NT):
                        u = i * NT + t
                        pe.wait_ge(s_free, tt * 2 * NT + u + 1)
                        for k in range(nk):
                            m = nc.tensor.matmul(bank[u % 4][0:P, 0:cw], lhs(k, t), w[:, k, :],
                                                 start=(k == 0), stop=(k == nk - 1))
                        m.then_inc(s_mm, 1)
                    pe.wait_ge(s_mm, tt * 2 * NT + (i + 1) * NT)
                    pe.sem_inc(w_used, 1)

        def phase_h0():
            s_mm, s_free, s_a, s_own = sem("h0_mm"), sem("h0_free"), sem("h0_a"), sem("h0_own")
            s0 = take(NC)
            al, ar = small[0:P, 128:128 + NT], small[0:P, 144:144 + NT]
            arow = stage3[0:P, 0:2 * D].rearrange("p (i n) -> p i n", i=2)
            junk = stage1[0:P, 0:D]
            with nc.Block() as block:
                @block.sync
                def _(sp):
                    sp.dma_start(arow, A["L0_gnn_a"].rearrange("o (i n) -> o i n", i=2)
                                 .to_broadcast([P, 2, D])).then_inc(s_a, 16)
                    load_slots(sp, s0 + NC + 2)

                @block.tensor
                def _(pe):
                    pe_tok(pe, s0, lambda k, t: featA[:, k, t * P:(t + 1) * P], KD, s_mm, s_free)

                @block.scalar
                def _(act):
                    act.sem_inc(s_free, 4)
                    with act.Fori(0, NC // 2) as tt:
                        for i in range(2):
                            for t in range(NT):
                                u = i * NT + t
                                act.wait_ge(s_mm, tt * 2 * NT + u + 1)
                                nc.scalar.copy(tokB[:, t, ds((tt * 2 + i) * CW, CW)],
                                               bank[u % 4][0:P, 0:CW]).then_inc(s_free, 1)

                @block.vector
                def _(dve):
                    st = Steps(dve, s_own)
                    dve.wait_ge(s_a, 16)
                    for t in range(NT):
                        dve.wait_ge(s_free, 4 + (NC - 1) * NT + t + 1)
                        for i, dst in ((0, al), (1, ar)):
                            st.link(nc.vector.tensor_tensor_reduce(junk, tokB[:, t, :], arow[:, i], 1.0, 0.0,
                                                                   ALU.mult, ALU.add, dst[:, t:t + 1]))

        def batches(eng, d):
            return [eng.value_load(table[0:1, i, ds(d, 1)], min_val=0, max_val=(NB - 1, NB, NB * NT)[i])
                    for i in range(3)]

        def batch(lo, r, past=0):
            return nc.s_assert_within(lo + r, 0, NB - 1 + past, skip_runtime_bounds_check_because="the table keeps "
                                      "first <= NB - 1 and first + count <= NB")

        def phase_edges0():
            s_dg, s_al, s_alb, s_z, s_ez, s_c, s_free, s_oh, s_used, s_own = (sem("e0_" + x) for x in (
                "diag", "al", "alb", "z", "expz", "count", "free", "onehot", "used", "own"))
            al, ar = small[0:P, 128:128 + NT], small[0:P, 144:144 + NT]
            ohs = stage1[0:P, :].bitcast(F16)[:, 0:HB * N].rearrange("p (q n) -> p q n", q=HB)
            ohd = stage2[0:P, :].bitcast(F16)[:, 0:SUB * P].rearrange("p (q n) -> p q n", q=SUB)
            z = stage2[0:P, SUB * P // 2:SUB * P // 2 + N]
            alb = stage3[0:P, 0:N]
            zero16 = gatT[0:P, 0, 0:P // 2 + 1].bitcast(F16)[:, 0:P]
            diag = gatT[0:P, 1, 0:N].rearrange("p (t n) -> p t n", t=NT)
            emat = bigC[0:P, 0:NT * N].rearrange("p (t n) -> p t n", t=NT)
            with nc.Block() as block:
                @block.vector
                def _(dve):
                    nc.vector.memset(zero16, 0.0)
                    nc.vector.tensor_tensor(diag, ident[0:P, 0:P].rearrange("p (o n) -> p o n", o=1)
                                            .to_broadcast([P, NT, P]),
                                            al.rearrange("p (t o) -> p t o", o=1).to_broadcast([P, NT, P]),
                                            ALU.mult).then_inc(s_dg, 1)
                    dve.wait_ge(s_alb, 3)
                    dve.sem_inc(s_free, 2)
                    with dve.Fori(0, NT) as d:
                        lo, cnt, base = batches(dve, d)
                        st = Steps(dve, s_own, d, 1)
                        dve.wait_ge(s_free, d + 2)
                        st.link(nc.vector.tensor_scalar(z, alb, ar[:, ds(d, 1)], None, ALU.add))
                        nc.vector.scalar_tensor_tensor(out=z, in0=z, scalar=0.1, in1=z, op0=ALU.mult,
                                                       op1=ALU.max).then_inc(s_z, 1)
                        st.end()
                        with dve.Fori(0, cnt) as r:
                            for q in range(SUB):
                                u = (base + r) * SUB + q
                                j = batch(lo, r) * SUB + q
                                dve.wait_ge(s_used, u + 1)
                                if q % HB == 0:
                                    nc.vector.tensor_tensor(
                                        ohd[:, q:q + HB, :],
                                        iota16[:, ds(d * P, P)].rearrange("p (o n) -> p o n", o=1).to_broadcast([P, HB, P]),
                                        dst_f[:, ds(j, HB)].rearrange("p (q o) -> p q o", o=1).to_broadcast([P, HB, P]),
                                        ALU.is_equal)
                                nc.vector.tensor_scalar(ohs[:, q % HB, :], iota16[:], src_f[:, ds(j, 1)], None,
                                                        ALU.is_equal).then_inc(s_oh, 1)
                        dve.wait_ge(s_ez, d + 1)
                        dve.wait_ge(s_c, d + 1)
                        for ch, (a, w) in enumerate(FCH):
                            m = nc.vector.tensor_tensor(emat[:, ds(d, 1), a:a + w].rearrange("p o n -> p (o n)"),
                                                        bank[ch][0:P, 0:w], z[:, a:a + w], ALU.mult)
                        m.then_inc(s_free, 1)

                @block.scalar
                def _(act):
                    act.wait_ge(s_al, 1)
                    for ch, (a, w) in enumerate(FCH):
                        nc.scalar.copy(alb[:, a:a + w], bank[5 + ch][0:P, 0:w]).then_inc(s_alb, 1)
                    with act.Fori(0, NT) as d:
                        act.wait_ge(s_z, d + 1)
                        nc.scalar.activation(z, z, ACT.Exp, scale=-1.0).then_inc(s_ez, 1)

                @block.tensor
                def _(pe):
                    pe.wait_ge(s_dg, 1)
                    for t in range(NT):
                        m = nc.tensor.matmul(bank[5 + t // 4][0:P, (t % 4) * P:(t % 4 + 1) * P], ones[0:P, 0:P],
                                             diag[:, t, :], start=True, stop=True)
                    m.then_inc(s_al, 1)
                    pe.sem_inc(s_used, HB)
                    with pe.Fori(0, NT) as d:
                        lo, cnt, base = batches(pe, d)
                        pe.wait_ge(s_free, d + 2)
                        for ch, (a, w) in enumerate(FCH):
                            nc.tensor.matmul(bank[ch][0:P, 0:w], zero16, iota16[:, a:a + w], start=True, stop=False,
                                             skip_group_check=True)
                        with pe.Fori(0, cnt) as r:
                            for q in range(SUB):
                                pe.wait_ge(s_oh, (base + r) * SUB + q + 1)
                                for ch, (a, w) in enumerate(FCH):
                                    m = nc.tensor.matmul(bank[ch][0:P, 0:w], ohd[:, q, :], ohs[:, q % HB, a:a + w],
                                                         start=False, stop=False, skip_group_check=True)
                                m.then_inc(s_used, 1)
                        for ch, (a, w) in enumerate(FCH):
                            m = nc.tensor.matmul(bank[ch][0:P, 0:w], zero16, iota16[:, a:a + w], start=False,
                                                 stop=True, skip_group_check=True)
                        m.then_inc(s_c, 1)

        def phase_agg0():
            s_rs, s_rr, s_mm, s_free, s_m, s_e, s_own, s_ch = (sem("a0_" + x) for x in (
                "rowsum", "recip", "mm", "free", "min", "exp", "own", "chunk"))
            s_x = [sem(f"a0_x{i}") for i in range(2)]
            s_st = [sem(f"a0_stored{i}") for i in range(2)]
            emat = bigC[0:P, 0:NT * N].rearrange("p (t n) -> p t n", t=NT)
            rs = small[0:P, 160:160 + NT]
            xch = [s_[0:P, :].rearrange("p (t n) -> p t n", t=NT) for s_ in (stage1, stage2)]
            low = stage3[0:P, :]
            hp = stage4[0:P, :]
            xv, rv = ptile(A["x"]), ptile(XR)
            with nc.Block() as block:
                @block.sync
                def _(sp):
                    for c in range(NC + 2):
                        if c >= 2:
                            sp.wait_ge(s_ch, c)
                            sp.dma_start(rv[:, :, (c - 2) * CW:(c - 1) * CW], xch[c % 2]).then_inc(s_st[c % 2], 16)
                            sp.wait_ge(s_st[c % 2], 16 * (c // 2))
                        if c < NC:
                            sp.dma_start(xch[c % 2], xv[:, :, c * CW:(c + 1) * CW]).then_inc(s_x[c % 2], 16)

                @block.tensor
                def _(pe):
                    for t in range(NT):
                        for d in range(NT):
                            m = nc.tensor.matmul(bank[7][0:P, t:t + 1], emat[:, d, t * P:(t + 1) * P], ones[0:P, 0:1],
                                                 start=(d == 0), stop=(d == NT - 1))
                    m.then_inc(s_rs, 1)
                    with pe.Fori(0, NC // 2) as cc:
                        for u in range(2 * NT):
                            t = u % NT
                            pe.wait_ge(s_free, cc * 2 * NT + u + 1)
                            for d in range(NT):
                                m = nc.tensor.matmul(bank[u % 4][0:P, 0:CW], emat[:, d, t * P:(t + 1) * P],
                                                     tokB[:, d, ds((cc * 2 + u // NT) * CW, CW)],
                                                     start=(d == 0), stop=(d == NT - 1))
                            m.then_inc(s_mm, 1)

                @block.vector
                def _(dve):
                    st = Steps(dve, s_own)
                    dve.wait_ge(s_rs, 1)
                    st.link(nc.vector.tensor_scalar(rs, bank[7][0:P, 0:NT], 1e-5, None, ALU.add))
                    st.link(nc.vector.reciprocal(rs, rs))
                    nc.vector.sem_inc(s_rr, 1)
                    with dve.Fori(0, NC // 2) as cc:
                        st = Steps(dve, s_own, cc, 4, base=2)
                        for c in range(2):
                            dve.wait_ge(s_free, (cc * 2 + c) * NT + NT + 4)
                            nc.vector.tensor_scalar(low, hp, 0.0, None, ALU.min).then_inc(s_m, 1)
                            dve.wait_ge(s_e, cc * 2 + c + 1)
                            st.link(nc.vector.scalar_tensor_tensor(out=hp, in0=low, scalar=-1.0, in1=hp,
                                                                   op0=ALU.add, op1=ALU.max))
                            dve.wait_ge(s_x[c], cc * 16 + 16)
                            xc = xch[c].rearrange("p t n -> p (t n)")
                            st.link(nc.vector.tensor_tensor(xc, xc, hp, ALU.add))
                            nc.vector.sem_inc(s_ch, 1)
                        st.end()

                @block.scalar
                def _(act):
                    act.wait_ge(s_rr, 1)
                    act.sem_inc(s_free, 4)
                    act.sem_inc(s_ch, 1)
                    with act.Fori(0, NC // 2) as cc:
                        for c in range(2):
                            act.wait_ge(s_ch, cc * 2 + c + 1)
                            for t in range(NT):
                                u = c * NT + t
                                act.wait_ge(s_mm, cc * 2 * NT + u + 1)
                                nc.scalar.activation(hp[:, t * CW:(t + 1) * CW], bank[u % 4][0:P, 0:CW], ACT.Copy,
                                                     scale=rs[:, t:t + 1]).then_inc(s_free, 1)
                            act.wait_ge(s_m, cc * 2 + c + 1)
                            nc.scalar.activation(low, low, ACT.Exp).then_inc(s_e, 1)

        def phase_mix(name, normed):
            (s_row, s_q, s_qe, s_mq, s_eq, s_q2, s_n, s_ne, s_t, s_te, s_mk, s_ek, s_k2, s_kn, s_kr, s_kv, s_kve,
             s_cx, s_ce, s_own) = (sem(f"{name}_" + x) for x in (
                 "rows", "q", "qevac", "qmin", "qexp", "qsq", "norm", "normevac", "tok", "tokevac", "kmin", "kexp",
                 "ksq", "knorm", "kvin", "kv", "kvevac", "ctx", "ctxevac", "own"))
            s0 = take(3 * NC)
            qt = bigC[:, 0:2 * N].rearrange("p (m n) -> p m n", m=2)
            qv = bigC[:, 2 * N:4 * N].rearrange("p (m n) -> p m n", m=2)
            qt_all, qv_all = bigC[:, 0:2 * N], bigC[:, 2 * N:4 * N]
            tk = bigC[0:P, 4 * N:4 * N + NT * CW]
            kc, vc = stage1[0:P, :], stage2[0:P, :]
            kv = stage3[:, 0:512].rearrange("p (j n) -> p j n", j=4)
            n2, kn, rk = (small[0:P, 0 + 64 * i:40 + 64 * i] for i in range(3))
            rows = stage4[0:P, 0:2 * D].rearrange("p (i n) -> p i n", i=2)
            units = [(m, ch, a, w) for m in range(2) for ch, (a, w) in enumerate(FCH)]
            NU = len(units)

            U4 = HB * HID
            slot4 = [bigC[0:P, 7680:7680 + 2 * U4], bigC[0:P, 7680 + 2 * U4:7680 + 4 * U4], stage4[0:P, 0:2 * U4],
                     stage3[0:P, 512:512 + 2 * U4]]
            slot4 = [x.rearrange("p (s g n) -> p s g n", s=2, g=HB) for x in slot4]
            NQ = NB * SUB // HB
            if not normed:
                s_gx = [sem(f"{name}_gather{i}") for i in range(4)]
                s_used, s_idx, s_so, s_at = (sem(f"{name}_" + x) for x in ("slotused", "idx", "score", "att"))

            def score_unit(dve, st2, q_at, k):
                xl, xr = slot4[k % 4][:, 0], slot4[k % 4][:, 1]
                flat = xl.rearrange("p g n -> p (g n)")
                dve.wait_ge(s_gx[k % 4], st2.turn * (NQ // 8 * 128) + (k // 4 + 1) * 128)
                st2.link(nc.vector.tensor_tensor(xl, xl, xr, ALU.add))
                st2.link(nc.vector.scalar_tensor_tensor(out=flat, in0=flat, scalar=0.2, in1=flat, op0=ALU.mult,
                                                        op1=ALU.max))
                st2.link(nc.vector.tensor_tensor(xl, xl, attrow[:, :].rearrange("p (o n) -> p o n", o=1)
                                                 .to_broadcast([P, HB, HID]), ALU.mult))
                nc.vector.tensor_reduce(scores[:, ds((q_at + k) * HB * GH, HB * GH)],
                                        flat.rearrange("p (h n) -> p h n", n=GD), AX.X, ALU.add).then_inc(s_used, 1)

            with nc.Block() as block:
                if not normed:
                    @block.gpsimd
                    def _(pool):
                        idx = edge_ix[:, :, :, :]
                        pool.sem_inc(s_used, 4)
                        with pool.Fori(0, NQ // 4) as qq:
                            for k in range(4):
                                q = qq * 4 + k
                                pool.wait_ge(s_used, q + 1)
                                hold(pool)
                                nc.gpsimd.tensor_copy(idx[:, k], edge_i[:, :, ds(q * HB, HB)]).then_inc(s_idx, 1)
                                pool.wait_ge(s_idx, q + 1)
                                hold(pool)
                                for side, rows_of in ((0, XL), (1, XRD)):
                                    for g in range(HB):
                                        nc.gpsimd.indirect_dma_start(
                                            out=slot4[k][:, side, g, :], out_offset=None, in_=rows_of,
                                            in_offset=bass.IndirectOffsetOnAxis(
                                                ap=idx[:, k, side, g:g + 1].bitcast(U32), axis=0)
                                        ).then_inc(s_gx[k], 16)

                @block.sync
                def _(sp):
                    if normed:
                        sp.dma_start(rows[:, 0], row_bc(A["L0_mix_bk"], D)).then_inc(s_row, 16)
                        sp.dma_start(rows[:, 1], row_bc(A["L0_mix_bv"], D)).then_inc(s_row, 16)
                    load_slots(sp, s0 + 3 * NC + 2)

                @block.tensor
                def _(pe):
                    pe.sem_inc(s_ce, 1)
                    with pe.Fori(0, NC // 2) as cc:
                        for i in range(2):
                            c = cc * 2 + i

                            def slot(j):
                                s = s0 + 3 * i + j
                                w_wait(pe, s, cc, 48)
                                return ring_k(s % 2, KD, CW)

                            w = slot(0)
                            for j, (m, ch, a, wd) in enumerate(units):
                                if j < 3:
                                    pe.wait_ge(s_ce, c * NU + 1)
                                else:
                                    pe.wait_ge(s_qe, c * NU + j - 2)
                                for k in range(KD):
                                    x = nc.tensor.matmul(bank[4 + ch][:, 0:wd], w[:, k, m * 128:(m + 1) * 128],
                                                         featA[:, k, a:a + wd], start=(k == 0), stop=(k == KD - 1))
                                x.then_inc(s_q, 1)
                            pe.wait_ge(s_q, c * NU + NU)
                            pe.sem_inc(w_used, 1)

                            def tok(j):
                                w = slot(1 + j)
                                for t in range(NT):
                                    u = j * NT + t
                                    pe.wait_ge(s_te, c * 2 * NT + u + 1)
                                    for k in range(KD):
                                        x = nc.tensor.matmul(bank[u % 4][0:P, 0:CW], featA[:, k, t * P:(t + 1) * P],
                                                             w[:, k, :], start=(k == 0), stop=(k == KD - 1))
                                    x.then_inc(s_t, 1)
                                pe.wait_ge(s_t, c * 2 * NT + (j + 1) * NT)
                                pe.sem_inc(w_used, 1)

                            def scales(lhs):
                                for j, (m, ch, a, wd) in enumerate(units):
                                    if j < 3:
                                        pe.wait_ge(s_qe, c * NU + 4 + j)
                                    else:
                                        pe.wait_ge(s_ne, c * NU + j - 2)
                                    rhs = qv if normed else qt
                                    nc.tensor.matmul(bank[4 + ch][:, 0:wd], lhs(m), rhs[:, m, a:a + wd], start=True,
                                                     stop=True).then_inc(s_n, 1)

                            tok(0)
                            if normed:
                                pe.wait_ge(s_q2, c + 1)
                                scales(lambda m: blocks[:, :])
                            tok(1)
                            pe.wait_ge(s_kr, c + 1)
                            for m in range(2):
                                for what in range(1 if normed else 2):
                                    for t in range(NT):
                                        col = t * CW + m * 128
                                        x = nc.tensor.matmul(
                                            bank[7][:, (2 * m + what) * 128:(2 * m + what + 1) * 128],
                                            kc[:, col:col + 128], ones[0:P, :] if what else vc[:, col:col + 128],
                                            start=(t == 0), stop=(t == NT - 1))
                            x.then_inc(s_kv, 1)
                            pe.wait_ge(s_kve, c + 1)
                            if not normed:
                                scales(lambda m: kv[:, 2 * m + 1, :])
                            for j, (m, ch, a, wd) in enumerate(units):
                                if j < 3:
                                    pe.wait_ge(s_ne, c * NU + 4 + j)
                                else:
                                    pe.wait_ge(s_ce, c * NU + j - 1)
                                nc.tensor.matmul(bank[4 + ch][:, 0:wd], kv[:, 2 * m, :], qt[:, m, a:a + wd],
                                                 start=True, stop=True).then_inc(s_cx, 1)

                @block.scalar
                def _(act):
                    act.sem_inc(s_te, 4)
                    with act.Fori(0, NC // 2) as cc:
                        for i in range(2):
                            c = cc * 2 + i
                            for j, (m, ch, a, wd) in enumerate(units):
                                act.wait_ge(s_q, c * NU + j + 1)
                                if normed:
                                    hold(act)
                                    nc.scalar.activation(qt[:, m, a:a + wd], bank[4 + ch][:, 0:wd], ACT.Identity,
                                                         bias=bcol[:, ds(c * 2 + m, 1)]).then_inc(s_qe, 1)
                                else:
                                    nc.scalar.copy(qt[:, m, a:a + wd], bank[4 + ch][:, 0:wd]).then_inc(s_qe, 1)
                            act.wait_ge(s_mq, c + 1)
                            nc.scalar.activation(qv_all, qv_all, ACT.Exp).then_inc(s_eq, 1)

                            def evac(j, dst):
                                for t in range(NT):
                                    u = j * NT + t
                                    act.wait_ge(s_t, c * 2 * NT + u + 1)
                                    nc.scalar.copy(dst[:, t * CW:(t + 1) * CW], bank[u % 4][0:P, 0:CW]).then_inc(s_te, 1)

                            evac(0, kc)
                            act.wait_ge(s_mk, c + 1)
                            nc.scalar.activation(tk, tk, ACT.Exp).then_inc(s_ek, 1)
                            if normed:
                                for j, (m, ch, a, wd) in enumerate(units):
                                    act.wait_ge(s_n, c * NU + j + 1)
                                    nc.scalar.sqrt(qv[:, m, a:a + wd], bank[4 + ch][:, 0:wd]).then_inc(s_ne, 1)
                            evac(1, vc)
                            if normed:
                                act.wait_ge(s_k2, c + 1)
                                nc.scalar.sqrt(kn, n2).then_inc(s_kn, 1)

                @block.vector
                def _(dve):
                    if normed:
                        dve.wait_ge(s_row, 32)
                    with dve.Fori(0, NC // 2) as cc:
                        st = Steps(dve, s_own, cc, 16 if normed else 6)
                        if not normed:
                            st2 = Steps(dve, s_so, cc, NQ // 2 * 3)
                            done = [0]

                        def fill(k):
                            if not normed:
                                for _ in range(k):
                                    score_unit(dve, st2, cc * (NQ // 2), done[0])
                                    done[0] += 1

                        for i in range(2):
                            c = cc * 2 + i

                            def row(j):
                                return rows[:, j, ds(c * CW, CW)].rearrange("p (o n) -> p o n", o=1).to_broadcast([P, NT, CW])

                            def by_tile(v):
                                return v.rearrange("p (t n) -> p t n", t=NT)

                            dve.wait_ge(s_ce, c * NU + 1)
                            fill(3)
                            dve.wait_ge(s_qe, c * NU + NU)
                            nc.vector.tensor_scalar(qv_all, qt_all, 0.0, None, ALU.min).then_inc(s_mq, 1)
                            dve.wait_ge(s_eq, c + 1)
                            if normed:
                                st.link(nc.vector.scalar_tensor_tensor(out=qt_all, in0=qv_all, scalar=-1.0, in1=qt_all,
                                                                       op0=ALU.add, op1=ALU.max))
                                nc.vector.tensor_tensor(qv_all, qt_all, qt_all, ALU.mult).then_inc(s_q2, 1)
                            else:
                                st.link(nc.vector.scalar_tensor_tensor(out=qt_all, in0=qt_all, scalar=1.0, in1=qv_all,
                                                                       op0=ALU.add, op1=ALU.max))
                            fill(4)
                            dve.wait_ge(s_te, c * 2 * NT + NT + 4)
                            if normed:
                                st.link(nc.vector.tensor_tensor(by_tile(kc), by_tile(kc), row(0), ALU.add))
                            nc.vector.tensor_scalar(tk, kc, 0.0, None, ALU.min).then_inc(s_mk, 1)
                            dve.wait_ge(s_ek, c + 1)
                            if normed:
                                st.link(nc.vector.scalar_tensor_tensor(out=kc, in0=tk, scalar=-1.0, in1=kc,
                                                                       op0=ALU.add, op1=ALU.max))
                                st.link(nc.vector.tensor_tensor(tk, kc, kc, ALU.mult))
                                nc.vector.tensor_reduce(n2, tk.rearrange("p (h n) -> p h n", n=64), AX.X,
                                                        ALU.add).then_inc(s_k2, 1)
                                dve.wait_ge(s_ne, c * NU + NU)
                                st.link(nc.vector.reciprocal(qv_all, qv_all))
                                dve.wait_ge(s_kn, c + 1)
                                st.link(nc.vector.reciprocal(rk, kn))
                                kh = kc.rearrange("p (h n) -> p h n", n=64)
                                st.link(nc.vector.tensor_tensor(kh, kh, rk.rearrange("p (h o) -> p h o", o=1)
                                                                .to_broadcast([P, 4 * NT, 64]), ALU.mult))
                                st.link(nc.vector.tensor_tensor(by_tile(vc), by_tile(vc), row(1), ALU.add))
                            else:
                                st.link(nc.vector.scalar_tensor_tensor(out=kc, in0=kc, scalar=1.0, in1=tk,
                                                                       op0=ALU.add, op1=ALU.max))
                                fill(4)
                                dve.wait_ge(s_te, c * 2 * NT + 2 * NT + 4)
                            nc.vector.sem_inc(s_kr, 1)
                            fill(1)
                            dve.wait_ge(s_kv, c + 1)
                            b7 = bank[7][:, :].rearrange("p (j n) -> p j n", j=4)
                            mask = blocks[:, :].rearrange("p (o n) -> p o n", o=1)
                            if normed:
                                nc.vector.scalar_tensor_tensor(out=kv[:, 0:4:2, :], in0=b7[:, 0:4:2, :], scalar=0.125,
                                                               in1=mask.to_broadcast([128, 2, 128]), op0=ALU.mult,
                                                               op1=ALU.mult).then_inc(s_kve, 1)
                            else:
                                nc.vector.tensor_tensor(kv, b7, mask.to_broadcast([128, 4, 128]),
                                                        ALU.mult).then_inc(s_kve, 1)
                                for j, (m, ch, a, wd) in enumerate(units):
                                    dve.wait_ge(s_n, c * NU + j + 1)
                                    nc.vector.tensor_scalar(qv[:, m, a:a + wd], bank[4 + ch][:, 0:wd], 1e-6, None,
                                                            ALU.add).then_inc(s_ne, 1)
                                dve.wait_ge(s_ne, c * NU + NU)
                                st.link(nc.vector.reciprocal(qv_all, qv_all))
                            for j, (m, ch, a, wd) in enumerate(units):
                                dve.wait_ge(s_cx, c * NU + j + 1)
                                dst = featB[:, ds(c * 2 + m, 1), a:a + wd].rearrange("p o n -> p (o n)")
                                nc.vector.tensor_tensor(dst, bank[4 + ch][:, 0:wd], qv[:, m, a:a + wd],
                                                        ALU.mult).then_inc(s_ce, 1)
                            fill(8)
                        st.end()
                        if not normed:
                            assert done[0] == NQ // 2
                            st2.end()

        def phase_out(name, lhs, nk, bias, residual):
            s_mm, s_free, s_b, s_own, s_ch = (sem(f"{name}_" + x) for x in ("mm", "free", "bias", "own", "chunk"))
            s_r = [sem(f"{name}_res{i}") for i in range(2)]
            s0 = take(NC)
            res = [x[0:P, :].rearrange("p (t n) -> p t n", t=NT) for x in (stage1, stage2)]
            brow = stage3[0:P, 0:D]
            rv = ptile(residual)
            with nc.Block() as block:
                @block.sync
                def _(sp):
                    sp.dma_start(brow, row_bc(bias, D)).then_inc(s_b, 16)
                    for c in range(NC):
                        if c >= 2:
                            sp.wait_ge(s_ch, c - 1)
                        sp.dma_start(res[c % 2], rv[:, :, c * CW:(c + 1) * CW]).then_inc(s_r[c % 2], 16)
                    load_slots(sp, s0 + NC + 2)

                @block.tensor
                def _(pe):
                    pe_tok(pe, s0, lhs, nk, s_mm, s_free)

                @block.scalar
                def _(act):
                    act.sem_inc(s_free, 4)
                    with act.Fori(0, NC // 2) as tt:
                        for i in range(2):
                            for t in range(NT):
                                u = i * NT + t
                                act.wait_ge(s_mm, tt * 2 * NT + u + 1)
                                nc.scalar.copy(tokC[:, t, ds((tt * 2 + i) * CW, CW)],
                                               bank[u % 4][0:P, 0:CW]).then_inc(s_free, 1)

                @block.vector
                def _(dve):
                    dve.wait_ge(s_b, 16)
                    for c in range(NC):
                        chunk = tokC[:, :, c * CW:(c + 1) * CW]
                        dve.wait_ge(s_r[c % 2], 16 * (c // 2) + 16)
                        dve.wait_ge(s_free, 4 + (c + 1) * NT)
                        nc.vector.tensor_tensor(chunk, chunk, res[c % 2], ALU.add).then_inc(s_ch, 1)
                        dve.wait_ge(s_ch, c + 1)
                        nc.vector.tensor_tensor(chunk, chunk, brow[:, c * CW:(c + 1) * CW]
                                                .rearrange("p (o n) -> p o n", o=1).to_broadcast([P, NT, CW]), ALU.add)

        def phase_up(name, weights, bias_at):
            s_mm, s_ev = sem(f"{name}_mm"), sem(f"{name}_gelu")
            s0 = take(2) if weights is None else 0
            with nc.Block() as block:
                if weights is None:
                    @block.sync
                    def _(sp):
                        load_slots(sp, s0 + 4)

                @block.tensor
                def _(pe):
                    for m in range(4):
                        if weights is None:
                            w_wait(pe, s0 + m // 2)
                            w = ring_k((s0 + m // 2) % 2, KD, CW)[:, :, (m % 2) * 128:(m % 2 + 1) * 128]
                        else:
                            w = weights(m)
                        for ch, (a, wd) in enumerate(FCH):
                            if m:
                                pe.wait_ge(s_ev, 3 * m + ch - 2)
                            for k in range(KD):
                                x = nc.tensor.matmul(bank[4 + ch][:, 0:wd], w[:, k, :], featA[:, k, a:a + wd],
                                                     start=(k == 0), stop=(k == KD - 1))
                            x.then_inc(s_mm, 1)
                        if weights is None and m % 2:
                            pe.wait_ge(s_mm, 3 * m + 3)
                            pe.sem_inc(w_used, 1)

                @block.scalar
                def _(act):
                    for m in range(4):
                        for ch, (a, wd) in enumerate(FCH):
                            act.wait_ge(s_mm, 3 * m + ch + 1)
                            nc.scalar.activation(featB[:, m, a:a + wd], bank[4 + ch][:, 0:wd], ACT.Gelu,
                                                 bias=bcol[:, bias_at + m:bias_at + m + 1]).then_inc(s_ev, 1)

        def phase_down(name, weights, bias, dram=None):
            s_mm, s_free, s_b, s_ch, s_st = (sem(f"{name}_" + x) for x in ("mm", "free", "bias", "chunk", "stored"))
            s0 = take(2) if weights is None else 0
            brow = stage3[0:P, 0:D]
            with nc.Block() as block:
                @block.sync
                def _(sp):
                    sp.dma_start(brow, row_bc(bias, D)).then_inc(s_b, 16)
                    if weights is None:
                        load_slots(sp, s0 + 4)
                    if dram is not None:
                        for c in range(2):
                            sp.wait_ge(s_ch, c + 1)
                            sp.dma_start(ptile(dram)[:, :, c * 512:(c + 1) * 512],
                                         tokC[:, :, c * 512:(c + 1) * 512]).then_inc(s_st, 16)
                        sp.wait_ge(s_st, 32)

                @block.tensor
                def _(pe):
                    for c in range(2):
                        if weights is None:
                            w_wait(pe, s0 + c)
                            w = ring_k((s0 + c) % 2, 4, 512)
                        else:
                            w = weights(c)
                        for t in range(NT):
                            u = c * NT + t
                            if u >= 4:
                                pe.wait_ge(s_free, u - 3)
                            for k in range(4):
                                m = nc.tensor.matmul(bank[u % 4][0:P, :], featB[:, k, t * P:(t + 1) * P], w[:, k, :],
                                                     start=(k == 0), stop=(k == 3))
                            m.then_inc(s_mm, 1)
                        if weights is None:
                            pe.wait_ge(s_mm, c * NT + NT)
                            pe.sem_inc(w_used, 1)

                @block.vector
                def _(dve):
                    dve.wait_ge(s_b, 16)
                    for c in range(2):
                        for t in range(NT):
                            u = c * NT + t
                            part = tokC[:, t, c * 512:(c + 1) * 512]
                            dve.wait_ge(s_mm, u + 1)
                            nc.vector.tensor_tensor(part, bank[u % 4][0:P, :], part, ALU.add).then_inc(s_free, 1)
                        dve.wait_ge(s_free, c * NT + NT)
                        part = tokC[:, :, c * 512:(c + 1) * 512]
                        nc.vector.tensor_tensor(part, part, brow[:, c * 512:(c + 1) * 512]
                                                .rearrange("p (o n) -> p o n", o=1).to_broadcast([P, NT, 512]),
                                                ALU.add).then_inc(s_ch, 1)

        def phase_route():
            s_ld, s_lg, s_own, s_e, s_ex, s_ct, s_cs, s_bm, s_be, s_r = (sem("rt_" + x) for x in (
                "in", "logits", "own", "comb", "exp", "turned", "turnedevac", "b2", "b2evac", "rows"))
            wr = stage1[:, 0:KD * NEXP].rearrange("p (k n) -> p k n", k=KD)
            b2 = stage2[0:NEXP, 0:D]
            br = stage3[0:P, 0:NEXP]
            combT = stage4[0:NEXP, 0:N]
            work = stage3[0:P, 256:256 + 8 * NT * NEXP].rearrange("p (a t n) -> p a t n", a=8, t=NT)
            lg, ex, eq = work[:, 0], work[:, 1], work[:, 2]
            mx, sm, ws = (small[0:P, 64 + 16 * i:64 + 16 * i + NT] for i in range(3))
            top = work[:, 3, :, 0:8]
            top_at = work[:, 4, :, 0:8].bitcast(U32)
            atf = work[:, 5, :, 0:8]
            col = lambda v, n: v.rearrange("p (t o) -> p t o", o=1).to_broadcast([P, NT, n])
            with nc.Block() as block:
                @block.sync
                def _(sp):
                    sp.dma_start(wr, A["L0_ffn_Wr"].rearrange("(k p) n -> p k n", p=128)).then_inc(s_ld, 16)
                    sp.dma_start(b2, A["L0_ffn_b2"]).then_inc(s_r, 16)
                    sp.dma_start(br, row_bc(A["L0_ffn_br"], NEXP)).then_inc(s_r, 16)

                @block.tensor
                def _(pe):
                    pe.wait_ge(s_ld, 16)
                    for t in range(NT):
                        for k in range(KD):
                            m = nc.tensor.matmul(bank[0][0:P, t * NEXP:(t + 1) * NEXP], featA[:, k, t * P:(t + 1) * P],
                                                 wr[:, k, :], start=(k == 0), stop=(k == KD - 1))
                    m.then_inc(s_lg, 1)
                    pe.wait_ge(s_e, 1)
                    for t in range(NT):
                        m = nc.tensor.transpose(bank[4 + t // 4][0:NEXP, (t % 4) * P:(t % 4 + 1) * P], comb[:, t, :],
                                                ident[0:P, 0:P])
                    m.then_inc(s_ct, 1)
                    pe.wait_ge(s_cs, 3)
                    pe.wait_ge(s_r, 32)
                    for u in range(2 * NT):
                        if u >= 4:
                            pe.wait_ge(s_be, u - 3)
                        nc.tensor.matmul(bank[u % 4][0:P, :], combT[:, (u // 2) * P:(u // 2 + 1) * P],
                                         b2[:, (u % 2) * 512:(u % 2 + 1) * 512], start=True,
                                         stop=True).then_inc(s_bm, 1)

                @block.scalar
                def _(act):
                    act.wait_ge(s_ex, 1)
                    nc.scalar.activation(ex, lg, ACT.Exp).then_inc(s_ex, 1)
                    act.wait_ge(s_ct, 1)
                    for ch, (a, w) in enumerate(FCH):
                        nc.scalar.copy(combT[:, a:a + w], bank[4 + ch][0:NEXP, 0:w]).then_inc(s_cs, 1)

                @block.vector
                def _(dve):
                    st = Steps(dve, s_own)
                    dve.wait_ge(s_r, 32)
                    dve.wait_ge(s_lg, 1)
                    st.link(nc.vector.tensor_tensor(lg, bank[0][0:P, 0:NT * NEXP].rearrange("p (t n) -> p t n", t=NT),
                                                    br.rearrange("p (o n) -> p o n", o=1).to_broadcast([P, NT, NEXP]),
                                                    ALU.add))
                    st.link(nc.vector.tensor_reduce(mx, lg, AX.X, ALU.max))
                    nc.vector.tensor_tensor(lg, lg, col(mx, NEXP), ALU.subtract).then_inc(s_ex, 1)
                    dve.wait_ge(s_ex, 2)
                    st.link(nc.vector.tensor_reduce(sm, ex, AX.X, ALU.add))
                    st.link(nc.vector.reciprocal(sm, sm))
                    st.link(nc.vector.tensor_tensor(ex, ex, col(sm, NEXP), ALU.mult))
                    for t in range(NT):
                        last = nc.vector.max(top[:, t, :], ex[:, t, :])
                    st.link(last)
                    for t in range(NT):
                        last = nc.vector.max_index(top_at[:, t, :], top[:, t, :], ex[:, t, :])
                    st.link(last)
                    st.link(nc.vector.tensor_copy(atf, top_at))
                    st.link(nc.vector.tensor_reduce(ws, top[:, :, 0:2], AX.X, ALU.add))
                    st.link(nc.vector.tensor_scalar(ws, ws, 1e-9, None, ALU.max))
                    st.link(nc.vector.reciprocal(ws, ws))
                    st.link(nc.vector.tensor_tensor(top[:, :, 0:2], top[:, :, 0:2], col(ws, 2), ALU.mult))
                    iota = iota16[:, 0:NEXP].rearrange("p (o n) -> p o n", o=1).to_broadcast([P, NT, NEXP])
                    for i in range(2):
                        st.link(nc.vector.tensor_tensor(eq, iota, atf[:, :, i:i + 1].to_broadcast([P, NT, NEXP]),
                                                        ALU.is_equal))
                        st.link(nc.vector.tensor_tensor(eq if i else comb, eq,
                                                        top[:, :, i:i + 1].to_broadcast([P, NT, NEXP]), ALU.mult))
                    nc.vector.tensor_tensor(comb, comb, eq, ALU.add).then_inc(s_e, 1)
                    for u in range(2 * NT):
                        dve.wait_ge(s_bm, u + 1)
                        part = tokB[:, u // 2, (u % 2) * 512:(u % 2 + 1) * 512]
                        nc.vector.tensor_tensor(part, bank[u % 4][0:P, :], part, ALU.add).then_inc(s_be, 1)

        def three_products(out_, pairs):
            todo = [(a, b) for (ah, al), (bh, bl) in pairs for a, b in ((ah, bh), (ah, bl), (al, bh))]
            for i, (a, b) in enumerate(todo):
                m = nc.tensor.matmul(out_, a, b, start=(i == 0), stop=(i == len(todo) - 1))
            return m

        def phase_moe():
            s_f, s_ge, s_tm, s_ae, s_xh, s_xl, s_wh, s_wl, s_hh, s_hl = (sem("moe_" + x) for x in (
                "up", "gelu", "down", "added", "xhi", "xlo", "whi", "wlo", "hhi", "hlo"))
            s0 = take(2 * NEXP)
            x_hi = bigC_r[:, 0:KD * N].rearrange("p (k n) -> p k n", k=KD)
            ht = stage1[:, 0:2 * N].rearrange("p (m n) -> p m n", m=2)
            ht_lo, ht_hi = (stage_r[i][:, 0:2 * N].rearrange("p (m n) -> p m n", m=2) for i in range(2))
            w_hi = [stage_r[2][:, 0:KD * EH].rearrange("p (k n) -> p k n", k=KD),
                    stage_r[3][:, 0:2 * D].rearrange("p (k n) -> p k n", k=2)]
            w_at, w_lo = ([ring_k(s0 % 2, KD, EH, x), ring_k((s0 + 1) % 2, 2, D, x)] for x in (ring, ring_r))
            units = [(m, ch, a, w) for m in range(2) for ch, (a, w) in enumerate(RCH)]
            as32 = lambda v: v.bitcast(F32)
            with nc.Block() as block:
                @block.sync
                def _(sp):
                    load_slots(sp, s0 + 2 * NEXP + 2)

                @block.tensor
                def _(pe):
                    pe.wait_ge(s_xl, 2)
                    with pe.Fori(0, NEXP) as e:
                        pe.wait_ge(s_wl, e * 2 + 1)
                        for j, (m, ch, a, wd) in enumerate(units):
                            pe.wait_ge(s_ge, e * 6 + j + 1)
                            three_products(bank[4 + ch][:, 0:wd], [
                                ((w_hi[0][:, k, m * 128:(m + 1) * 128], w_lo[0][:, k, m * 128:(m + 1) * 128]),
                                 (x_hi[:, k, a:a + wd], featA_r[:, k, a:a + wd])) for k in range(KD)]).then_inc(s_f, 1)
                        pe.wait_ge(s_f, e * 6 + 6)
                        pe.sem_inc(w_used, 1)
                        pe.wait_ge(s_wl, e * 2 + 2)
                        pe.wait_ge(s_hl, e * 6 + 6)
                        for t in range(NT):
                            for n in range(2):
                                u = t * 2 + n
                                pe.wait_ge(s_ae, e * 2 * NT + u + 1)
                                three_products(bank[u % 4][0:P, :], [
                                    ((ht_hi[:, k, t * P:(t + 1) * P], ht_lo[:, k, t * P:(t + 1) * P]),
                                     (w_hi[1][:, k, n * 512:(n + 1) * 512], w_lo[1][:, k, n * 512:(n + 1) * 512]))
                                    for k in range(2)]).then_inc(s_tm, 1)
                        pe.wait_ge(s_tm, (e + 1) * 2 * NT)
                        pe.sem_inc(w_used, 1)

                @block.scalar
                def _(act):
                    act.sem_inc(s_ge, 3)
                    for h in range(2):
                        nc.scalar.copy(x_hi[:, 4 * h:4 * h + 4], featA[:, 4 * h:4 * h + 4]).then_inc(s_xh, 1)
                    with act.Fori(0, NEXP) as e:
                        for i in range(2):
                            w_wait(act, s0 + i, e, 16)
                            nc.scalar.copy(w_hi[i], w_at[i]).then_inc(s_wh, 1)
                        for j, (m, ch, a, wd) in enumerate(units):
                            act.wait_ge(s_f, e * 6 + j + 1)
                            hold(act)
                            nc.scalar.activation(ht[:, m, a:a + wd], bank[4 + ch][:, 0:wd], ACT.Gelu,
                                                 bias=bcol[:, ds(e * 2 + 12 + m, 1)]).then_inc(s_ge, 1)
                            act.wait_ge(s_ge, e * 6 + j + 4)
                            nc.scalar.copy(ht_hi[:, m, a:a + wd], ht[:, m, a:a + wd]).then_inc(s_hh, 1)

                @block.vector
                def _(dve):
                    dve.sem_inc(s_ae, 4)
                    flat = comb.rearrange("p t n -> p (t n)")

                    def rest_of_w(i, e):
                        dve.wait_ge(s_wh, e * 2 + i + 1)
                        nc.vector.tensor_tensor(w_lo[i], w_at[i], as32(w_hi[i]), ALU.subtract).then_inc(s_wl, 1)

                    def expert(e, more):
                        rest_of_w(1, e)
                        for j, (m, ch, a, wd) in enumerate(units):
                            dve.wait_ge(s_hh, e * 6 + j + 1)
                            nc.vector.tensor_tensor(ht_lo[:, m, a:a + wd], ht[:, m, a:a + wd], as32(ht_hi[:, m, a:a + wd]),
                                                    ALU.subtract).then_inc(s_hl, 1)
                        for u in range(2 * NT):
                            t, n = divmod(u, 2)
                            part = tokB[:, t, n * 512:(n + 1) * 512]
                            dve.wait_ge(s_tm, e * 2 * NT + u + 1)
                            nc.vector.scalar_tensor_tensor(out=part, in0=bank[u % 4][0:P, :],
                                                           scalar=flat[:, ds(e + t * NEXP, 1)], in1=part,
                                                           op0=ALU.mult, op1=ALU.add).then_inc(s_ae, 1)
                            if more and u == 14:
                                rest_of_w(0, e + 1)

                    for h in range(2):
                        dve.wait_ge(s_xh, h + 1)
                        nc.vector.tensor_tensor(featA_r[:, 4 * h:4 * h + 4], featA[:, 4 * h:4 * h + 4],
                                                as32(x_hi[:, 4 * h:4 * h + 4]), ALU.subtract).then_inc(s_xl, 1)
                    rest_of_w(0, 0)
                    with dve.Fori(0, NEXP - 1) as e:
                        expert(e, True)
                    expert(NEXP - 1, False)

        xlr = bigC[0:P, 0:NT * 2 * HID].rearrange("p (t n) -> p t n", t=NT)
        self_score = small[0:P, 208:208 + NT * GH].rearrange("p (t h) -> p t h", t=NT)

        def phase_gat_in():
            (s_own, s_rq, s_sq, s_w, s_mm, s_ev, s_tr, s_te, s_lr, s_le, s_st, s_at) = (sem("gi_" + x) for x in (
                "own", "sumsq", "sqrt", "scaled", "mm", "evac", "turned", "turnedevac", "lr", "lrevac", "stored", "att"))
            s0 = take(2)
            rq = small[0:P, 160:160 + NT]
            xd = stage1[0:P, :].rearrange("p (t n) -> p t n", t=NT)
            xdT = stage2[:, 0:2 * N].rearrange("p (k n) -> p k n", k=2)
            att = attrow[:, :]
            zs = bigC[0:P, 2 * D * 3:2 * D * 3 + NT * HID]
            with nc.Block() as block:
                @block.sync
                def _(sp):
                    sp.dma_start(att, A["L1_gnn_att_row"].rearrange("(o n) -> o n", o=1)
                                 .to_broadcast([P, HID])).then_inc(s_at, 16)
                    load_slots(sp, s0 + 2)
                    sp.wait_ge(s_le, NT)
                    sp.dma_start(ptile(XL), xlr[:, :, 0:HID]).then_inc(s_st, 16)
                    sp.dma_start(ptile(XRD), xlr[:, :, HID:2 * HID]).then_inc(s_st, 16)
                    load_slots(sp, s0 + 4)
                    sp.wait_ge(s_st, 32)

                @block.vector
                def _(dve):
                    st = Steps(dve, s_own)
                    nc.vector.tensor_scalar(rq, rq, 1.0 / D, 1e-6, ALU.mult, ALU.add).then_inc(s_rq, 1)
                    w_wait(dve, s0)
                    w = ring_k(s0 % 2, KD, CW)
                    gains = bcol[:, 48:48 + KD].rearrange("p (k o) -> p k o", o=1).to_broadcast([128, KD, CW])
                    nc.vector.tensor_tensor(w, w, gains, ALU.mult).then_inc(s_w, 1)
                    dve.wait_ge(s_sq, 1)
                    nc.vector.reciprocal(rq, rq).then_inc(s_rq, 1)
                    for t in range(NT):
                        dve.wait_ge(s_tr, t + 1)
                        nc.vector.tensor_copy(xdT[:, :, t * P:(t + 1) * P],
                                              bank[4 + t % 2][:, 0:2 * P].rearrange("p (k n) -> p k n", k=2)
                                              ).then_inc(s_te, 1)
                    dve.wait_ge(s_le, NT)
                    dve.wait_ge(s_at, 16)
                    zt = zs.rearrange("p (t n) -> p t n", t=NT)
                    st.link(nc.vector.tensor_tensor(zt, xlr[:, :, 0:HID], xlr[:, :, HID:2 * HID], ALU.add))
                    st.link(nc.vector.scalar_tensor_tensor(out=zs, in0=zs, scalar=0.2, in1=zs, op0=ALU.mult,
                                                           op1=ALU.max))
                    st.link(nc.vector.tensor_tensor(zt, zt, att.rearrange("p (o n) -> p o n", o=1)
                                                    .to_broadcast([P, NT, HID]), ALU.mult))
                    nc.vector.tensor_reduce(self_score.rearrange("p t h -> p (t h)"),
                                            zs.rearrange("p (h n) -> p h n", n=GD), AX.X, ALU.add)

                @block.scalar
                def _(act):
                    act.wait_ge(s_rq, 1)
                    nc.scalar.sqrt(rq, rq).then_inc(s_sq, 1)
                    act.wait_ge(s_rq, 2)
                    for t in range(NT):
                        act.wait_ge(s_mm, t + 1)
                        nc.scalar.activation(xd[:, t, :], bank[t % 4][0:P, 0:CW], ACT.Copy,
                                             scale=rq[:, t:t + 1]).then_inc(s_ev, 1)
                    for t in range(NT):
                        act.wait_ge(s_lr, t + 1)
                        nc.scalar.copy(xlr[:, t, :], bank[t % 4][0:P, :]).then_inc(s_le, 1)

                @block.tensor
                def _(pe):
                    pe.wait_ge(s_w, 1)
                    w = ring_k(s0 % 2, KD, CW)
                    for t in range(NT):
                        if t >= 4:
                            pe.wait_ge(s_ev, t - 3)
                        for k in range(KD):
                            m = nc.tensor.matmul(bank[t % 4][0:P, 0:CW], featA[:, k, t * P:(t + 1) * P], w[:, k, :],
                                                 start=(k == 0), stop=(k == KD - 1))
                        m.then_inc(s_mm, 1)
                    pe.wait_ge(s_mm, NT)
                    pe.sem_inc(w_used, 1)
                    for t in range(NT):
                        pe.wait_ge(s_ev, t + 1)
                        if t >= 2:
                            pe.wait_ge(s_te, t - 1)
                        for k in range(2):
                            m = nc.tensor.transpose(bank[4 + t % 2][:, k * P:(k + 1) * P], xd[:, t, k * 128:(k + 1) * 128],
                                                    ident[0:P, 0:P])
                        m.then_inc(s_tr, 1)
                    w_wait(pe, s0 + 1)
                    w = ring_k((s0 + 1) % 2, 4, HID)
                    for t in range(NT):
                        pe.wait_ge(s_te, t + 1)
                        if t >= 4:
                            pe.wait_ge(s_le, t - 3)
                        for side in range(2):
                            for k in range(2):
                                m = nc.tensor.matmul(bank[t % 4][0:P, side * HID:(side + 1) * HID],
                                                     xdT[:, k, t * P:(t + 1) * P], w[:, 2 * side + k, :],
                                                     start=(k == 0), stop=(k == 1))
                        m.then_inc(s_lr, 1)
                    pe.wait_ge(s_lr, NT)
                    pe.sem_inc(w_used, 1)

        def phase_gat():
            (s_rl, s_ru, s_b1, s_ng, s_sl, s_sps, s_spt, s_spc, s_bc, s_tm, s_in, s_n1) = (sem("g1_" + x) for x in (
                "row", "rowused", "bcast", "neg", "slice", "parts", "partsT", "partsTcopy", "scores", "max", "init",
                "own"))
            (s_m, s_b2, s_oht, s_oh, s_me, s_x, s_p, s_r, s_ag, s_idx, s_dn, s_n2, s_self, s_end, s_n3, s_gt) = (
                sem("g2_" + x) for x in (
                    "max", "bcast", "onehotT", "onehot", "maxback", "shifted", "p", "rhs", "agg", "idx", "tile", "own",
                    "self", "last", "own_tile", "turned"))
            s_g = [sem(f"g2_gather{h}") for h in range(2)]
            s_m2, s_xl, s_rx = sem("g2_selfp"), sem("g2_xl"), sem("g2_extrarow")
            zero = stage4[0:P, 0:P]
            pos = [0]

            def inC(n, parts=P):
                a = pos[0]
                pos[0] += n
                assert pos[0] <= NT * N, pos[0]
                return bigC[0:parts, a:a + n]

            xg = [x[0:P, 0:HB * HID].rearrange("p (g n) -> p g n", g=HB) for x in (stage1, stage2)]
            xs = stage1[0:P, 1024:1024 + SUB * GH].rearrange("p (g n) -> p g n", g=SUB)
            away = stage1[0:P, 1056:1056 + SUB]
            m_ = stage1[0:P, 1064:1064 + GH + 1]
            pself = stage1[0:P, 1072:1072 + GH]
            rden = stage1[0:P, 1080:1080 + GH]
            idx = edge_ix[:, 0, :, :]
            neg = stage2[0:P, 1024:1024 + BE]
            oht = neg
            junk = stage3[0:P, 0:1000].rearrange("p (h n) -> p h n", h=2)
            oh = stage3[0:P, 1000:2000].rearrange("p (g n) -> p g n", g=SUB)
            spt = stage3[0:12, 2000:2500].bitcast(BF16)
            rhs = inC(SUB * (HID + GH)).rearrange("p (g n) -> p g n", g=SUB)
            rself = inC(HID + GH)
            gout = inC(NT * HID).rearrange("p (t n) -> p t n", t=NT)
            xl_own = inC(NT * HID).rearrange("p (t n) -> p t n", t=NT)
            inA = featA[0:P, :, :].rearrange("p k n -> p (k n)")
            parts_all = inA[:, 0:(NB + 1) * SUB * 6].bitcast(BF16).rearrange("p (j n) -> p j n", n=12)
            rest = inA[:, 2048:2048 + 2 * NB * SUB * GH].rearrange("p (i j n) -> p i j n", i=2, n=GH)
            row = inA[0:1, 4608:4608 + BE // 2].bitcast(F16)
            one16 = inA[0:1, 5632:5632 + 64].bitcast(F16)[:, 0:P]
            psl = inA[:, 5696:5696 + SUB * 6].bitcast(BF16).rearrange("p (g n) -> p g n", g=SUB)
            sel = inA[0:12, 5760:5760 + GH * P // 2].bitcast(BF16).rearrange("p (h n) -> p h n", h=GH)
            t12 = small[0:12, 0:GH]
            by_head = lambda v: v.rearrange("p (h n) -> p h n", n=GD)
            ov = lambda v, n: v.rearrange("p (h o) -> p h o", o=1).to_broadcast([P, v.shape[1], n])
            sc = scores[:, :].rearrange("p (j n) -> p j n", n=GH)
            tb = bank[2][0:12, :].bitcast(BF16).rearrange("p (g n) -> p g n", g=SUB)
            meb = bank[2][0:P, 0:5 * SUB].rearrange("p (g n) -> p g n", g=SUB)
            accb = bank[3][0:P, 0:HID + GH]

            with nc.Block() as block:
                @block.sync
                def _(sp):
                    sp.dma_start(xl_own, ptile(XL)).then_inc(s_xl, 16)
                    sp.dma_start(DR[NB:NB + 1, :], iota16[0:1, 0:BE]).then_inc(s_rx, 16)
                    sp.wait_ge(s_rx, 16)
                    sp.sem_inc(s_ru, 1)
                    with sp.Fori(0, NT) as d:
                        lo, cnt, base = batches(sp, d)
                        for half in range(2):
                            with sp.Fori(0, cnt + 1) as r:
                                at = (base + d) * 2 + half * (cnt + 1) + r
                                sp.wait_ge(s_ru, at + 1)
                                sp.dma_start(row[:, :], DR[ds(batch(lo, r, 1), 1), :]).then_inc(s_rl, 16)

                @block.gpsimd
                def _(pool):
                    with pool.Fori(0, NT) as d:
                        lo, cnt, base = batches(pool, d)
                        with pool.Fori(0, cnt) as r:
                            for h in range(2):
                                pool.wait_ge(s_r, (base + r) * 2 + h + 1)
                                hold(pool)
                                nc.gpsimd.tensor_copy(idx[:, h, :], src_i[:, ds(batch(lo, r) * SUB + h * HB, HB)]
                                                      ).then_inc(s_idx, 1)
                                pool.wait_ge(s_idx, (base + r) * 2 + h + 1)
                                hold(pool)
                                for g in range(HB):
                                    nc.gpsimd.indirect_dma_start(
                                        out=xg[h][:, g, :], out_offset=None, in_=XL,
                                        in_offset=bass.IndirectOffsetOnAxis(ap=idx[:, h, g:g + 1].bitcast(U32), axis=0),
                                        ).then_inc(s_g[h], 16)

                @block.tensor
                def _(pe):
                    def broadcast_row(at, s_out, n_out):
                        pe.wait_ge(s_rl, at * 16 + 16)
                        hold(pe)
                        for h in range(2):
                            m = nc.tensor.matmul(bank[h][0:P, 0:500], one16[:, :], row[:, h * 500:(h + 1) * 500],
                                                 start=True, stop=True)
                        m.then_inc(s_out, 1)
                        pe.wait_ge(s_out, n_out)
                        pe.sem_inc(s_ru, 1)

                    def turn_parts(step):
                        pe.wait_ge(s_sps, step + 1)
                        pe.wait_ge(s_spc, step + 1)
                        hold(pe)
                        for g in range(SUB):
                            m = nc.tensor.transpose(tb[:, g, 0:P], psl[:, g, :], ident16[0:P, 0:P])
                        m.then_inc(s_spt, 1)

                    pe.sem_inc(s_bc, 8)
                    pe.wait_ge(s_in, 1)
                    with pe.Fori(0, NT) as d:
                        lo, cnt, base = batches(pe, d)
                        pe.wait_ge(s_dn, d + 1)
                        hold(pe)
                        broadcast_row((base + d) * 2, s_b1, base + d + 1)
                        turn_parts(base + d)
                        hold(pe)
                        with pe.Fori(0, cnt) as r:
                            step = base + r
                            pe.wait_ge(s_spc, step + d + 2)
                            for hd in range(GH):
                                if hd == 2:
                                    pe.wait_ge(s_ng, step + 1)
                                    hold(pe)
                                    broadcast_row((base + d) * 2 + r + 1, s_b1, step + d + 2)
                                    turn_parts(step + d + 1)
                                for h in range(2):
                                    u = hd * 2 + h
                                    pe.wait_ge(s_tm, step * 8 + u + 1)
                                    hold(pe)
                                    nc.tensor.matmul(bank[4 + u % 4][0:P, 0:500], sel[:, hd, :],
                                                     spt[:, h * 500:(h + 1) * 500], start=True, stop=True
                                                     ).then_inc(s_bc, 1)
                        pe.wait_ge(s_spc, base + d + cnt + 2)
                        hold(pe)
                        broadcast_row((base + d) * 2 + cnt + 1, s_b2, base + d + 1)
                        pe.wait_ge(s_self, d + 1)
                        nc.tensor.matmul(accb, ident[0:P, 0:P], rself, start=True, stop=False, skip_group_check=True)
                        with pe.Fori(0, cnt) as r:
                            step = base + r
                            pe.wait_ge(s_oht, step + d + 1)
                            pe.wait_ge(s_x, step + 1)
                            for g in range(SUB):
                                m = nc.tensor.matmul(meb[:, g, :], oht[:, g:BE:SUB], m_, start=True, stop=True)
                            m.then_inc(s_me, 1)
                            broadcast_row((base + d) * 2 + cnt + r + 2, s_b2, step + d + 2)
                            for h in range(2):
                                pe.wait_ge(s_r, step * 2 + h + 3)
                                for g in range(h * HB, h * HB + HB):
                                    m = nc.tensor.matmul(accb, oh[:, g, :], rhs[:, g, :], start=False, stop=False,
                                                         skip_group_check=True)
                            m.then_inc(s_ag, 1)
                        pe.wait_ge(s_self, d + 1)
                        nc.tensor.matmul(accb, zero, rself, start=False, stop=True, skip_group_check=True
                                         ).then_inc(s_end, 1)
                    pe.wait_ge(s_dn, NT + 1)
                    for t in range(NT):
                        for k in range(2):
                            c = t * 2 + k
                            m = nc.tensor.transpose(bank[3 + c // 4][:, (c % 4) * P:(c % 4 + 1) * P],
                                                    gout[:, t, k * 128:(k + 1) * 128], ident[0:P, 0:P])
                    m.then_inc(s_gt, 1)

                @block.scalar
                def _(act):
                    act.sem_inc(s_spc, 1)
                    act.wait_ge(s_sl, 1)
                    with act.Fori(0, NT) as d:
                        lo, cnt, base = batches(act, d)
                        with act.Fori(0, cnt + 1) as r:
                            step = base + d + r
                            nc.scalar.copy(psl[:, :, :], parts_all[:, ds(batch(lo, r, 1) * SUB, SUB), :]
                                           ).then_inc(s_sps, 1)
                            act.wait_ge(s_spt, step + 1)
                            act.wait_ge(s_bc, (base + r) * 8 + 8)
                            nc.scalar.copy(spt.rearrange("p (n g) -> p g n", g=SUB), tb[:, :, 0:P]).then_inc(s_spc, 1)
                        act.wait_ge(s_m, d + 1)
                        nc.scalar.activation(rself[:, HID:HID + GH], pself, ACT.Exp).then_inc(s_m2, 1)
                        with act.Fori(0, cnt) as r:
                            step = base + r
                            act.wait_ge(s_x, step + 2)
                            nc.scalar.activation(rhs[:, :, HID:HID + GH], xs, ACT.Exp).then_inc(s_p, 1)
                    act.wait_ge(s_gt, 1)
                    for t in range(NT):
                        c = t * 2
                        nc.scalar.copy(gatT[:, :, t * P:(t + 1) * P],
                                       bank[3 + c // 4][:, (c % 4) * P:(c % 4 + 2) * P]
                                       .rearrange("p (k n) -> p k n", k=2))

                @block.vector
                def _(dve):
                    st = Steps(dve, s_n1)
                    part = lambda i: parts_all[:, 0:NB * SUB, i * GH:(i + 1) * GH]
                    st.link(nc.vector.tensor_copy(part(0), sc))
                    st.link(nc.vector.tensor_tensor(rest[:, 0], sc, part(0), ALU.subtract))
                    st.link(nc.vector.tensor_copy(part(1), rest[:, 0]))
                    st.link(nc.vector.tensor_tensor(rest[:, 1], rest[:, 0], part(1), ALU.subtract))
                    st.link(nc.vector.tensor_copy(part(2), rest[:, 1]))
                    st.link(nc.vector.memset(parts_all[:, NB * SUB:(NB + 1) * SUB, :], 0.0))
                    nc.vector.sem_inc(s_sl, 1)
                    st.link(nc.vector.tensor_tensor(t12, ident[0:12, 0:4], ident[0:12, 4:8], ALU.add))
                    st.link(nc.vector.tensor_tensor(t12, t12, ident[0:12, 8:12], ALU.add))
                    st.link(nc.vector.tensor_copy(sel[:, :, :], t12.rearrange("p (h o) -> p h o", o=1)
                                                  .to_broadcast([12, GH, P])))
                    st.link(nc.vector.memset(one16[:, :], 1.0))
                    st.link(nc.vector.memset(zero, 0.0))
                    st.link(nc.vector.memset(m_, 1.0))
                    nc.vector.sem_inc(s_in, 1)
                    dve.sem_inc(s_x, 1)
                    dve.sem_inc(s_ag, 1)
                    dve.sem_inc(s_dn, 1)
                    dve.sem_inc(s_tm, 4)
                    dve.sem_inc(s_r, 2)
                    dve.wait_ge(s_xl, 16)
                    with dve.Fori(0, NT) as d:
                        lo, cnt, base = batches(dve, d)
                        so = Steps(dve, s_n3, d, 6)
                        id_d = ids[:, ds(d, 1)]

                        def onehot_t(step):
                            dve.wait_ge(s_b2, step + 1)
                            for h in range(2):
                                x = nc.vector.tensor_scalar(oht[:, h * 500:(h + 1) * 500], bank[h][0:P, 0:500], id_d,
                                                            None, ALU.is_equal)
                            x.then_inc(s_oht, 1)

                        dve.wait_ge(s_dn, d + 1)
                        so.link(nc.vector.tensor_copy(m_[:, 0:GH],
                                                      self_score[:, ds(d, 1), :].rearrange("p o h -> p (o h)")))
                        hold(dve)
                        with dve.Fori(0, cnt) as r:
                            step = base + r
                            dve.wait_ge(s_b1, step + d + 1)
                            dve.wait_ge(s_tm, step * 8 + 4)
                            for h in range(2):
                                x = nc.vector.tensor_scalar(neg[:, h * 500:(h + 1) * 500], bank[h][0:P, 0:500], id_d,
                                                            -BIG, ALU.not_equal, ALU.mult)
                            x.then_inc(s_ng, 1)
                            dve.wait_ge(s_ng, step + 1)
                            for hd in range(GH):
                                for h in range(2):
                                    u = hd * 2 + h
                                    dve.wait_ge(s_bc, step * 8 + u + 9)
                                    dve.wait_ge(s_tm, step * 8 + u + 3 + h)
                                    hold(dve)
                                    nc.vector.tensor_tensor_reduce(
                                        junk[:, h, :], bank[4 + u % 4][0:P, 0:500], neg[:, h * 500:(h + 1) * 500],
                                        1.0, m_[:, hd:hd + 1], ALU.add, ALU.max, m_[:, hd:hd + 1]).then_inc(s_tm, 1)
                        dve.wait_ge(s_tm, (base + cnt) * 8 + 4)
                        so.link(nc.vector.tensor_tensor(pself, self_score[:, ds(d, 1), :].rearrange("p o h -> p (o h)"),
                                                        m_[:, 0:GH], ALU.subtract))
                        nc.vector.sem_inc(s_m, 1)
                        dve.wait_ge(s_m2, d + 1)
                        so.link(nc.vector.tensor_tensor(by_head(rself[:, 0:HID]),
                                                        xl_own[:, ds(d, 1), :].rearrange("p o (h n) -> p (o h) n", n=GD),
                                                        ov(rself[:, HID:HID + GH], GD), ALU.mult))
                        nc.vector.sem_inc(s_self, 1)
                        onehot_t(base + d)
                        with dve.Fori(0, cnt) as r:
                            step = base + r
                            st = Steps(dve, s_n2, step, 2)
                            dve.wait_ge(s_ag, step + 1)
                            nc.vector.tensor_tensor(
                                oh, iota16[:, ds(d * P, P)].rearrange("p (o n) -> p o n", o=1).to_broadcast([P, SUB, P]),
                                dst_f[:, ds(batch(lo, r) * SUB, SUB)].rearrange("p (q o) -> p q o", o=1)
                                .to_broadcast([P, SUB, P]), ALU.is_equal)
                            dve.wait_ge(s_me, step + 1)
                            a3 = away.rearrange("p (g o) -> p g o", o=1)
                            st.link(nc.vector.tensor_tensor(xs, sc[:, ds(batch(lo, r) * SUB, SUB), :], meb[:, :, 0:GH],
                                                            ALU.subtract))
                            st.link(nc.vector.tensor_scalar(a3, meb[:, :, GH:GH + 1], 1.0, BIG, ALU.subtract, ALU.mult))
                            nc.vector.tensor_tensor(xs, xs, a3.to_broadcast([P, SUB, GH]), ALU.add).then_inc(s_x, 1)
                            st.end()
                            dve.wait_ge(s_p, step + 1)
                            for h in range(2):
                                dve.wait_ge(s_g[h], step * 64 + 64)
                                hs = slice(h * HB, h * HB + HB)
                                nc.vector.tensor_tensor(
                                    rhs[:, hs, 0:HID].rearrange("p g (h n) -> p g h n", n=GD),
                                    xg[h].rearrange("p g (h n) -> p g h n", n=GD),
                                    rhs[:, hs, HID:HID + GH].rearrange("p g (h o) -> p g h o", o=1)
                                    .to_broadcast([P, HB, GH, GD]), ALU.mult).then_inc(s_r, 1)
                            onehot_t(step + d + 1)
                        dve.wait_ge(s_oht, base + d + cnt + 1)
                        dve.wait_ge(s_end, d + 1)
                        so.link(nc.vector.tensor_scalar(rden, accb[:, HID:HID + GH], 1e-16, None, ALU.add))
                        so.link(nc.vector.reciprocal(rden, rden))
                        so.link(nc.vector.tensor_tensor(gout[:, ds(d, 1), :].rearrange("p o (h n) -> p (o h) n", h=GH),
                                                        by_head(accb[:, 0:HID]), ov(rden, GD), ALU.mult))
                        nc.vector.sem_inc(s_dn, 1)
                        so.end()

        w1T = bigB[:, 5120:5120 + KD * 512].rearrange("p (k n) -> p k n", k=KD)
        w2T = ring[:, :].rearrange("p i k n -> p (i k n)")[:, 0:4 * D].rearrange("p (k n) -> p k n", k=4)

        def phase_binarize():
            s_ab, s_sg, s_own, s_tr, s_ev = (sem("bw_" + x) for x in ("abs", "sign", "own", "turned", "evac"))
            s_trb = sem("bw_banks")
            s_ld = [sem(f"bw_in{i}") for i in range(2)]
            pieces = [(A["L1_ffn_w1"], j, D, w1T) for j in range(4)] + [(A["L1_ffn_w2"], j, 512, w2T) for j in range(8)]
            wn = [x[:, 0:D] for x in (stage1, stage2)]
            sg = stage3[:, 0:2 * D].rearrange("p (i n) -> p i n", i=2)
            def evac(dve, q):
                src, j, n, dst = pieces[q]
                for b in range(n // 512):
                    dve.wait_ge(s_trb, sum(p[2] // 512 for p in pieces[:q]) + b + 1)
                    nc.vector.tensor_copy(dst[:, 4 * b:4 * b + 4, j * 128:(j + 1) * 128],
                                          bank[2 * (q % 2) + b][:, :].rearrange("p (k n) -> p k n", k=4)
                                          ).then_inc(s_ev, 1)

            with nc.Block() as block:
                @block.sync
                def _(sp):
                    for q, (src, j, n, _) in enumerate(pieces):
                        if q >= 2:
                            sp.wait_ge(s_tr, q - 1)
                        sp.dma_start(wn[q % 2][:, 0:n], src[j * 128:(j + 1) * 128, :]).then_inc(s_ld[q % 2], 16)

                @block.scalar
                def _(act):
                    for q, (src, j, n, dst) in enumerate(pieces):
                        act.wait_ge(s_ld[q % 2], 16 * (q // 2) + 16)
                        if q >= 2:
                            act.wait_ge(s_ab, q - 1)
                        nc.scalar.sign(sg[:, q % 2, 0:n], wn[q % 2][:, 0:n]).then_inc(s_sg, 1)

                @block.vector
                def _(dve):
                    st = Steps(dve, s_own)
                    for q, (src, j, n, dst) in enumerate(pieces):
                        w, s = wn[q % 2][:, 0:n], sg[:, q % 2, 0:n]
                        mean = small[:, 250:251]
                        dve.wait_ge(s_ld[q % 2], 16 * (q // 2) + 16)
                        st.link(nc.vector.tensor_reduce(mean, w, AX.X, ALU.add, apply_absolute_value=True))
                        st.link(nc.vector.tensor_scalar(mean, mean, 1.0 / n, None, ALU.mult))
                        dve.wait_ge(s_sg, q + 1)
                        st.link(nc.vector.scalar_tensor_tensor(out=s, in0=s, scalar=mean, in1=w, op0=ALU.mult,
                                                               op1=ALU.subtract))
                        nc.vector.tensor_tensor(w, w, s, ALU.add).then_inc(s_ab, 1)
                        dve.wait_ge(s_ab, q + 1)
                        if q:
                            evac(dve, q - 1)
                    evac(dve, len(pieces) - 1)

                @block.tensor
                def _(pe):
                    for q, (src, j, n, dst) in enumerate(pieces):
                        pe.wait_ge(s_ab, q + 1)
                        if q >= 2:
                            pe.wait_ge(s_ev, sum(p[2] // 512 for p in pieces[:q - 1]))
                        for k in range(n // 128):
                            m = nc.tensor.transpose(bank[2 * (q % 2) + k // 4][:, (k % 4) * 128:(k % 4 + 1) * 128],
                                                    wn[q % 2][:, k * 128:(k + 1) * 128], ident[:, :])
                            if k % 4 == 3:
                                m.then_inc(s_trb, 1)
                        pe.wait_ge(s_trb, sum(p[2] // 512 for p in pieces[:q + 1]))
                        pe.sem_inc(s_tr, 1)

        phase_start()
        if stop >= 1:
            phase_norm("n0", load=A["x"], store=XN)
        if stop >= 2:
            phase_h0()
        if stop >= 3:
            phase_edges0()
        if stop >= 4:
            phase_agg0()
        if stop >= 5:
            phase_mix("m0", True)
        if stop >= 6:
            phase_out("o0", lambda k, t: featB[:, k, t * P:(t + 1) * P], KD, A["L0_mix_bo"], XN)
        if stop >= 7:
            phase_norm("na", gain=(A["L0_mix_g1"], A["L0_mix_be1"]), keep=True, eps=1e-12)
        if stop >= 8:
            phase_up("u0", None, COLS["L0_mix_b1"][0])
        if stop >= 9:
            phase_down("d0", None, A["L0_mix_b2"])
        if stop >= 10:
            phase_norm("nb", gain=(A["L0_mix_g2"], A["L0_mix_be2"]), add=XR, keep=True, turn=False, eps=1e-12)
        if stop >= 11:
            phase_norm("n1", keep_sum=True)
        if stop >= 12:
            phase_route()
        if stop >= 13:
            phase_moe()
            recycle()
        if stop >= 14:
            phase_norm("n2", tok=tokB, store_src=XR, rms=160)
        if stop >= 15:
            phase_gat_in()
        if stop >= 16:
            phase_mix("m1", False)
        if stop >= 17:
            phase_gat()
        if stop >= 18:
            phase_out("o1", lambda k, t: (featB if k < KD else gatT)[:, k % KD, t * P:(t + 1) * P], KD + 2,
                      A["L1_mix_b_proj"], XR)
        if stop >= 19:
            phase_norm("n3")
            phase_binarize()
            phase_up("u1", lambda m: w1T[:, :, m * 128:(m + 1) * 128], COLS["L1_ffn_b1"][0])
        if stop >= 20:
            phase_down("d1", lambda c: w2T[:, :, c * 512:(c + 1) * 512], A["L1_ffn_b2"], dram=out)
        if stop < 20:
            with nc.Block() as block:
                @block.sync
                def _(sp):
                    for i in range(2):
                        if fulls[i]:
                            sp.wait_ge(w_full[i], fulls[i][-1])


def kernel(**inputs):
    import numpy as _np
    import concourse.bacc as _bacc
    from concourse import mybir as _mybir
    from concourse.bass_utils import run_bass_kernel_spmd as _run

    nc = _bacc.Bacc("TRN2", target_bir_lowering=False, num_devices=1)
    given = {name: _np.asarray(a) for name, a in inputs.items()}
    given["L1_gnn_att_row"] = given["L1_gnn_att"].reshape(-1)
    arrays, aps = {}, {}
    for name, a in given.items():
        if name in COLS:
            a = a.reshape(-1, 128).T
        a = _np.ascontiguousarray(a)
        arrays[f"in_{name}"] = a
        aps[name] = nc.dram_tensor(f"in_{name}", a.shape, _mybir.dt.from_np(a.dtype), kind="ExternalInput").ap()
    out = nc.dram_tensor("out", (N, D), F32, kind="ExternalOutput").ap()
    build(nc, aps, out)
    return _run(nc, [arrays], core_ids=[0]).results[0]["out"]
```

```python
from contextlib import ExitStack

import concourse.bass as bass
from concourse import mybir

F32 = mybir.dt.float32
F32R = mybir.dt.float32r
F16 = mybir.dt.float16
BF16 = mybir.dt.bfloat16
I32 = mybir.dt.int32
U32 = mybir.dt.uint32
ALU = mybir.AluOpType
ACT = mybir.ActivationFunctionType
AX = mybir.AxisListType
ds = bass.ds

N = 1250
P = 125
NT = N // P
D = 1024
KD = D // 128
CW = 256
NC = D // CW
E = 40000
SUB = 8
BE = SUB * P
NB = E // BE
HB = SUB // 2
FCH = [(0, 500), (500, 500), (1000, 250)]
RCH = [(0, 418), (418, 416), (834, 416)]
NEXP = 16
EH = 256
HID = 256
GH = 4
GD = HID // GH
BIG = 2.0 ** 100
COLS = {"L0_mix_bq": (0, 8), "L0_mix_b1": (8, 4), "L0_ffn_b1": (12, 32), "L1_ffn_b1": (44, 4),
        "L1_gnn_rms_w": (48, 8), "L1_gnn_att": (56, 2)}


class Steps:

    def __init__(self, eng, sem, turn=None, per=0, base=0):
        self.eng, self.sem, self.n, self.turn, self.per, self.base = eng, sem, 0, turn, per, base

    def value(self):
        return self.base + self.n if self.turn is None else self.turn * self.per + self.base + self.n

    def link(self, ins):
        self.n += 1
        ins.then_inc(self.sem, 1)
        self.eng.wait_ge(self.sem, self.value())

    def end(self):
        assert self.turn is None or self.n == self.per, (self.n, self.per)


def build(nc, A, out, stop=99):
    with ExitStack() as ctx:
        def sb(name, shape, dt=F32):
            return ctx.enter_context(nc.sbuf_tensor(name, shape, dt))

        phase_sems = []

        def sem(name):
            phase_sems.append(nc.alloc_semaphore(name=name))
            return phase_sems[-1]

        def stream_sem(name):
            return nc.alloc_semaphore(name=name)

        def recycle():
            nc.clear_and_free_semaphores(list(phase_sems))
            phase_sems.clear()
            nc.all_engine_barrier()

        def scratch(name, shape, dt=F32):
            return nc.dram_tensor(name, shape, dt, kind="Internal").ap()

        shapes = [("featA", [128, KD, N]),
                  ("bigB", [128, NT * D]),
                  ("bigC", [128, NT * N]),
                  ("ring", [128, 2, 10, CW])] + [
                  (f"stage{i}", [128, NT * CW]) for i in range(1, 5)]
        with ExitStack() as rounded:
            featA_r, bigB_r, bigC_r, ring_r, *stage_r = [
                rounded.enter_context(nc.sbuf_tensor(name + "_r", shape, F32R)) for name, shape in shapes]
        featA, bigB, bigC, ring, stage1, stage2, stage3, stage4 = [sb(name, shape) for name, shape in shapes]
        gatT = stage4[:, 0:2 * N].rearrange("p (k n) -> p k n", k=2)
        tokB = bigB[0:P, 0:NT * D].rearrange("p (t n) -> p t n", t=NT)
        tokC = bigC[0:P, 0:NT * D].rearrange("p (t n) -> p t n", t=NT)
        featB = bigB[:, 0:KD * N].rearrange("p (k n) -> p k n", k=KD)
        ident = sb("ident", [128, 128])
        ident16 = sb("ident16", [128, 128], BF16)
        ones = sb("ones", [128, 128])
        ids_i = sb("ids_i", [P, NT], I32)[:, :]
        ids = sb("ids", [P, NT])[:, :]
        blocks = sb("blocks", [128, 128])
        iota_i = bigC[0:P, NT * N // 2:NT * N // 2 + N].bitcast(I32)
        iota16 = sb("iota16", [P, N], F16)
        edge_i = sb("edge_i", [P, 2, NB * SUB], I32)
        src_i, dst_i = edge_i[:, 0, :], edge_i[:, 1, :]
        src_f = sb("src_f", [P, NB * SUB])
        dst_f = sb("dst_f", [P, NB * SUB])
        scores = sb("scores", [P, NB * SUB * GH])
        table = sb("table", [1, 4, NT], I32)
        small = sb("small", [128, 256])
        bcol = sb("bcol", [128, 64])
        edge_ix = sb("edge_ix", [P, 4, 2, HB], I32)
        attrow = sb("attrow", [P, HID])
        comb = sb("comb", [P, NT, NEXP])[:, :, :]
        bank = [ctx.enter_context(nc.psum_tensor(f"bank{i}", [128, 512], F32)) for i in range(8)]

        XR = scratch("XR", (N, D))
        XN = scratch("XN", (N, D))
        XL = scratch("XL", (N, HID))
        XRD = scratch("XRD", (N, HID))
        CTX = scratch("CTX", (128, KD, N))
        DR = scratch("DR", (NB + 1, BE), F16)
        ptile = lambda ap: ap.rearrange("(t p) n -> p t n", p=P)

        slots = []

        def chunked(w, n, cw=CW):
            v = w.rearrange("(k p) n -> p k n", p=128)
            for c in range(n):
                slots.append([(slice(0, v.shape[1]), v[:, :, c * cw:(c + 1) * cw])])

        w_full = [stream_sem("w_full0"), stream_sem("w_full1")]
        w_used = stream_sem("w_used")
        loaded = [0]
        took = [0]

        def ring_k(i, nk, cw, ring=ring):
            return ring[:, i].rearrange("p k n -> p (k n)")[:, 0:nk * cw].rearrange("p (k n) -> p k n", k=nk)

        def load_slots(sp, upto):
            while loaded[0] < min(upto, len(slots)):
                s = loaded[0]
                if s >= 2:
                    sp.wait_ge(w_used, s - 1)
                parts = slots[s]
                for kk, v in parts:
                    nk, cw = v.shape[1], v.shape[2]
                    dst = ring[:, s % 2, kk, :] if cw == CW else ring_k(s % 2, nk, cw)
                    sp.dma_start(dst, v).then_inc(w_full[s % 2], 16)
                fulls[s % 2].append((fulls[s % 2][-1] if fulls[s % 2] else 0) + 16 * len(parts))
                loaded[0] += 1

        fulls = [[], []]

        def full_value(s):
            return sum(16 * len(slots[q]) for q in range(s % 2, s + 1, 2))

        chunked(A["L0_gnn_W"], NC)
        q0 = [A[f"L0_mix_W{x}"].rearrange("(k p) n -> p k n", p=128) for x in "qkv"]
        for c in range(NC):
            for w in q0:
                slots.append([(slice(0, KD), w[:, :, c * CW:(c + 1) * CW])])
        chunked(A["L0_mix_Wo"], NC)
        chunked(A["L0_mix_W1"], 2)
        chunked(A["L0_mix_W2"], 2, 512)
        for e in range(NEXP):
            slots.append([(slice(0, KD), A["L0_ffn_W1"][e].rearrange("(k p) n -> p k n", p=128))])
            slots.append([(slice(0, 2), A["L0_ffn_W2"][e].rearrange("(k p) n -> p k n", p=128))])
        chunked(A["L1_gnn_W_down"], 1)
        wl = A["L1_gnn_Wl"].rearrange("(k p) n -> p k n", p=128)
        wr = A["L1_gnn_Wr"].rearrange("(k p) n -> p k n", p=128)
        slots.append([(slice(0, 2), wl), (slice(2, 4), wr)])
        qkv = A["L1_mix_W_qkv"].rearrange("(k p) n -> p k n", p=128)
        for c in range(NC):
            for j in range(3):
                slots.append([(slice(0, KD), qkv[:, :, j * D + c * CW:j * D + (c + 1) * CW])])
        wp = A["L1_mix_W_proj"].rearrange("(k p) n -> p k n", p=128)
        wu = A["L1_gnn_W_up"].rearrange("(k p) n -> p k n", p=128)
        for c in range(NC):
            slots.append([(slice(0, KD), wp[:, :, c * CW:(c + 1) * CW]),
                          (slice(KD, KD + 2), wu[:, :, c * CW:(c + 1) * CW])])

        def take(n):
            s = took[0]
            took[0] += n
            return s

        def w_wait(eng, s, turn=None, per=0):
            eng.wait_ge(w_full[s % 2], full_value(s) if turn is None else turn * per + full_value(s))


        idle = stream_sem("idle")

        def hold(eng):
            eng.sem_inc(idle, 1)

        def row_bc(v, n):
            return v.rearrange("(o n) -> o n", o=1).to_broadcast([P, n])

        def phase_start():
            s_bc = sem("columns_in")
            s_ld, s_c, s_t, s_x, s_p = sem("edges_in"), sem("consts"), sem("start_dve"), sem("start_pe"), sem("start_pool")
            dw = stage1[0:NB, 0:BE].bitcast(I32)
            dwf = stage2[0:NB, 0:BE]
            dw16 = stage3[0:NB, 0:BE // 2].bitcast(F16)
            s_dr = sem("rows_stored")
            mm = small[0:NB, 0:2]
            row = small[0:1, 16:16 + 2 * NB]
            big = bigC[0:1, 0:8 * NT * NB].rearrange("p (a t b) -> p a t b", a=8, t=NT)
            with nc.Block() as block:
                @block.sync
                def _(sp):
                    for v, t in ((A["src"], src_i), (A["dst"], dst_i)):
                        sp.dma_start(t.rearrange("p (b g) -> p b g", g=SUB),
                                     v.rearrange("(b p g) -> p b g", p=P, g=SUB)).then_inc(s_ld, 16)
                    sp.dma_start(dw, A["dst"].rearrange("(b e) -> b e", b=NB)).then_inc(s_ld, 16)
                    for name, (at, n) in COLS.items():
                        sp.dma_start(bcol[:, at:at + n], A[name]).then_inc(s_bc, 16)
                    load_slots(sp, 2)
                    sp.wait_ge(s_bc, 16 * len(COLS))
                    sp.wait_ge(s_dr, 1)
                    sp.dma_start(DR[0:NB, :], dw16).then_inc(s_dr, 16)
                    sp.wait_ge(s_dr, 17)

                @block.gpsimd
                def _(pool):
                    nc.gpsimd.iota(iota_i[:], pattern=[[1, N]], base=0, channel_multiplier=0).then_inc(s_p, 1)
                    nc.gpsimd.iota(ids_i, pattern=[[P, NT]], base=0, channel_multiplier=1)
                    nc.gpsimd.memset(ones[:], 1.0).then_inc(s_p, 1)
                    pool.wait_ge(s_p, 2)
                    nc.gpsimd.affine_select(out=ident[:], in_=ones[:], compare_op=ALU.is_equal, fill=0.0, base=0,
                                            pattern=[[-1, 128]], channel_multiplier=1).then_inc(s_p, 1)
                    nc.gpsimd.memset(blocks[:], 0.0).then_inc(s_p, 1)
                    pool.wait_ge(s_p, 4)
                    nc.gpsimd.memset(blocks[0:64, 0:64], 1.0).then_inc(s_p, 1)
                    nc.gpsimd.memset(blocks[64:128, 64:128], 1.0).then_inc(s_p, 1)

                @block.tensor
                def _(pe):
                    pe.wait_ge(s_p, 6)
                    pe.wait_ge(s_t, 1)
                    for i in range(2):
                        last = nc.tensor.transpose(bank[0][0:1, i * NB:(i + 1) * NB], mm[:, i:i + 1], ident[0:NB, 0:NB])
                    last.then_inc(s_x, 1)

                @block.vector
                def _(dve):
                    st = Steps(dve, s_c)
                    dve.wait_ge(s_ld, 48)
                    nc.vector.tensor_copy(src_f[:], src_i)
                    nc.vector.tensor_copy(dst_f[:], dst_i)
                    nc.vector.tensor_copy(dw16, dw).then_inc(s_dr, 1)
                    st.link(nc.vector.tensor_copy(dwf, dw))
                    nc.vector.tensor_reduce(mm[:, 0:1], dwf, AX.X, ALU.max)
                    nc.vector.tensor_reduce(mm[:, 1:2], dwf, AX.X, ALU.min).then_inc(s_t, 1)
                    dve.wait_ge(s_p, 3)
                    nc.vector.tensor_copy(ident16[:], ident[:])
                    nc.vector.tensor_copy(ids, ids_i)
                    st.link(nc.vector.tensor_copy(iota16[:], iota_i[:]))
                    dve.wait_ge(s_x, 1)
                    st.link(nc.vector.tensor_copy(row, bank[0][0:1, 0:2 * NB]))
                    tile_at = iota16[0:1, 0:N:P].rearrange("p (t o) -> p t o", o=1).to_broadcast([1, NT, NB])
                    b_at = iota16[0:1, 0:NB].rearrange("p (o b) -> p o b", o=1).to_broadcast([1, NT, NB])
                    rows = row.rearrange("p (a o b) -> p a o b", a=2, o=1)
                    bmax, bmin = (rows[:, a].to_broadcast([1, NT, NB]) for a in range(2))
                    st.link(nc.vector.tensor_tensor(big[:, 0], bmax, tile_at, ALU.is_lt))
                    st.link(nc.vector.scalar_tensor_tensor(out=big[:, 1], in0=big[:, 0], scalar=1000.0, in1=b_at,
                                                           op0=ALU.mult, op1=ALU.add))
                    st.link(nc.vector.scalar_tensor_tensor(out=big[:, 2], in0=bmin, scalar=float(P), in1=tile_at,
                                                           op0=ALU.subtract, op1=ALU.is_lt))
                    st.link(nc.vector.scalar_tensor_tensor(out=big[:, 3], in0=b_at, scalar=1.0, in1=big[:, 2],
                                                           op0=ALU.add, op1=ALU.mult))
                    lo, hi, cnt, base = (small[0:1, 128 + 16 * i:128 + 16 * i + NT] for i in range(4))
                    st.link(nc.vector.tensor_reduce(lo, big[:, 1], AX.X, ALU.min))
                    st.link(nc.vector.tensor_reduce(hi, big[:, 3], AX.X, ALU.max))
                    st.link(nc.vector.tensor_scalar(lo, lo, float(NB - 1), None, ALU.min))
                    st.link(nc.vector.tensor_tensor(cnt, hi, lo, ALU.subtract))
                    st.link(nc.vector.tensor_scalar(cnt, cnt, 1.0, None, ALU.max))
                    st.link(nc.vector.memset(base[:, 0:1], 0.0))
                    for t in range(1, NT):
                        st.link(nc.vector.tensor_tensor(base[:, t:t + 1], base[:, t - 1:t], cnt[:, t - 1:t], ALU.add))
                    nc.vector.tensor_copy(table[:, 0], lo)
                    nc.vector.tensor_copy(table[:, 1], cnt)
                    nc.vector.tensor_copy(table[:, 2], base)

        def phase_norm(name, load=None, gain=None, add=None, keep=None, keep_sum=None, turn=True, store=None,
                       store_src=None, rms=None, eps=1e-5, tok=None):
            tok = tokC if tok is None else tok
            copy_kept = keep and turn
            sem_if = lambda what, *names: [sem(f"{name}_{x}") if what else None for x in names]
            s_in = sem_if(load is not None, "in0", "in1")
            s_ad = sem_if(add is not None, "add0", "add1")
            s_st = sem_if(store is not None or store_src is not None, "stored0", "stored1")
            s_row, = sem_if(gain is not None, "rows")
            s_tr, s_ev = sem_if(turn, "turned", "evac")
            s_kp, = sem_if(copy_kept, "kept")
            s_va, s_sd, s_y, s_own = sem_if(True, "var", "sd", "y", "own")
            ain = stage1[0:P, 0:2 * D].rearrange("p (i n) -> p i n", i=2)
            y = stage2[0:P, 0:2 * D].rearrange("p (i n) -> p i n", i=2)
            rows = stage3[0:P, 0:2 * D].rearrange("p (i n) -> p i n", i=2)
            junk = stage4[0:P, 0:D]
            stats = small[0:P, 20:44].rearrange("p (i n) -> p i n", i=2)
            moments = small[0:P, 0:2 * NT].rearrange("p (t n) -> p t n", n=2)
            sd = small[0:P, 44:44 + NT]
            pair = small[0:P, 54:58].rearrange("p (i n) -> p i n", i=2)
            with nc.Block() as block:
                @block.sync
                def _(sp):
                    if gain is not None:
                        for i in range(2):
                            sp.dma_start(rows[:, i], row_bc(gain[i], D)).then_inc(s_row, 16)
                    if load is not None:
                        for t in range(NT):
                            if t >= 2:
                                sp.wait_ge(s_own, 3 * (t // 2 - 1) + 1)
                            sp.dma_start(tok[:, t, :], load[t * P:(t + 1) * P, :]).then_inc(s_in[t % 2], 16)
                    for t in range(NT + 2):
                        i = t % 2
                        if t >= 2:
                            sp.wait_ge(s_y, t - 1)
                            if store is not None:
                                sp.dma_start(store[(t - 2) * P:(t - 1) * P, :], y[:, i]).then_inc(s_st[i], 16)
                            if store_src is not None:
                                sp.dma_start(store_src[(t - 2) * P:(t - 1) * P, :],
                                             tok[:, t - 2]).then_inc(s_st[i], 16)
                        if t < NT and add is not None:
                            sp.dma_start(ain[:, i], add[t * P:(t + 1) * P, :]).then_inc(s_ad[i], 16)
                    load_slots(sp, took[0] + 2)
                    if store is not None or store_src is not None:
                        for i in range(2):
                            sp.wait_ge(s_st[i], 16 * NT // 2 + (16 if store is not None else 0))

                @block.vector
                def _(dve):
                    with dve.Fori(0, NT // 2) as tt:
                        st = Steps(dve, s_own, tt, 3)
                        for i in range(2):
                            t = tt * 2 + i
                            if load is not None:
                                dve.wait_ge(s_in[i], tt * 16 + 16)
                            for h in range(2):
                                last = nc.vector.bn_stats(stats[:, i, h * 6:h * 6 + 6],
                                                          tok[:, ds(t, 1), h * 512:(h + 1) * 512]
                                                          .rearrange("p o n -> p (o n)"))
                        st.link(last)
                        for i in range(2):
                            hold(dve)
                            last = nc.vector.bn_aggr(pair[:, i, :], stats[:, i, :])
                        st.link(last)
                        hold(dve)
                        st.link(nc.vector.tensor_copy(moments[:, ds(tt * 2, 2), :], pair))
                        st.end()
                    nc.vector.tensor_scalar(sd.rearrange("p (t o) -> p t o", o=1), moments[:, :, 1:2], eps, None,
                                            ALU.add).then_inc(s_va, 1)
                    per = 2 * (1 + (2 if gain is not None else 0) + (1 if rms is not None else 0)
                               + (1 if add is not None else 0) + (1 if keep_sum else 0))
                    base = 3 * NT // 2 + 1
                    if gain is not None:
                        dve.wait_ge(s_row, 32)
                    dve.wait_ge(s_sd, 1)
                    st = Steps(dve, s_own, base=base - 1)
                    st.link(nc.vector.reciprocal(sd, sd))
                    with dve.Fori(0, NT // 2) as tt:
                        st = Steps(dve, s_own, tt, per, base=base)
                        for i in range(2):
                            t = tt * 2 + i
                            x = tok[:, ds(t, 1), :].rearrange("p o n -> p (o n)")
                            if turn:
                                dve.wait_ge(s_tr, t * 2 + 2)
                            if store is not None:
                                dve.wait_ge(s_st[i], tt * 16 + 16)
                            if copy_kept:
                                dve.wait_ge(s_kp, t + 1)
                            steps_left = [(2 if gain is not None else 0) + (1 if add is not None else 0)]

                            def to():
                                steps_left[0] -= 1
                                return x if keep and not turn and steps_left[0] < 0 else y[:, i]

                            st.link(nc.vector.tensor_scalar(to(), x, moments[:, ds(t, 1), 0:1]
                                                            .rearrange("p o n -> p (o n)"), sd[:, ds(t, 1)],
                                                            ALU.subtract, ALU.mult))
                            if gain is not None:
                                st.link(nc.vector.tensor_tensor(to(), y[:, i], rows[:, 0], ALU.mult))
                                st.link(nc.vector.tensor_tensor(to(), y[:, i], rows[:, 1], ALU.add))
                            if add is not None:
                                dve.wait_ge(s_ad[i], tt * 16 + 16)
                                st.link(nc.vector.tensor_tensor(to(), y[:, i], ain[:, i], ALU.add))
                            if rms is not None:
                                st.link(nc.vector.scalar_tensor_tensor(
                                    out=junk, in0=y[:, i], scalar=1.0, in1=y[:, i], op0=ALU.mult, op1=ALU.mult,
                                    accum_out=small[0:P, ds(t + rms, 1)]))
                            if keep_sum:
                                st.link(nc.vector.tensor_tensor(tokB[:, ds(t, 1), :].rearrange("p o n -> p (o n)"),
                                                                x, y[:, i], ALU.add))
                            nc.vector.sem_inc(s_y, 1)
                        st.end()

                @block.scalar
                def _(act):
                    if turn:
                        act.sem_inc(s_tr, 4)
                        act.sem_inc(s_ev, 4)
                    if store is not None:
                        for i in range(2):
                            act.sem_inc(s_st[i], 16)
                    if copy_kept:
                        act.sem_inc(s_kp, 2)
                    act.wait_ge(s_va, 1)
                    nc.scalar.sqrt(sd, sd).then_inc(s_sd, 1)
                    with act.Fori(0, NT // 2) as tt:
                        for i in range(2):
                            t = tt * 2 + i
                            if copy_kept:
                                act.wait_ge(s_y, t + 1)
                                nc.scalar.copy(tokC[:, ds(t, 1), :].rearrange("p o n -> p (o n)"), y[:, i]
                                               ).then_inc(s_kp, 1)
                            if turn:
                                for h in range(2):
                                    act.wait_ge(s_tr, t * 2 + h + 5)
                                    nc.scalar.copy(
                                        featA[:, 4 * h:4 * h + 4, ds(t * P, P)],
                                        bank[2 * i + h][:, 0:4 * P].rearrange("p (k n) -> p k n", k=4)).then_inc(s_ev, 1)

                if turn:
                    @block.tensor
                    def _(pe):
                        with pe.Fori(0, NT // 2) as tt:
                            for i in range(2):
                                pe.wait_ge(s_y, tt * 2 + i + 1)
                                for k in range(KD):
                                    if k % 4 == 0:
                                        pe.wait_ge(s_ev, (tt * 2 + i) * 2 + k // 4 + 1)
                                    m = nc.tensor.transpose(bank[2 * i + k // 4][:, (k % 4) * P:(k % 4 + 1) * P],
                                                            y[:, i, k * 128:(k + 1) * 128], ident[0:P, 0:P])
                                    if k % 4 == 3:
                                        m.then_inc(s_tr, 1)

        def pe_tok(pe, s0, lhs, nk, s_mm, s_free, turns=NC // 2, cw=CW, rhs_more=None):
            with pe.Fori(0, turns) as tt:
                for i in range(2):
                    w_wait(pe, s0 + i, tt, 16 * len(slots[s0 + i]))
                    w = ring_k((s0 + i) % 2, nk, cw)
                    for t in range(NT):
                        u = i * NT + t
                        pe.wait_ge(s_free, tt * 2 * NT + u + 1)
                        for k in range(nk):
                            m = nc.tensor.matmul(bank[u % 4][0:P, 0:cw], lhs(k, t), w[:, k, :],
                                                 start=(k == 0), stop=(k == nk - 1))
                        m.then_inc(s_mm, 1)

        def phase_h0():
            s_mm, s_free, s_a, s_own = sem("h0_mm"), sem("h0_free"), sem("h0_a"), sem("h0_own")
            s0 = take(NC)
            al, ar = small[0:P, 128:128 + NT], small[0:P, 144:144 + NT]
            arow = stage3[0:P, 0:2 * D].rearrange("p (i n) -> p i n", i=2)
            junk = stage1[0:P, 0:D]
            with nc.Block() as block:
                @block.sync
                def _(sp):
                    sp.dma_start(arow, A["L0_gnn_a"].rearrange("o (i n) -> o i n", i=2)
                                 .to_broadcast([P, 2, D])).then_inc(s_a, 16)
                    load_slots(sp, s0 + NC + 2)

                @block.tensor
                def _(pe):
                    pe_tok(pe, s0, lambda k, t: featA[:, k, t * P:(t + 1) * P], KD, s_mm, s_free)

                @block.scalar
                def _(act):
                    act.sem_inc(s_free, 4)
                    with act.Fori(0, NC // 2) as tt:
                        for i in range(2):
                            for t in range(NT):
                                u = i * NT + t
                                act.wait_ge(s_mm, tt * 2 * NT + u + 1)
                                if t == NT - 1:
                                    act.sem_inc(w_used, 1)
                                nc.scalar.copy(tokB[:, t, ds((tt * 2 + i) * CW, CW)],
                                               bank[u % 4][0:P, 0:CW]).then_inc(s_free, 1)

                @block.vector
                def _(dve):
                    st = Steps(dve, s_own)
                    dve.wait_ge(s_a, 16)
                    for t in range(NT):
                        dve.wait_ge(s_free, 4 + (NC - 1) * NT + t + 1)
                        for i, dst in ((0, al), (1, ar)):
                            st.link(nc.vector.tensor_tensor_reduce(junk, tokB[:, t, :], arow[:, i], 1.0, 0.0,
                                                                   ALU.mult, ALU.add, dst[:, t:t + 1]))

        def batches(eng, d):
            return [eng.value_load(table[0:1, i, ds(d, 1)], min_val=0, max_val=(NB - 1, NB, NB * NT)[i])
                    for i in range(3)]

        def batch(lo, r, past=0):
            return nc.s_assert_within(lo + r, 0, NB - 1 + past, skip_runtime_bounds_check_because="the table keeps "
                                      "first <= NB - 1 and first + count <= NB")

        def phase_edges0():
            s_dg, s_al, s_alb, s_z, s_ez, s_c, s_free, s_oh, s_used, s_own = (sem("e0_" + x) for x in (
                "diag", "al", "alb", "z", "expz", "count", "free", "onehot", "used", "own"))
            al, ar = small[0:P, 128:128 + NT], small[0:P, 144:144 + NT]
            ohs = stage1[0:P, :].bitcast(F16)[:, 0:HB * N].rearrange("p (q n) -> p q n", q=HB)
            ohd = stage2[0:P, :].bitcast(F16)[:, 0:SUB * P].rearrange("p (q n) -> p q n", q=SUB)
            z = stage2[0:P, SUB * P // 2:SUB * P // 2 + N]
            alb = stage3[0:P, 0:N]
            zero16 = gatT[0:P, 0, 0:P // 2 + 1].bitcast(F16)[:, 0:P]
            diag = gatT[0:P, 1, 0:N].rearrange("p (t n) -> p t n", t=NT)
            emat = bigC[0:P, 0:NT * N].rearrange("p (t n) -> p t n", t=NT)
            with nc.Block() as block:
                @block.vector
                def _(dve):
                    nc.vector.memset(zero16, 0.0)
                    nc.vector.tensor_tensor(diag, ident[0:P, 0:P].rearrange("p (o n) -> p o n", o=1)
                                            .to_broadcast([P, NT, P]),
                                            al.rearrange("p (t o) -> p t o", o=1).to_broadcast([P, NT, P]),
                                            ALU.mult).then_inc(s_dg, 1)
                    dve.wait_ge(s_alb, 3)
                    dve.sem_inc(s_free, 2)
                    with dve.Fori(0, NT) as d:
                        lo, cnt, base = batches(dve, d)
                        st = Steps(dve, s_own, d, 1)
                        dve.wait_ge(s_free, d + 2)
                        st.link(nc.vector.tensor_scalar(z, alb, ar[:, ds(d, 1)], None, ALU.add))
                        nc.vector.scalar_tensor_tensor(out=z, in0=z, scalar=0.1, in1=z, op0=ALU.mult,
                                                       op1=ALU.max).then_inc(s_z, 1)
                        st.end()
                        with dve.Fori(0, cnt) as r:
                            for q in range(SUB):
                                u = (base + r) * SUB + q
                                j = batch(lo, r) * SUB + q
                                dve.wait_ge(s_used, u + 1)
                                if q % HB == 0:
                                    nc.vector.tensor_tensor(
                                        ohd[:, q:q + HB, :],
                                        iota16[:, ds(d * P, P)].rearrange("p (o n) -> p o n", o=1).to_broadcast([P, HB, P]),
                                        dst_f[:, ds(j, HB)].rearrange("p (q o) -> p q o", o=1).to_broadcast([P, HB, P]),
                                        ALU.is_equal)
                                nc.vector.tensor_scalar(ohs[:, q % HB, :], iota16[:], src_f[:, ds(j, 1)], None,
                                                        ALU.is_equal).then_inc(s_oh, 1)
                        dve.wait_ge(s_ez, d + 1)
                        dve.wait_ge(s_c, d + 1)
                        for ch, (a, w) in enumerate(FCH):
                            m = nc.vector.tensor_tensor(emat[:, ds(d, 1), a:a + w].rearrange("p o n -> p (o n)"),
                                                        bank[ch][0:P, 0:w], z[:, a:a + w], ALU.mult)
                        m.then_inc(s_free, 1)

                @block.scalar
                def _(act):
                    act.wait_ge(s_al, 1)
                    for ch, (a, w) in enumerate(FCH):
                        nc.scalar.copy(alb[:, a:a + w], bank[5 + ch][0:P, 0:w]).then_inc(s_alb, 1)
                    with act.Fori(0, NT) as d:
                        act.wait_ge(s_z, d + 1)
                        nc.scalar.activation(z, z, ACT.Exp, scale=-1.0).then_inc(s_ez, 1)

                @block.tensor
                def _(pe):
                    pe.wait_ge(s_dg, 1)
                    for t in range(NT):
                        m = nc.tensor.matmul(bank[5 + t // 4][0:P, (t % 4) * P:(t % 4 + 1) * P], ones[0:P, 0:P],
                                             diag[:, t, :], start=True, stop=True)
                    m.then_inc(s_al, 1)
                    pe.sem_inc(s_used, HB)
                    with pe.Fori(0, NT) as d:
                        lo, cnt, base = batches(pe, d)
                        pe.wait_ge(s_free, d + 2)
                        for ch, (a, w) in enumerate(FCH):
                            nc.tensor.matmul(bank[ch][0:P, 0:w], zero16, iota16[:, a:a + w], start=True, stop=False,
                                             skip_group_check=True)
                        with pe.Fori(0, cnt) as r:
                            for q in range(SUB):
                                pe.wait_ge(s_oh, (base + r) * SUB + q + 1)
                                for ch, (a, w) in enumerate(FCH):
                                    m = nc.tensor.matmul(bank[ch][0:P, 0:w], ohd[:, q, :], ohs[:, q % HB, a:a + w],
                                                         start=False, stop=False, skip_group_check=True)
                                m.then_inc(s_used, 1)
                        for ch, (a, w) in enumerate(FCH):
                            m = nc.tensor.matmul(bank[ch][0:P, 0:w], zero16, iota16[:, a:a + w], start=False,
                                                 stop=True, skip_group_check=True)
                        m.then_inc(s_c, 1)

        def phase_agg0():
            s_rs, s_rr, s_mm, s_free, s_m, s_e, s_own, s_ch = (sem("a0_" + x) for x in (
                "rowsum", "recip", "mm", "free", "min", "exp", "own", "chunk"))
            s_x = [sem(f"a0_x{i}") for i in range(2)]
            s_st = [sem(f"a0_stored{i}") for i in range(2)]
            emat = bigC[0:P, 0:NT * N].rearrange("p (t n) -> p t n", t=NT)
            rs = small[0:P, 160:160 + NT]
            xch = [s_[0:P, :].rearrange("p (t n) -> p t n", t=NT) for s_ in (stage1, stage2)]
            low = stage3[0:P, :]
            hp = stage4[0:P, :]
            xv, rv = ptile(A["x"]), ptile(XR)
            with nc.Block() as block:
                @block.sync
                def _(sp):
                    for c in range(NC + 2):
                        if c >= 2:
                            sp.wait_ge(s_ch, c)
                            sp.dma_start(rv[:, :, (c - 2) * CW:(c - 1) * CW], xch[c % 2]).then_inc(s_st[c % 2], 16)
                            sp.wait_ge(s_st[c % 2], 16 * (c // 2))
                        if c < NC:
                            sp.dma_start(xch[c % 2], xv[:, :, c * CW:(c + 1) * CW]).then_inc(s_x[c % 2], 16)

                @block.tensor
                def _(pe):
                    for t in range(NT):
                        for d in range(NT):
                            m = nc.tensor.matmul(bank[7][0:P, t:t + 1], emat[:, d, t * P:(t + 1) * P], ones[0:P, 0:1],
                                                 start=(d == 0), stop=(d == NT - 1))
                    m.then_inc(s_rs, 1)
                    with pe.Fori(0, NC // 2) as cc:
                        for u in range(2 * NT):
                            t = u % NT
                            pe.wait_ge(s_free, cc * 2 * NT + u + 1)
                            for d in range(NT):
                                m = nc.tensor.matmul(bank[u % 4][0:P, 0:CW], emat[:, d, t * P:(t + 1) * P],
                                                     tokB[:, d, ds((cc * 2 + u // NT) * CW, CW)],
                                                     start=(d == 0), stop=(d == NT - 1))
                            m.then_inc(s_mm, 1)

                @block.vector
                def _(dve):
                    st = Steps(dve, s_own)
                    dve.wait_ge(s_rs, 1)
                    st.link(nc.vector.tensor_scalar(rs, bank[7][0:P, 0:NT], 1e-5, None, ALU.add))
                    st.link(nc.vector.reciprocal(rs, rs))
                    nc.vector.sem_inc(s_rr, 1)
                    with dve.Fori(0, NC // 2) as cc:
                        st = Steps(dve, s_own, cc, 4, base=2)
                        for c in range(2):
                            dve.wait_ge(s_free, (cc * 2 + c) * NT + NT + 4)
                            nc.vector.tensor_scalar(low, hp, 0.0, None, ALU.min).then_inc(s_m, 1)
                            dve.wait_ge(s_e, cc * 2 + c + 1)
                            st.link(nc.vector.scalar_tensor_tensor(out=hp, in0=low, scalar=-1.0, in1=hp,
                                                                   op0=ALU.add, op1=ALU.max))
                            dve.wait_ge(s_x[c], cc * 16 + 16)
                            xc = xch[c].rearrange("p t n -> p (t n)")
                            st.link(nc.vector.tensor_tensor(xc, xc, hp, ALU.add))
                            nc.vector.sem_inc(s_ch, 1)
                        st.end()

                @block.scalar
                def _(act):
                    act.wait_ge(s_rr, 1)
                    act.sem_inc(s_free, 4)
                    act.sem_inc(s_ch, 1)
                    with act.Fori(0, NC // 2) as cc:
                        for c in range(2):
                            act.wait_ge(s_ch, cc * 2 + c + 1)
                            for t in range(NT):
                                u = c * NT + t
                                act.wait_ge(s_mm, cc * 2 * NT + u + 1)
                                nc.scalar.activation(hp[:, t * CW:(t + 1) * CW], bank[u % 4][0:P, 0:CW], ACT.Copy,
                                                     scale=rs[:, t:t + 1]).then_inc(s_free, 1)
                            act.wait_ge(s_m, cc * 2 + c + 1)
                            nc.scalar.activation(low, low, ACT.Exp).then_inc(s_e, 1)

        def three_products(out_, pairs):
            todo = [(a, b) for (ah, al), (bh, bl) in pairs for a, b in ((ah, bh), (ah, bl), (al, bh))]
            for i, (a, b) in enumerate(todo):
                m = nc.tensor.matmul(out_, a, b, start=(i == 0), stop=(i == len(todo) - 1))
            return m

        def phase_mix(name, normed):
            (s_row, s_q, s_qe, s_mq, s_eq, s_q2, s_n, s_ne, s_t, s_te, s_mk, s_ek, s_k2, s_kn, s_kr, s_kv, s_kve,
             s_cx, s_ce, s_own) = (sem(f"{name}_" + x) for x in (
                 "rows", "q", "qevac", "qmin", "qexp", "qsq", "norm", "normevac", "tok", "tokevac", "kmin", "kexp",
                 "ksq", "knorm", "kvin", "kv", "kvevac", "ctx", "ctxevac", "own"))
            s0 = take(3 * NC)
            qt = bigC[:, 0:2 * N].rearrange("p (m n) -> p m n", m=2)
            qv = bigC[:, 2 * N:4 * N].rearrange("p (m n) -> p m n", m=2)
            qt_all, qv_all = bigC[:, 0:2 * N], bigC[:, 2 * N:4 * N]
            tk = bigC[0:P, 4 * N:4 * N + NT * CW]
            kc, vc = stage1[0:P, :], stage2[0:P, :]
            kv = stage3[:, 0:512].rearrange("p (j n) -> p j n", j=4)
            n2, kn, rk = (small[0:P, 0 + 64 * i:40 + 64 * i] for i in range(3))
            rows = stage4[0:P, 0:2 * D].rearrange("p (i n) -> p i n", i=2)
            units = [(m, ch, a, w) for m in range(2) for ch, (a, w) in enumerate(RCH if normed else FCH)]
            NU = len(units)

            if normed:
                s_xh, s_xl, s_wh, s_wl, s_cst, s_back = (sem(f"{name}_" + x) for x in (
                    "xhi", "xlo", "whi", "wlo", "ctxstored", "ctxback"))
                x_hi = bigB_r[:, 0:KD * N].rearrange("p (k n) -> p k n", k=KD)
                w_hi = [x.rearrange("p (k n) -> p k n", k=KD) for x in (
                    bigC_r[:, 10060:10060 + KD * CW], stage_r[2][:, 512:512 + KD * CW])]
                ctx_c = bigC[:, 7560:7560 + 2 * N].rearrange("p (m n) -> p m n", m=2)

            def x_at(k, lo, n):
                at = slice(lo, lo + n)
                return (x_hi[:, k, at], featA_r[:, k, at]) if normed else featA[:, k, at]

            def products(out_, pairs):
                if normed:
                    return three_products(out_, pairs)
                for k, (a, b) in enumerate(pairs):
                    x = nc.tensor.matmul(out_, a, b, start=(k == 0), stop=(k == KD - 1))
                return x

            def w_hi_of(act, i, c, j, turn):
                if normed:
                    s = s0 + 3 * i + j
                    w_wait(act, s, turn, 48)
                    nc.scalar.copy(w_hi[s % 2], ring_k(s % 2, KD, CW)).then_inc(s_wh, 1)

            def w_lo_of(dve, i, c, j):
                if normed:
                    s = s0 + 3 * i + j
                    dve.wait_ge(s_wh, c * 3 + j + 1)
                    nc.vector.tensor_tensor(ring_k(s % 2, KD, CW, ring_r), ring_k(s % 2, KD, CW),
                                            w_hi[s % 2].bitcast(F32), ALU.subtract).then_inc(s_wl, 1)

            U4 = HB * HID
            slot4 = [bigC[0:P, 7680:7680 + 2 * U4], bigC[0:P, 7680 + 2 * U4:7680 + 4 * U4], stage4[0:P, 0:2 * U4],
                     stage3[0:P, 512:512 + 2 * U4]]
            slot4 = [x.rearrange("p (s g n) -> p s g n", s=2, g=HB) for x in slot4]
            NQ = NB * SUB // HB
            if not normed:
                s_gx = [sem(f"{name}_gather{i}") for i in range(4)]
                s_used, s_idx, s_so, s_at = (sem(f"{name}_" + x) for x in ("slotused", "idx", "score", "att"))

            def score_unit(dve, st2, q_at, k):
                xl, xr = slot4[k % 4][:, 0], slot4[k % 4][:, 1]
                flat = xl.rearrange("p g n -> p (g n)")
                dve.wait_ge(s_gx[k % 4], st2.turn * (NQ // 8 * 128) + (k // 4 + 1) * 128)
                st2.link(nc.vector.tensor_tensor(xl, xl, xr, ALU.add))
                st2.link(nc.vector.scalar_tensor_tensor(out=flat, in0=flat, scalar=0.2, in1=flat, op0=ALU.mult,
                                                        op1=ALU.max))
                st2.link(nc.vector.tensor_tensor(xl, xl, attrow[:, :].rearrange("p (o n) -> p o n", o=1)
                                                 .to_broadcast([P, HB, HID]), ALU.mult))
                nc.vector.tensor_reduce(scores[:, ds((q_at + k) * HB * GH, HB * GH)],
                                        flat.rearrange("p (h n) -> p h n", n=GD), AX.X, ALU.add).then_inc(s_used, 1)

            with nc.Block() as block:
                if not normed:
                    @block.gpsimd
                    def _(pool):
                        idx = edge_ix[:, :, :, :]
                        pool.sem_inc(s_used, 4)
                        with pool.Fori(0, NQ // 4) as qq:
                            for k in range(4):
                                q = qq * 4 + k
                                pool.wait_ge(s_used, q + 1)
                                hold(pool)
                                nc.gpsimd.tensor_copy(idx[:, k], edge_i[:, :, ds(q * HB, HB)]).then_inc(s_idx, 1)
                                pool.wait_ge(s_idx, q + 1)
                                hold(pool)
                                for side, rows_of in ((0, XL), (1, XRD)):
                                    for g in range(HB):
                                        nc.gpsimd.indirect_dma_start(
                                            out=slot4[k][:, side, g, :], out_offset=None, in_=rows_of,
                                            in_offset=bass.IndirectOffsetOnAxis(
                                                ap=idx[:, k, side, g:g + 1].bitcast(U32), axis=0)
                                        ).then_inc(s_gx[k], 16)

                @block.sync
                def _(sp):
                    if normed:
                        sp.dma_start(rows[:, 0], row_bc(A["L0_mix_bk"], D)).then_inc(s_row, 16)
                        sp.dma_start(rows[:, 1], row_bc(A["L0_mix_bv"], D)).then_inc(s_row, 16)
                    if normed:
                        sp.sem_inc(s_cst, 16)
                        for c in range(NC):
                            load_slots(sp, s0 + 3 * c + 4)
                            if c == NC - 1:
                                load_slots(sp, s0 + 3 * NC)
                                sp.wait_ge(s_t, 2 * NT * NC)
                                sp.dma_start(featB[:, 0:2 * c, :], CTX[:, 0:2 * c, :]).then_inc(s_back, 16)
                            sp.wait_ge(s_ce, (c + 1) * NU + 1)
                            sp.dma_start(CTX[:, 2 * c:2 * c + 2, :] if c < NC - 1 else featB[:, 2 * c:2 * c + 2, :],
                                         ctx_c).then_inc(s_cst, 16)
                            sp.wait_ge(s_cst, 16 * (c + 2))
                        sp.wait_ge(s_back, 16)
                    load_slots(sp, s0 + 3 * NC + 2)

                @block.tensor
                def _(pe):
                    pe.sem_inc(s_ce, 1)
                    with pe.Fori(0, NC // 2) as cc:
                        for i in range(2):
                            c = cc * 2 + i

                            def slot(j):
                                s = s0 + 3 * i + j
                                if normed:
                                    pe.wait_ge(s_wl, c * 3 + j + 1)
                                    parts = w_hi[s % 2], ring_k(s % 2, KD, CW, ring_r)
                                    return lambda k, lo, n: tuple(x[:, k, lo:lo + n] for x in parts)
                                w_wait(pe, s, cc, 48)
                                return lambda k, lo, n: ring_k(s % 2, KD, CW)[:, k, lo:lo + n]

                            w = slot(0)
                            for j, (m, ch, a, wd) in enumerate(units):
                                if j < 3:
                                    pe.wait_ge(s_ce, c * NU + 1)
                                else:
                                    pe.wait_ge(s_qe, c * NU + j - 2)
                                if normed:
                                    pe.wait_ge(s_xl, ch + 1)
                                products(bank[4 + ch][:, 0:wd], [(w(k, m * 128, 128), x_at(k, a, wd))
                                                                 for k in range(KD)]).then_inc(s_q, 1)

                            def tok(j):
                                w = slot(1 + j)
                                for t in range(NT):
                                    u = j * NT + t
                                    pe.wait_ge(s_te, c * 2 * NT + u + 1)
                                    products(bank[u % 4][0:P, 0:CW], [(x_at(k, t * P, P), w(k, 0, CW))
                                                                      for k in range(KD)]).then_inc(s_t, 1)

                            def scales(lhs):
                                for j, (m, ch, a, wd) in enumerate(units):
                                    if j < 3:
                                        pe.wait_ge(s_qe, c * NU + 4 + j)
                                    else:
                                        pe.wait_ge(s_ne, c * NU + j - 2)
                                    rhs = qv if normed else qt
                                    nc.tensor.matmul(bank[4 + ch][:, 0:wd], lhs(m), rhs[:, m, a:a + wd], start=True,
                                                     stop=True).then_inc(s_n, 1)

                            tok(0)
                            if normed:
                                pe.wait_ge(s_q2, c + 1)
                                scales(lambda m: blocks[:, :])
                            tok(1)
                            pe.wait_ge(s_kr, c + 1)
                            for m in range(2):
                                for what in range(1 if normed else 2):
                                    for t in range(NT):
                                        col = t * CW + m * 128
                                        x = nc.tensor.matmul(
                                            bank[7][:, (2 * m + what) * 128:(2 * m + what + 1) * 128],
                                            kc[:, col:col + 128], ones[0:P, :] if what else vc[:, col:col + 128],
                                            start=(t == 0), stop=(t == NT - 1))
                            x.then_inc(s_kv, 1)
                            pe.wait_ge(s_kve, c + 1)
                            if not normed:
                                scales(lambda m: kv[:, 2 * m + 1, :])
                            for j, (m, ch, a, wd) in enumerate(units):
                                if j < 3:
                                    pe.wait_ge(s_ne, c * NU + 4 + j)
                                else:
                                    pe.wait_ge(s_ce, c * NU + j - 1)
                                nc.tensor.matmul(bank[4 + ch][:, 0:wd], kv[:, 2 * m, :], qt[:, m, a:a + wd],
                                                 start=True, stop=True).then_inc(s_cx, 1)

                @block.scalar
                def _(act):
                    act.sem_inc(s_te, 4)
                    for a, wd in RCH if normed else ():
                        nc.scalar.copy(x_hi[:, :, a:a + wd], featA[:, :, a:a + wd]).then_inc(s_xh, 1)
                    with act.Fori(0, NC // 2) as cc:
                        for i in range(2):
                            c = cc * 2 + i
                            w_hi_of(act, i, c, 0, cc)
                            for j, (m, ch, a, wd) in enumerate(units):
                                if j == 3:
                                    w_hi_of(act, i, c, 1, cc)
                                act.wait_ge(s_q, c * NU + j + 1)
                                if j == NU - 1:
                                    act.sem_inc(w_used, 1)
                                if normed:
                                    hold(act)
                                    nc.scalar.activation(qt[:, m, a:a + wd], bank[4 + ch][:, 0:wd], ACT.Identity,
                                                         bias=bcol[:, ds(c * 2 + m, 1)]).then_inc(s_qe, 1)
                                else:
                                    nc.scalar.copy(qt[:, m, a:a + wd], bank[4 + ch][:, 0:wd]).then_inc(s_qe, 1)
                            act.wait_ge(s_mq, c + 1)
                            nc.scalar.activation(qv_all, qv_all, ACT.Exp).then_inc(s_eq, 1)

                            def evac(j, dst):
                                for t in range(NT):
                                    if j == 0 and t == 4:
                                        w_hi_of(act, i, c, 2, cc)
                                    if normed and j == 1 and t == 6:
                                        act.wait_ge(s_k2, c + 1)
                                        nc.scalar.sqrt(kn, n2).then_inc(s_kn, 1)
                                    u = j * NT + t
                                    act.wait_ge(s_t, c * 2 * NT + u + 1)
                                    if t == NT - 1:
                                        act.sem_inc(w_used, 1)
                                    nc.scalar.copy(dst[:, t * CW:(t + 1) * CW], bank[u % 4][0:P, 0:CW]).then_inc(s_te, 1)

                            evac(0, kc)
                            act.wait_ge(s_mk, c + 1)
                            nc.scalar.activation(tk, tk, ACT.Exp).then_inc(s_ek, 1)
                            if normed:
                                for j, (m, ch, a, wd) in enumerate(units):
                                    act.wait_ge(s_n, c * NU + j + 1)
                                    nc.scalar.sqrt(qv[:, m, a:a + wd], bank[4 + ch][:, 0:wd]).then_inc(s_ne, 1)
                            evac(1, vc)

                @block.vector
                def _(dve):
                    if normed:
                        for ch, (a, wd) in enumerate(RCH):
                            dve.wait_ge(s_xh, ch + 1)
                            nc.vector.tensor_tensor(featA_r[:, :, a:a + wd], featA[:, :, a:a + wd],
                                                    x_hi[:, :, a:a + wd].bitcast(F32), ALU.subtract).then_inc(s_xl, 1)
                        dve.wait_ge(s_row, 32)
                    with dve.Fori(0, NC // 2) as cc:
                        st = Steps(dve, s_own, cc, 18 if normed else 6)
                        if not normed:
                            st2 = Steps(dve, s_so, cc, NQ // 2 * 3)
                            done = [0]

                        def fill(k):
                            if not normed:
                                for _ in range(k):
                                    score_unit(dve, st2, cc * (NQ // 2), done[0])
                                    done[0] += 1

                        for i in range(2):
                            c = cc * 2 + i

                            def row(j):
                                return rows[:, j, ds(c * CW, CW)].rearrange("p (o n) -> p o n", o=1).to_broadcast([P, NT, CW])

                            def by_tile(v):
                                return v.rearrange("p (t n) -> p t n", t=NT)

                            w_lo_of(dve, i, c, 0)
                            w_lo_of(dve, i, c, 1)
                            dve.wait_ge(s_ce, c * NU + 1)
                            fill(3)
                            dve.wait_ge(s_qe, c * NU + NU)
                            nc.vector.tensor_scalar(qv_all, qt_all, 0.0, None, ALU.min).then_inc(s_mq, 1)
                            dve.wait_ge(s_eq, c + 1)
                            if normed:
                                st.link(nc.vector.scalar_tensor_tensor(out=qt_all, in0=qv_all, scalar=-1.0, in1=qt_all,
                                                                       op0=ALU.add, op1=ALU.max))
                                nc.vector.tensor_tensor(qv_all, qt_all, qt_all, ALU.mult).then_inc(s_q2, 1)
                            else:
                                st.link(nc.vector.scalar_tensor_tensor(out=qt_all, in0=qt_all, scalar=1.0, in1=qv_all,
                                                                       op0=ALU.add, op1=ALU.max))
                            w_lo_of(dve, i, c, 2)
                            fill(4)
                            dve.wait_ge(s_te, c * 2 * NT + NT + 4)
                            if normed:
                                st.link(nc.vector.tensor_tensor(by_tile(kc), by_tile(kc), row(0), ALU.add))
                            nc.vector.tensor_scalar(tk, kc, 0.0, None, ALU.min).then_inc(s_mk, 1)
                            dve.wait_ge(s_ek, c + 1)
                            if normed:
                                st.link(nc.vector.scalar_tensor_tensor(out=kc, in0=tk, scalar=-1.0, in1=kc,
                                                                       op0=ALU.add, op1=ALU.max))
                                st.link(nc.vector.tensor_tensor(tk, kc, kc, ALU.mult))
                                nc.vector.tensor_reduce(n2, tk.rearrange("p (h n) -> p h n", n=64), AX.X,
                                                        ALU.add).then_inc(s_k2, 1)
                                dve.wait_ge(s_ne, c * NU + NU)
                                st.link(nc.vector.reciprocal(qv_all, qv_all))
                                dve.wait_ge(s_kn, c + 1)
                                st.link(nc.vector.reciprocal(rk, kn))
                                kh = kc.rearrange("p (h n) -> p h n", n=64)
                                st.link(nc.vector.tensor_tensor(kh, kh, rk.rearrange("p (h o) -> p h o", o=1)
                                                                .to_broadcast([P, 4 * NT, 64]), ALU.mult))
                                for a, b in ((0, 8), (8, NT)):
                                    dve.wait_ge(s_te, c * 2 * NT + NT + b + 4)
                                    part = by_tile(vc)[:, a:b]
                                    bias = (rows[:, 1, ds(c * CW, CW)].rearrange("p (o n) -> p o n", o=1)
                                            .to_broadcast([P, b - a, CW]))
                                    st.link(nc.vector.tensor_tensor(part, part, bias, ALU.add))
                            else:
                                st.link(nc.vector.scalar_tensor_tensor(out=kc, in0=kc, scalar=1.0, in1=tk,
                                                                       op0=ALU.add, op1=ALU.max))
                                fill(4)
                                dve.wait_ge(s_te, c * 2 * NT + 2 * NT + 4)
                            nc.vector.sem_inc(s_kr, 1)
                            fill(1)
                            dve.wait_ge(s_kv, c + 1)
                            b7 = bank[7][:, :].rearrange("p (j n) -> p j n", j=4)
                            mask = blocks[:, :].rearrange("p (o n) -> p o n", o=1)
                            if normed:
                                nc.vector.scalar_tensor_tensor(out=kv[:, 0:4:2, :], in0=b7[:, 0:4:2, :], scalar=0.125,
                                                               in1=mask.to_broadcast([128, 2, 128]), op0=ALU.mult,
                                                               op1=ALU.mult).then_inc(s_kve, 1)
                            else:
                                nc.vector.tensor_tensor(kv, b7, mask.to_broadcast([128, 4, 128]),
                                                        ALU.mult).then_inc(s_kve, 1)
                                for j, (m, ch, a, wd) in enumerate(units):
                                    dve.wait_ge(s_n, c * NU + j + 1)
                                    nc.vector.tensor_scalar(qv[:, m, a:a + wd], bank[4 + ch][:, 0:wd], 1e-6, None,
                                                            ALU.add).then_inc(s_ne, 1)
                                dve.wait_ge(s_ne, c * NU + NU)
                                st.link(nc.vector.reciprocal(qv_all, qv_all))
                            if normed:
                                dve.wait_ge(s_cst, c * 16 + 16)
                            for j, (m, ch, a, wd) in enumerate(units):
                                dve.wait_ge(s_cx, c * NU + j + 1)
                                dst = ctx_c[:, m, a:a + wd] if normed else featB[:, ds(c * 2 + m, 1), a:a + wd].rearrange("p o n -> p (o n)")
                                nc.vector.tensor_tensor(dst, bank[4 + ch][:, 0:wd], qv[:, m, a:a + wd],
                                                        ALU.mult).then_inc(s_ce, 1)
                            fill(8)
                        st.end()
                        if not normed:
                            assert done[0] == NQ // 2
                            st2.end()

        def phase_out(name, sides, nk, bias, residual):
            s_mm, s_free, s_b, s_ch, s_xh, s_xl, s_wh, s_wl = (sem(f"{name}_" + x) for x in (
                "mm", "free", "bias", "chunk", "xhi", "xlo", "whi", "wlo"))
            s_r = [sem(f"{name}_res{c}") for c in range(NC)]
            s0 = take(NC)
            brow = bigC[0:P, NT * D:NT * D + D]
            rv = ptile(residual)
            w_hi = [ring_part.rearrange("p (k n) -> p k n", k=nk)
                    for ring_part in (stage_r[1][:, 0:nk * CW], stage_r[2][:, 0:nk * CW])]
            blocks_of = [(side, k) for side in sides for k in range(side[3])]
            with nc.Block() as block:
                @block.sync
                def _(sp):
                    sp.dma_start(brow, row_bc(bias, D)).then_inc(s_b, 16)
                    for c in range(NC):
                        sp.dma_start(tokC[:, :, c * CW:(c + 1) * CW], rv[:, :, c * CW:(c + 1) * CW]).then_inc(s_r[c], 16)
                    load_slots(sp, s0 + NC + 2)

                @block.tensor
                def _(pe):
                    pe.sem_inc(s_free, 4)
                    with pe.Fori(0, NC // 2) as tt:
                        for i in range(2):
                            c = tt * 2 + i
                            pe.wait_ge(s_wl, c + 1)
                            w = w_hi[(s0 + i) % 2], ring_k((s0 + i) % 2, nk, CW, ring_r)
                            for t in range(NT):
                                u = i * NT + t
                                pe.wait_ge(s_xl, (t + 1) * len(sides))
                                pe.wait_ge(s_free, tt * 2 * NT + u + 1)
                                at = slice(t * P, (t + 1) * P)
                                three_products(bank[u % 4][0:P, 0:CW], [
                                    ((side[2][:, k, at], side[1][:, k, at]), (w[0][:, kk], w[1][:, kk]))
                                    for kk, (side, k) in enumerate(blocks_of)]).then_inc(s_mm, 1)

                @block.scalar
                def _(act):
                    def rounded_w(c):
                        w_wait(act, s0 + c)
                        nc.scalar.copy(w_hi[(s0 + c) % 2], ring_k((s0 + c) % 2, nk, CW)).then_inc(s_wh, 1)

                    rounded_w(0)
                    for t in range(NT):
                        at = slice(t * P, (t + 1) * P)
                        for x, _, hi, _ in sides:
                            nc.scalar.copy(hi[:, :, at], x[:, :, at]).then_inc(s_xh, 1)
                    for c in range(1, NC):
                        rounded_w(c)

                @block.vector
                def _(dve):
                    def rest_of_w(c):
                        dve.wait_ge(s_wh, c + 1)
                        nc.vector.tensor_tensor(ring_k((s0 + c) % 2, nk, CW, ring_r), ring_k((s0 + c) % 2, nk, CW),
                                                w_hi[(s0 + c) % 2].bitcast(F32), ALU.subtract).then_inc(s_wl, 1)

                    rest_of_w(0)
                    for t in range(NT):
                        at = slice(t * P, (t + 1) * P)
                        for i, (x, lo, hi, _) in enumerate(sides):
                            dve.wait_ge(s_xh, t * len(sides) + i + 1)
                            nc.vector.tensor_tensor(lo[:, :, at], x[:, :, at], hi[:, :, at].bitcast(F32),
                                                    ALU.subtract).then_inc(s_xl, 1)
                    dve.wait_ge(s_b, 16)
                    for c in range(NC):
                        dve.wait_ge(s_r[c], 16)
                        for t in range(NT):
                            part = tokC[:, t, c * CW:(c + 1) * CW]
                            dve.wait_ge(s_mm, c * NT + t + 1)
                            if t == NT - 1:
                                dve.sem_inc(w_used, 1)
                            nc.vector.tensor_tensor(part, bank[(c * NT + t) % 4][0:P, 0:CW], part, ALU.add
                                                    ).then_inc(s_free, 1)
                            if t == NT // 2 and c < NC - 1:
                                rest_of_w(c + 1)
                        chunk = tokC[:, :, c * CW:(c + 1) * CW]
                        dve.wait_ge(s_free, 4 + (c + 1) * NT)
                        nc.vector.tensor_tensor(chunk, chunk, brow[:, c * CW:(c + 1) * CW]
                                                .rearrange("p (o n) -> p o n", o=1).to_broadcast([P, NT, CW]), ALU.add)

        def phase_up(name, weights, bias_at):
            s_mm, s_ev = sem(f"{name}_mm"), sem(f"{name}_gelu")
            s0 = take(2) if weights is None else 0
            with nc.Block() as block:
                if weights is None:
                    @block.sync
                    def _(sp):
                        load_slots(sp, s0 + 4)

                @block.tensor
                def _(pe):
                    for m in range(4):
                        if weights is None:
                            w_wait(pe, s0 + m // 2)
                            w = ring_k((s0 + m // 2) % 2, KD, CW)[:, :, (m % 2) * 128:(m % 2 + 1) * 128]
                        else:
                            w = weights(m)
                        for ch, (a, wd) in enumerate(FCH):
                            if m:
                                pe.wait_ge(s_ev, 3 * m + ch - 2)
                            for k in range(KD):
                                x = nc.tensor.matmul(bank[4 + ch][:, 0:wd], w[:, k, :], featA[:, k, a:a + wd],
                                                     start=(k == 0), stop=(k == KD - 1))
                            x.then_inc(s_mm, 1)
                        if weights is None and m % 2:
                            pe.wait_ge(s_mm, 3 * m + 3)
                            pe.sem_inc(w_used, 1)

                @block.scalar
                def _(act):
                    for m in range(4):
                        for ch, (a, wd) in enumerate(FCH):
                            act.wait_ge(s_mm, 3 * m + ch + 1)
                            nc.scalar.activation(featB[:, m, a:a + wd], bank[4 + ch][:, 0:wd], ACT.Gelu,
                                                 bias=bcol[:, bias_at + m:bias_at + m + 1]).then_inc(s_ev, 1)

        def phase_down(name, weights, bias, dram=None):
            s_mm, s_free, s_b, s_ch, s_st = (sem(f"{name}_" + x) for x in ("mm", "free", "bias", "chunk", "stored"))
            s0 = take(2) if weights is None else 0
            brow = stage3[0:P, 0:D]
            with nc.Block() as block:
                @block.sync
                def _(sp):
                    sp.dma_start(brow, row_bc(bias, D)).then_inc(s_b, 16)
                    if weights is None:
                        load_slots(sp, s0 + 4)
                    if dram is not None:
                        for c in range(2):
                            sp.wait_ge(s_ch, c + 1)
                            sp.dma_start(ptile(dram)[:, :, c * 512:(c + 1) * 512],
                                         tokC[:, :, c * 512:(c + 1) * 512]).then_inc(s_st, 16)
                        sp.wait_ge(s_st, 32)

                @block.tensor
                def _(pe):
                    for c in range(2):
                        if weights is None:
                            w_wait(pe, s0 + c)
                            w = ring_k((s0 + c) % 2, 4, 512)
                        else:
                            w = weights(c)
                        for t in range(NT):
                            u = c * NT + t
                            if u >= 4:
                                pe.wait_ge(s_free, u - 3)
                            for k in range(4):
                                m = nc.tensor.matmul(bank[u % 4][0:P, :], featB[:, k, t * P:(t + 1) * P], w[:, k, :],
                                                     start=(k == 0), stop=(k == 3))
                            m.then_inc(s_mm, 1)
                        if weights is None:
                            pe.wait_ge(s_mm, c * NT + NT)
                            pe.sem_inc(w_used, 1)

                @block.vector
                def _(dve):
                    dve.wait_ge(s_b, 16)
                    for c in range(2):
                        for t in range(NT):
                            u = c * NT + t
                            part = tokC[:, t, c * 512:(c + 1) * 512]
                            dve.wait_ge(s_mm, u + 1)
                            nc.vector.tensor_tensor(part, bank[u % 4][0:P, :], part, ALU.add).then_inc(s_free, 1)
                        dve.wait_ge(s_free, c * NT + NT)
                        part = tokC[:, :, c * 512:(c + 1) * 512]
                        nc.vector.tensor_tensor(part, part, brow[:, c * 512:(c + 1) * 512]
                                                .rearrange("p (o n) -> p o n", o=1).to_broadcast([P, NT, 512]),
                                                ALU.add).then_inc(s_ch, 1)

        def phase_route():
            s_ld, s_lg, s_own, s_e, s_ex, s_ct, s_cs, s_bm, s_be, s_r = (sem("rt_" + x) for x in (
                "in", "logits", "own", "comb", "exp", "turned", "turnedevac", "b2", "b2evac", "rows"))
            wr = stage1[:, 0:KD * NEXP].rearrange("p (k n) -> p k n", k=KD)
            b2 = stage2[0:NEXP, 0:D]
            br = stage3[0:P, 0:NEXP]
            combT = stage4[0:NEXP, 0:N]
            work = stage3[0:P, 256:256 + 8 * NT * NEXP].rearrange("p (a t n) -> p a t n", a=8, t=NT)
            lg, ex, eq = work[:, 0], work[:, 1], work[:, 2]
            mx, sm, ws = (small[0:P, 64 + 16 * i:64 + 16 * i + NT] for i in range(3))
            top = work[:, 3, :, 0:8]
            top_at = work[:, 4, :, 0:8].bitcast(U32)
            atf = work[:, 5, :, 0:8]
            col = lambda v, n: v.rearrange("p (t o) -> p t o", o=1).to_broadcast([P, NT, n])
            with nc.Block() as block:
                @block.sync
                def _(sp):
                    sp.dma_start(wr, A["L0_ffn_Wr"].rearrange("(k p) n -> p k n", p=128)).then_inc(s_ld, 16)
                    sp.dma_start(b2, A["L0_ffn_b2"]).then_inc(s_r, 16)
                    sp.dma_start(br, row_bc(A["L0_ffn_br"], NEXP)).then_inc(s_r, 16)

                @block.tensor
                def _(pe):
                    pe.wait_ge(s_ld, 16)
                    for t in range(NT):
                        for k in range(KD):
                            m = nc.tensor.matmul(bank[0][0:P, t * NEXP:(t + 1) * NEXP], featA[:, k, t * P:(t + 1) * P],
                                                 wr[:, k, :], start=(k == 0), stop=(k == KD - 1))
                    m.then_inc(s_lg, 1)
                    pe.wait_ge(s_e, 1)
                    for t in range(NT):
                        m = nc.tensor.transpose(bank[4 + t // 4][0:NEXP, (t % 4) * P:(t % 4 + 1) * P], comb[:, t, :],
                                                ident[0:P, 0:P])
                    m.then_inc(s_ct, 1)
                    pe.wait_ge(s_cs, 3)
                    pe.wait_ge(s_r, 32)
                    for u in range(2 * NT):
                        if u >= 4:
                            pe.wait_ge(s_be, u - 3)
                        nc.tensor.matmul(bank[u % 4][0:P, :], combT[:, (u // 2) * P:(u // 2 + 1) * P],
                                         b2[:, (u % 2) * 512:(u % 2 + 1) * 512], start=True,
                                         stop=True).then_inc(s_bm, 1)

                @block.scalar
                def _(act):
                    act.wait_ge(s_ex, 1)
                    nc.scalar.activation(ex, lg, ACT.Exp).then_inc(s_ex, 1)
                    act.wait_ge(s_ct, 1)
                    for ch, (a, w) in enumerate(FCH):
                        nc.scalar.copy(combT[:, a:a + w], bank[4 + ch][0:NEXP, 0:w]).then_inc(s_cs, 1)

                @block.vector
                def _(dve):
                    st = Steps(dve, s_own)
                    dve.wait_ge(s_r, 32)
                    dve.wait_ge(s_lg, 1)
                    st.link(nc.vector.tensor_tensor(lg, bank[0][0:P, 0:NT * NEXP].rearrange("p (t n) -> p t n", t=NT),
                                                    br.rearrange("p (o n) -> p o n", o=1).to_broadcast([P, NT, NEXP]),
                                                    ALU.add))
                    st.link(nc.vector.tensor_reduce(mx, lg, AX.X, ALU.max))
                    nc.vector.tensor_tensor(lg, lg, col(mx, NEXP), ALU.subtract).then_inc(s_ex, 1)
                    dve.wait_ge(s_ex, 2)
                    st.link(nc.vector.tensor_reduce(sm, ex, AX.X, ALU.add))
                    st.link(nc.vector.reciprocal(sm, sm))
                    st.link(nc.vector.tensor_tensor(ex, ex, col(sm, NEXP), ALU.mult))
                    for t in range(NT):
                        last = nc.vector.max(top[:, t, :], ex[:, t, :])
                    st.link(last)
                    for t in range(NT):
                        last = nc.vector.max_index(top_at[:, t, :], top[:, t, :], ex[:, t, :])
                    st.link(last)
                    st.link(nc.vector.tensor_copy(atf, top_at))
                    st.link(nc.vector.tensor_reduce(ws, top[:, :, 0:2], AX.X, ALU.add))
                    st.link(nc.vector.tensor_scalar(ws, ws, 1e-9, None, ALU.max))
                    st.link(nc.vector.reciprocal(ws, ws))
                    st.link(nc.vector.tensor_tensor(top[:, :, 0:2], top[:, :, 0:2], col(ws, 2), ALU.mult))
                    iota = iota16[:, 0:NEXP].rearrange("p (o n) -> p o n", o=1).to_broadcast([P, NT, NEXP])
                    for i in range(2):
                        st.link(nc.vector.tensor_tensor(eq, iota, atf[:, :, i:i + 1].to_broadcast([P, NT, NEXP]),
                                                        ALU.is_equal))
                        st.link(nc.vector.tensor_tensor(eq if i else comb, eq,
                                                        top[:, :, i:i + 1].to_broadcast([P, NT, NEXP]), ALU.mult))
                    nc.vector.tensor_tensor(comb, comb, eq, ALU.add).then_inc(s_e, 1)
                    for u in range(2 * NT):
                        dve.wait_ge(s_bm, u + 1)
                        part = tokB[:, u // 2, (u % 2) * 512:(u % 2 + 1) * 512]
                        nc.vector.tensor_tensor(part, bank[u % 4][0:P, :], part, ALU.add).then_inc(s_be, 1)

        def phase_moe():
            s_f, s_ge, s_tm, s_ae, s_xh, s_xl, s_wh, s_wl, s_hh, s_hl = (sem("moe_" + x) for x in (
                "up", "gelu", "down", "added", "xhi", "xlo", "whi", "wlo", "hhi", "hlo"))
            s0 = take(2 * NEXP)
            x_hi = bigC_r[:, 0:KD * N].rearrange("p (k n) -> p k n", k=KD)
            ht = stage1[:, 0:2 * N].rearrange("p (m n) -> p m n", m=2)
            ht_lo, ht_hi = (stage_r[i][:, 0:2 * N].rearrange("p (m n) -> p m n", m=2) for i in range(2))
            w_hi = [stage_r[2][:, 0:KD * EH].rearrange("p (k n) -> p k n", k=KD),
                    stage_r[3][:, 0:2 * D].rearrange("p (k n) -> p k n", k=2)]
            w_at, w_lo = ([ring_k(s0 % 2, KD, EH, x), ring_k((s0 + 1) % 2, 2, D, x)] for x in (ring, ring_r))
            units = [(m, ch, a, w) for m in range(2) for ch, (a, w) in enumerate(RCH)]
            as32 = lambda v: v.bitcast(F32)
            with nc.Block() as block:
                @block.sync
                def _(sp):
                    load_slots(sp, s0 + 2 * NEXP + 2)

                @block.tensor
                def _(pe):
                    with pe.Fori(0, NEXP) as e:
                        pe.wait_ge(s_wl, e * 2 + 1)
                        for j, (m, ch, a, wd) in enumerate(units):
                            pe.wait_ge(s_ge, e * 6 + j + 1)
                            pe.wait_ge(s_xl, ch + 1)
                            three_products(bank[4 + ch][:, 0:wd], [
                                ((w_hi[0][:, k, m * 128:(m + 1) * 128], w_lo[0][:, k, m * 128:(m + 1) * 128]),
                                 (x_hi[:, k, a:a + wd], featA_r[:, k, a:a + wd])) for k in range(KD)]).then_inc(s_f, 1)
                        pe.wait_ge(s_wl, e * 2 + 2)
                        for t in range(NT):
                            pe.wait_ge(s_hl, e * 6 + 4 + sum(a < (t + 1) * P for a, _ in RCH[1:]))
                            for n in range(2):
                                u = t * 2 + n
                                pe.wait_ge(s_ae, e * 2 * NT + u + 1)
                                three_products(bank[u % 4][0:P, :], [
                                    ((ht_hi[:, k, t * P:(t + 1) * P], ht_lo[:, k, t * P:(t + 1) * P]),
                                     (w_hi[1][:, k, n * 512:(n + 1) * 512], w_lo[1][:, k, n * 512:(n + 1) * 512]))
                                    for k in range(2)]).then_inc(s_tm, 1)

                @block.scalar
                def _(act):
                    act.sem_inc(s_ge, 3)
                    for a, wd in RCH:
                        nc.scalar.copy(x_hi[:, :, a:a + wd], featA[:, :, a:a + wd]).then_inc(s_xh, 1)
                    with act.Fori(0, NEXP) as e:
                        for i in range(2):
                            w_wait(act, s0 + i, e, 16)
                            nc.scalar.copy(w_hi[i], w_at[i]).then_inc(s_wh, 1)
                        for j, (m, ch, a, wd) in enumerate(units):
                            act.wait_ge(s_f, e * 6 + j + 1)
                            hold(act)
                            nc.scalar.activation(ht[:, m, a:a + wd], bank[4 + ch][:, 0:wd], ACT.Gelu,
                                                 bias=bcol[:, ds(e * 2 + 12 + m, 1)]).then_inc(s_ge, 1)
                            act.wait_ge(s_ge, e * 6 + j + 4)
                            nc.scalar.copy(ht_hi[:, m, a:a + wd], ht[:, m, a:a + wd]).then_inc(s_hh, 1)

                @block.vector
                def _(dve):
                    dve.sem_inc(s_ae, 4)
                    flat = comb.rearrange("p t n -> p (t n)")

                    def rest_of_w(i, e):
                        dve.wait_ge(s_wh, e * 2 + i + 1)
                        nc.vector.tensor_tensor(w_lo[i], w_at[i], as32(w_hi[i]), ALU.subtract).then_inc(s_wl, 1)

                    def expert(e, more):
                        rest_of_w(1, e)
                        for j, (m, ch, a, wd) in enumerate(units):
                            dve.wait_ge(s_hh, e * 6 + j + 1)
                            nc.vector.tensor_tensor(ht_lo[:, m, a:a + wd], ht[:, m, a:a + wd], as32(ht_hi[:, m, a:a + wd]),
                                                    ALU.subtract).then_inc(s_hl, 1)
                        dve.sem_inc(w_used, 1)
                        for u in range(2 * NT):
                            t, n = divmod(u, 2)
                            part = tokB[:, t, n * 512:(n + 1) * 512]
                            dve.wait_ge(s_tm, e * 2 * NT + u + 1)
                            if u == 2 * NT - 1:
                                dve.sem_inc(w_used, 1)
                            nc.vector.scalar_tensor_tensor(out=part, in0=bank[u % 4][0:P, :],
                                                           scalar=flat[:, ds(e + t * NEXP, 1)], in1=part,
                                                           op0=ALU.mult, op1=ALU.add).then_inc(s_ae, 1)
                            if more and u == 14:
                                rest_of_w(0, e + 1)

                    for ch, (a, wd) in enumerate(RCH):
                        dve.wait_ge(s_xh, ch + 1)
                        nc.vector.tensor_tensor(featA_r[:, :, a:a + wd], featA[:, :, a:a + wd],
                                                as32(x_hi[:, :, a:a + wd]), ALU.subtract).then_inc(s_xl, 1)
                    rest_of_w(0, 0)
                    with dve.Fori(0, NEXP - 1) as e:
                        expert(e, True)
                    expert(NEXP - 1, False)

        xlr = bigC[0:P, 0:NT * 2 * HID].rearrange("p (t n) -> p t n", t=NT)
        self_score = small[0:P, 208:208 + NT * GH].rearrange("p (t h) -> p t h", t=NT)

        def phase_gat_in():
            (s_own, s_rq, s_sq, s_w, s_mm, s_ev, s_tr, s_te, s_lr, s_le, s_st, s_at) = (sem("gi_" + x) for x in (
                "own", "sumsq", "sqrt", "scaled", "mm", "evac", "turned", "turnedevac", "lr", "lrevac", "stored", "att"))
            s0 = take(2)
            rq = small[0:P, 160:160 + NT]
            xd = stage1[0:P, :].rearrange("p (t n) -> p t n", t=NT)
            xdT = stage2[:, 0:2 * N].rearrange("p (k n) -> p k n", k=2)
            att = attrow[:, :]
            zs = bigC[0:P, 2 * D * 3:2 * D * 3 + NT * HID]
            with nc.Block() as block:
                @block.sync
                def _(sp):
                    sp.dma_start(att, A["L1_gnn_att_row"].rearrange("(o n) -> o n", o=1)
                                 .to_broadcast([P, HID])).then_inc(s_at, 16)
                    load_slots(sp, s0 + 2)
                    sp.wait_ge(s_le, NT)
                    sp.dma_start(ptile(XL), xlr[:, :, 0:HID]).then_inc(s_st, 16)
                    sp.dma_start(ptile(XRD), xlr[:, :, HID:2 * HID]).then_inc(s_st, 16)
                    load_slots(sp, s0 + 4)
                    sp.wait_ge(s_st, 32)

                @block.vector
                def _(dve):
                    st = Steps(dve, s_own)
                    nc.vector.tensor_scalar(rq, rq, 1.0 / D, 1e-6, ALU.mult, ALU.add).then_inc(s_rq, 1)
                    w_wait(dve, s0)
                    w = ring_k(s0 % 2, KD, CW)
                    gains = bcol[:, 48:48 + KD].rearrange("p (k o) -> p k o", o=1).to_broadcast([128, KD, CW])
                    nc.vector.tensor_tensor(w, w, gains, ALU.mult).then_inc(s_w, 1)
                    dve.wait_ge(s_sq, 1)
                    nc.vector.reciprocal(rq, rq).then_inc(s_rq, 1)
                    for t in range(NT):
                        dve.wait_ge(s_tr, t + 1)
                        nc.vector.tensor_copy(xdT[:, :, t * P:(t + 1) * P],
                                              bank[4 + t % 2][:, 0:2 * P].rearrange("p (k n) -> p k n", k=2)
                                              ).then_inc(s_te, 1)
                    dve.wait_ge(s_le, NT)
                    dve.wait_ge(s_at, 16)
                    zt = zs.rearrange("p (t n) -> p t n", t=NT)
                    st.link(nc.vector.tensor_tensor(zt, xlr[:, :, 0:HID], xlr[:, :, HID:2 * HID], ALU.add))
                    st.link(nc.vector.scalar_tensor_tensor(out=zs, in0=zs, scalar=0.2, in1=zs, op0=ALU.mult,
                                                           op1=ALU.max))
                    st.link(nc.vector.tensor_tensor(zt, zt, att.rearrange("p (o n) -> p o n", o=1)
                                                    .to_broadcast([P, NT, HID]), ALU.mult))
                    nc.vector.tensor_reduce(self_score.rearrange("p t h -> p (t h)"),
                                            zs.rearrange("p (h n) -> p h n", n=GD), AX.X, ALU.add)

                @block.scalar
                def _(act):
                    act.wait_ge(s_rq, 1)
                    nc.scalar.sqrt(rq, rq).then_inc(s_sq, 1)
                    act.wait_ge(s_rq, 2)
                    for t in range(NT):
                        act.wait_ge(s_mm, t + 1)
                        nc.scalar.activation(xd[:, t, :], bank[t % 4][0:P, 0:CW], ACT.Copy,
                                             scale=rq[:, t:t + 1]).then_inc(s_ev, 1)
                    for t in range(NT):
                        act.wait_ge(s_lr, t + 1)
                        nc.scalar.copy(xlr[:, t, :], bank[t % 4][0:P, :]).then_inc(s_le, 1)

                @block.tensor
                def _(pe):
                    pe.wait_ge(s_w, 1)
                    w = ring_k(s0 % 2, KD, CW)
                    for t in range(NT):
                        if t >= 4:
                            pe.wait_ge(s_ev, t - 3)
                        for k in range(KD):
                            m = nc.tensor.matmul(bank[t % 4][0:P, 0:CW], featA[:, k, t * P:(t + 1) * P], w[:, k, :],
                                                 start=(k == 0), stop=(k == KD - 1))
                        m.then_inc(s_mm, 1)
                    pe.wait_ge(s_mm, NT)
                    pe.sem_inc(w_used, 1)
                    for t in range(NT):
                        pe.wait_ge(s_ev, t + 1)
                        if t >= 2:
                            pe.wait_ge(s_te, t - 1)
                        for k in range(2):
                            m = nc.tensor.transpose(bank[4 + t % 2][:, k * P:(k + 1) * P], xd[:, t, k * 128:(k + 1) * 128],
                                                    ident[0:P, 0:P])
                        m.then_inc(s_tr, 1)
                    w_wait(pe, s0 + 1)
                    w = ring_k((s0 + 1) % 2, 4, HID)
                    for t in range(NT):
                        pe.wait_ge(s_te, t + 1)
                        if t >= 4:
                            pe.wait_ge(s_le, t - 3)
                        for side in range(2):
                            for k in range(2):
                                m = nc.tensor.matmul(bank[t % 4][0:P, side * HID:(side + 1) * HID],
                                                     xdT[:, k, t * P:(t + 1) * P], w[:, 2 * side + k, :],
                                                     start=(k == 0), stop=(k == 1))
                        m.then_inc(s_lr, 1)
                    pe.wait_ge(s_lr, NT)
                    pe.sem_inc(w_used, 1)

        def phase_gat():
            (s_rl, s_ru, s_b1, s_ng, s_sl, s_sps, s_spt, s_spc, s_bc, s_tm, s_in, s_n1) = (sem("g1_" + x) for x in (
                "row", "rowused", "bcast", "neg", "slice", "parts", "partsT", "partsTcopy", "scores", "max", "init",
                "own"))
            (s_m, s_b2, s_oht, s_oh, s_me, s_x, s_p, s_r, s_ag, s_idx, s_dn, s_n2, s_self, s_end, s_n3, s_gt) = (
                sem("g2_" + x) for x in (
                    "max", "bcast", "onehotT", "onehot", "maxback", "shifted", "p", "rhs", "agg", "idx", "tile", "own",
                    "self", "last", "own_tile", "turned"))
            s_g = [sem(f"g2_gather{h}") for h in range(2)]
            s_m2, s_xl, s_rx = sem("g2_selfp"), sem("g2_xl"), sem("g2_extrarow")
            zero = stage4[0:P, 0:P]
            pos = [0]

            def inC(n, parts=P):
                a = pos[0]
                pos[0] += n
                assert pos[0] <= NT * N, pos[0]
                return bigC[0:parts, a:a + n]

            xg = [x[0:P, 0:HB * HID].rearrange("p (g n) -> p g n", g=HB) for x in (stage1, stage2)]
            xs = stage1[0:P, 1024:1024 + SUB * GH].rearrange("p (g n) -> p g n", g=SUB)
            away = stage1[0:P, 1056:1056 + SUB]
            m_ = stage1[0:P, 1064:1064 + GH + 1]
            pself = stage1[0:P, 1072:1072 + GH]
            rden = stage1[0:P, 1080:1080 + GH]
            minus_ids = stage1[0:P, 1090:1090 + NT]
            idx = edge_ix[:, 0, :, :]
            neg = stage2[0:P, 1024:1024 + BE]
            oht = neg
            junk = stage3[0:P, 0:1000].rearrange("p (h n) -> p h n", h=2)
            oh = stage3[0:P, 1000:2000].rearrange("p (g n) -> p g n", g=SUB)
            spt = stage3[0:12, 2000:2500].bitcast(BF16)
            rhs = inC(SUB * (HID + GH)).rearrange("p (g n) -> p g n", g=SUB)
            rself = inC(HID + GH)
            gout = inC(NT * HID).rearrange("p (t n) -> p t n", t=NT)
            xl_own = inC(NT * HID).rearrange("p (t n) -> p t n", t=NT)
            inA = featA[0:P, :, :].rearrange("p k n -> p (k n)")
            parts_all = inA[:, 0:(NB + 1) * SUB * 6].bitcast(BF16).rearrange("p (j n) -> p j n", n=12)
            rest = inA[:, 2048:2048 + 2 * NB * SUB * GH].rearrange("p (i j n) -> p i j n", i=2, n=GH)
            row = inA[0:1, 4608:4608 + BE // 2].bitcast(F16)
            one16 = inA[0:1, 5632:5632 + 64].bitcast(F16)[:, 0:P]
            psl = inA[:, 5696:5696 + SUB * 6].bitcast(BF16).rearrange("p (g n) -> p g n", g=SUB)
            sel = inA[0:12, 5760:5760 + GH * P // 2].bitcast(BF16).rearrange("p (h n) -> p h n", h=GH)
            t12 = small[0:12, 0:GH]
            by_head = lambda v: v.rearrange("p (h n) -> p h n", n=GD)
            ov = lambda v, n: v.rearrange("p (h o) -> p h o", o=1).to_broadcast([P, v.shape[1], n])
            sc = scores[:, :].rearrange("p (j n) -> p j n", n=GH)
            tb = bank[2][0:12, :].bitcast(BF16).rearrange("p (g n) -> p g n", g=SUB)
            meb = bank[2][0:P, 0:5 * SUB].rearrange("p (g n) -> p g n", g=SUB)
            accb = bank[3][0:P, 0:HID + GH]

            with nc.Block() as block:
                @block.sync
                def _(sp):
                    sp.dma_start(xl_own, ptile(XL)).then_inc(s_xl, 16)
                    sp.dma_start(DR[NB:NB + 1, :], iota16[0:1, 0:BE]).then_inc(s_rx, 16)
                    sp.wait_ge(s_rx, 16)
                    sp.sem_inc(s_ru, 1)
                    with sp.Fori(0, NT) as d:
                        lo, cnt, base = batches(sp, d)
                        for half in range(2):
                            with sp.Fori(0, cnt + 1) as r:
                                at = (base + d) * 2 + half * (cnt + 1) + r
                                sp.wait_ge(s_ru, at + 1)
                                sp.dma_start(row[:, :], DR[ds(batch(lo, r, 1), 1), :]).then_inc(s_rl, 16)

                @block.gpsimd
                def _(pool):
                    with pool.Fori(0, NT) as d:
                        lo, cnt, base = batches(pool, d)
                        with pool.Fori(0, cnt) as r:
                            for h in range(2):
                                pool.wait_ge(s_r, (base + r) * 2 + h + 1)
                                hold(pool)
                                nc.gpsimd.tensor_copy(idx[:, h, :], src_i[:, ds(batch(lo, r) * SUB + h * HB, HB)]
                                                      ).then_inc(s_idx, 1)
                                pool.wait_ge(s_idx, (base + r) * 2 + h + 1)
                                hold(pool)
                                for g in range(HB):
                                    nc.gpsimd.indirect_dma_start(
                                        out=xg[h][:, g, :], out_offset=None, in_=XL,
                                        in_offset=bass.IndirectOffsetOnAxis(ap=idx[:, h, g:g + 1].bitcast(U32), axis=0),
                                        ).then_inc(s_g[h], 16)

                @block.tensor
                def _(pe):
                    def broadcast_row(at, s_out, n_out):
                        pe.wait_ge(s_rl, at * 16 + 16)
                        hold(pe)
                        for h in range(2):
                            m = nc.tensor.matmul(bank[h][0:P, 0:500], one16[:, :], row[:, h * 500:(h + 1) * 500],
                                                 start=True, stop=True)
                        m.then_inc(s_out, 1)
                        pe.wait_ge(s_out, n_out)
                        pe.sem_inc(s_ru, 1)

                    def turn_parts(step):
                        pe.wait_ge(s_sps, step + 1)
                        pe.wait_ge(s_spc, step + 1)
                        hold(pe)
                        for g in range(SUB):
                            m = nc.tensor.transpose(tb[:, g, 0:P], psl[:, g, :], ident16[0:P, 0:P])
                        m.then_inc(s_spt, 1)

                    pe.sem_inc(s_bc, 8)
                    pe.wait_ge(s_in, 1)
                    with pe.Fori(0, NT) as d:
                        lo, cnt, base = batches(pe, d)
                        pe.wait_ge(s_dn, d + 1)
                        hold(pe)
                        broadcast_row((base + d) * 2, s_b1, base + d + 1)
                        turn_parts(base + d)
                        hold(pe)
                        with pe.Fori(0, cnt) as r:
                            step = base + r
                            pe.wait_ge(s_spc, step + d + 2)
                            for h in range(2):
                                if h == 1:
                                    pe.wait_ge(s_ng, (step + d) * 2 + 2)
                                    hold(pe)
                                    broadcast_row((base + d) * 2 + r + 1, s_b1, step + d + 2)
                                    turn_parts(step + d + 1)
                                for hd in range(GH):
                                    u = h * GH + hd
                                    pe.wait_ge(s_tm, step * 8 + u + 5)
                                    hold(pe)
                                    nc.tensor.matmul(bank[4 + u % 4][0:P, 0:500], sel[:, hd, :],
                                                     spt[:, h * 500:(h + 1) * 500], start=True, stop=True
                                                     ).then_inc(s_bc, 1)
                        pe.wait_ge(s_ng, (base + d + cnt) * 2 + 2)
                        pe.wait_ge(s_spc, base + d + cnt + 2)
                        hold(pe)
                        broadcast_row((base + d) * 2 + cnt + 1, s_b2, base + d + 1)
                        pe.wait_ge(s_self, d + 1)
                        nc.tensor.matmul(accb, ident[0:P, 0:P], rself, start=True, stop=False, skip_group_check=True)
                        with pe.Fori(0, cnt) as r:
                            step = base + r
                            pe.wait_ge(s_oht, step + d + 1)
                            pe.wait_ge(s_x, step + 1)
                            for g in range(SUB):
                                m = nc.tensor.matmul(meb[:, g, :], oht[:, g:BE:SUB], m_, start=True, stop=True)
                            m.then_inc(s_me, 1)
                            broadcast_row((base + d) * 2 + cnt + r + 2, s_b2, step + d + 2)
                            for h in range(2):
                                pe.wait_ge(s_r, step * 2 + h + 3)
                                for g in range(h * HB, h * HB + HB):
                                    m = nc.tensor.matmul(accb, oh[:, g, :], rhs[:, g, :], start=False, stop=False,
                                                         skip_group_check=True)
                            m.then_inc(s_ag, 1)
                        pe.wait_ge(s_self, d + 1)
                        nc.tensor.matmul(accb, zero, rself, start=False, stop=True, skip_group_check=True
                                         ).then_inc(s_end, 1)
                    pe.wait_ge(s_dn, NT + 1)
                    for t in range(NT):
                        for k in range(2):
                            c = t * 2 + k
                            m = nc.tensor.transpose(bank[3 + c // 4][:, (c % 4) * P:(c % 4 + 1) * P],
                                                    gout[:, t, k * 128:(k + 1) * 128], ident[0:P, 0:P])
                    m.then_inc(s_gt, 1)

                @block.scalar
                def _(act):
                    act.sem_inc(s_spc, 1)
                    act.wait_ge(s_sl, 1)
                    with act.Fori(0, NT) as d:
                        lo, cnt, base = batches(act, d)
                        with act.Fori(0, cnt + 1) as r:
                            step = base + d + r
                            nc.scalar.copy(psl[:, :, :], parts_all[:, ds(batch(lo, r, 1) * SUB, SUB), :]
                                           ).then_inc(s_sps, 1)

                            def away_half(h):
                                act.wait_ge(s_b1, step + 1)
                                act.wait_ge(s_tm, (base + r) * 8 + 4 + 4 * h)
                                hold(act)
                                nc.scalar.activation(neg[:, h * 500:(h + 1) * 500], bank[h][0:P, 0:500], ACT.Abs,
                                                     scale=BIG, bias=minus_ids[:, ds(d, 1)]).then_inc(s_ng, 1)

                            away_half(0)
                            act.wait_ge(s_spt, step + 1)
                            act.wait_ge(s_bc, (base + r) * 8 + 8)
                            nc.scalar.copy(spt.rearrange("p (n g) -> p g n", g=SUB), tb[:, :, 0:P]).then_inc(s_spc, 1)
                            away_half(1)
                        act.wait_ge(s_m, d + 1)
                        nc.scalar.activation(rself[:, HID:HID + GH], pself, ACT.Exp).then_inc(s_m2, 1)
                        with act.Fori(0, cnt) as r:
                            step = base + r
                            act.wait_ge(s_x, step + 2)
                            nc.scalar.activation(rhs[:, :, HID:HID + GH], xs, ACT.Exp).then_inc(s_p, 1)
                    act.wait_ge(s_gt, 1)
                    for t in range(NT):
                        c = t * 2
                        nc.scalar.copy(gatT[:, :, t * P:(t + 1) * P],
                                       bank[3 + c // 4][:, (c % 4) * P:(c % 4 + 2) * P]
                                       .rearrange("p (k n) -> p k n", k=2))

                @block.vector
                def _(dve):
                    st = Steps(dve, s_n1)
                    part = lambda i: parts_all[:, 0:NB * SUB, i * GH:(i + 1) * GH]
                    st.link(nc.vector.tensor_copy(part(0), sc))
                    st.link(nc.vector.tensor_tensor(rest[:, 0], sc, part(0), ALU.subtract))
                    st.link(nc.vector.tensor_copy(part(1), rest[:, 0]))
                    st.link(nc.vector.tensor_tensor(rest[:, 1], rest[:, 0], part(1), ALU.subtract))
                    st.link(nc.vector.tensor_copy(part(2), rest[:, 1]))
                    st.link(nc.vector.memset(parts_all[:, NB * SUB:(NB + 1) * SUB, :], 0.0))
                    nc.vector.sem_inc(s_sl, 1)
                    st.link(nc.vector.tensor_tensor(t12, ident[0:12, 0:4], ident[0:12, 4:8], ALU.add))
                    st.link(nc.vector.tensor_tensor(t12, t12, ident[0:12, 8:12], ALU.add))
                    st.link(nc.vector.tensor_copy(sel[:, :, :], t12.rearrange("p (h o) -> p h o", o=1)
                                                  .to_broadcast([12, GH, P])))
                    st.link(nc.vector.tensor_scalar(minus_ids, ids, -BIG, None, ALU.mult))
                    st.link(nc.vector.memset(one16[:, :], 1.0))
                    st.link(nc.vector.memset(zero, 0.0))
                    st.link(nc.vector.memset(m_, 1.0))
                    nc.vector.sem_inc(s_in, 1)
                    dve.sem_inc(s_x, 1)
                    dve.sem_inc(s_ag, 1)
                    dve.sem_inc(s_dn, 1)
                    dve.sem_inc(s_tm, 8)
                    dve.sem_inc(s_r, 2)
                    dve.wait_ge(s_xl, 16)
                    with dve.Fori(0, NT) as d:
                        lo, cnt, base = batches(dve, d)
                        so = Steps(dve, s_n3, d, 6)
                        id_d = ids[:, ds(d, 1)]

                        def onehot_t(step):
                            dve.wait_ge(s_b2, step + 1)
                            for h in range(2):
                                x = nc.vector.tensor_scalar(oht[:, h * 500:(h + 1) * 500], bank[h][0:P, 0:500], id_d,
                                                            None, ALU.is_equal)
                            x.then_inc(s_oht, 1)

                        dve.wait_ge(s_dn, d + 1)
                        so.link(nc.vector.tensor_copy(m_[:, 0:GH],
                                                      self_score[:, ds(d, 1), :].rearrange("p o h -> p (o h)")))
                        hold(dve)
                        with dve.Fori(0, cnt) as r:
                            step = base + r
                            for h in range(2):
                                for hd in range(GH):
                                    u = h * GH + hd
                                    dve.wait_ge(s_ng, (step + d) * 2 + h + 1)
                                    dve.wait_ge(s_bc, step * 8 + u + 9)
                                    dve.wait_ge(s_tm, step * 8 + u + 7)
                                    hold(dve)
                                    nc.vector.tensor_tensor_reduce(
                                        junk[:, u % 2, :], bank[4 + u % 4][0:P, 0:500], neg[:, h * 500:(h + 1) * 500],
                                        1.0, m_[:, hd:hd + 1], ALU.subtract, ALU.max, m_[:, hd:hd + 1]
                                    ).then_inc(s_tm, 1)
                        dve.wait_ge(s_tm, (base + cnt) * 8 + 8)
                        so.link(nc.vector.tensor_tensor(pself, self_score[:, ds(d, 1), :].rearrange("p o h -> p (o h)"),
                                                        m_[:, 0:GH], ALU.subtract))
                        nc.vector.sem_inc(s_m, 1)
                        dve.wait_ge(s_m2, d + 1)
                        so.link(nc.vector.tensor_tensor(by_head(rself[:, 0:HID]),
                                                        xl_own[:, ds(d, 1), :].rearrange("p o (h n) -> p (o h) n", n=GD),
                                                        ov(rself[:, HID:HID + GH], GD), ALU.mult))
                        nc.vector.sem_inc(s_self, 1)
                        onehot_t(base + d)
                        with dve.Fori(0, cnt) as r:
                            step = base + r
                            st = Steps(dve, s_n2, step, 2)
                            dve.wait_ge(s_ag, step + 1)
                            nc.vector.tensor_tensor(
                                oh, iota16[:, ds(d * P, P)].rearrange("p (o n) -> p o n", o=1).to_broadcast([P, SUB, P]),
                                dst_f[:, ds(batch(lo, r) * SUB, SUB)].rearrange("p (q o) -> p q o", o=1)
                                .to_broadcast([P, SUB, P]), ALU.is_equal)
                            dve.wait_ge(s_me, step + 1)
                            a3 = away.rearrange("p (g o) -> p g o", o=1)
                            st.link(nc.vector.tensor_tensor(xs, sc[:, ds(batch(lo, r) * SUB, SUB), :], meb[:, :, 0:GH],
                                                            ALU.subtract))
                            st.link(nc.vector.tensor_scalar(a3, meb[:, :, GH:GH + 1], 1.0, BIG, ALU.subtract, ALU.mult))
                            nc.vector.tensor_tensor(xs, xs, a3.to_broadcast([P, SUB, GH]), ALU.add).then_inc(s_x, 1)
                            st.end()
                            dve.wait_ge(s_p, step + 1)
                            for h in range(2):
                                dve.wait_ge(s_g[h], step * 64 + 64)
                                hs = slice(h * HB, h * HB + HB)
                                nc.vector.tensor_tensor(
                                    rhs[:, hs, 0:HID].rearrange("p g (h n) -> p g h n", n=GD),
                                    xg[h].rearrange("p g (h n) -> p g h n", n=GD),
                                    rhs[:, hs, HID:HID + GH].rearrange("p g (h o) -> p g h o", o=1)
                                    .to_broadcast([P, HB, GH, GD]), ALU.mult).then_inc(s_r, 1)
                            onehot_t(step + d + 1)
                        dve.wait_ge(s_oht, base + d + cnt + 1)
                        dve.wait_ge(s_end, d + 1)
                        so.link(nc.vector.tensor_scalar(rden, accb[:, HID:HID + GH], 1e-16, None, ALU.add))
                        so.link(nc.vector.reciprocal(rden, rden))
                        so.link(nc.vector.tensor_tensor(gout[:, ds(d, 1), :].rearrange("p o (h n) -> p (o h) n", h=GH),
                                                        by_head(accb[:, 0:HID]), ov(rden, GD), ALU.mult))
                        nc.vector.sem_inc(s_dn, 1)
                        so.end()

        w1T = bigB[:, 5120:5120 + KD * 512].rearrange("p (k n) -> p k n", k=KD)
        w2T = ring[:, :].rearrange("p i k n -> p (i k n)")[:, 0:4 * D].rearrange("p (k n) -> p k n", k=4)

        def phase_binarize():
            s_ab, s_sg, s_own, s_tr, s_ev = (sem("bw_" + x) for x in ("abs", "sign", "own", "turned", "evac"))
            s_trb = sem("bw_banks")
            s_ld = [sem(f"bw_in{i}") for i in range(2)]
            pieces = [(A["L1_ffn_w1"], j, D, w1T) for j in range(4)] + [(A["L1_ffn_w2"], j, 512, w2T) for j in range(8)]
            wn = [x[:, 0:D] for x in (stage1, stage2)]
            sg = stage3[:, 0:2 * D].rearrange("p (i n) -> p i n", i=2)
            def evac(dve, q):
                src, j, n, dst = pieces[q]
                for b in range(n // 512):
                    dve.wait_ge(s_trb, sum(p[2] // 512 for p in pieces[:q]) + b + 1)
                    nc.vector.tensor_copy(dst[:, 4 * b:4 * b + 4, j * 128:(j + 1) * 128],
                                          bank[2 * (q % 2) + b][:, :].rearrange("p (k n) -> p k n", k=4)
                                          ).then_inc(s_ev, 1)

            with nc.Block() as block:
                @block.sync
                def _(sp):
                    for q, (src, j, n, _) in enumerate(pieces):
                        if q >= 2:
                            sp.wait_ge(s_tr, q - 1)
                        sp.dma_start(wn[q % 2][:, 0:n], src[j * 128:(j + 1) * 128, :]).then_inc(s_ld[q % 2], 16)

                @block.scalar
                def _(act):
                    for q, (src, j, n, dst) in enumerate(pieces):
                        act.wait_ge(s_ld[q % 2], 16 * (q // 2) + 16)
                        if q >= 2:
                            act.wait_ge(s_ab, q - 1)
                        nc.scalar.sign(sg[:, q % 2, 0:n], wn[q % 2][:, 0:n]).then_inc(s_sg, 1)

                @block.vector
                def _(dve):
                    st = Steps(dve, s_own)
                    for q, (src, j, n, dst) in enumerate(pieces):
                        w, s = wn[q % 2][:, 0:n], sg[:, q % 2, 0:n]
                        mean = small[:, 250:251]
                        dve.wait_ge(s_ld[q % 2], 16 * (q // 2) + 16)
                        st.link(nc.vector.tensor_reduce(mean, w, AX.X, ALU.add, apply_absolute_value=True))
                        st.link(nc.vector.tensor_scalar(mean, mean, 1.0 / n, None, ALU.mult))
                        dve.wait_ge(s_sg, q + 1)
                        st.link(nc.vector.scalar_tensor_tensor(out=s, in0=s, scalar=mean, in1=w, op0=ALU.mult,
                                                               op1=ALU.subtract))
                        nc.vector.tensor_tensor(w, w, s, ALU.add).then_inc(s_ab, 1)
                        dve.wait_ge(s_ab, q + 1)
                        if q:
                            evac(dve, q - 1)
                    evac(dve, len(pieces) - 1)

                @block.tensor
                def _(pe):
                    for q, (src, j, n, dst) in enumerate(pieces):
                        pe.wait_ge(s_ab, q + 1)
                        if q >= 2:
                            pe.wait_ge(s_ev, sum(p[2] // 512 for p in pieces[:q - 1]))
                        for k in range(n // 128):
                            m = nc.tensor.transpose(bank[2 * (q % 2) + k // 4][:, (k % 4) * 128:(k % 4 + 1) * 128],
                                                    wn[q % 2][:, k * 128:(k + 1) * 128], ident[:, :])
                            if k % 4 == 3:
                                m.then_inc(s_trb, 1)
                        pe.wait_ge(s_trb, sum(p[2] // 512 for p in pieces[:q + 1]))
                        pe.sem_inc(s_tr, 1)

        feat_major = lambda x, k: x.rearrange("p (k n) -> p k n", k=k)
        ctx_side = featB, feat_major(bigB_r[:, 0:KD * N], KD), featA_r[:, :, :], KD
        gat_side = gatT, feat_major(stage_r[3][:, 0:2 * N], 2), feat_major(stage_r[0][:, 0:2 * N], 2), 2
        phase_start()
        if stop >= 1:
            phase_norm("n0", load=A["x"], store=XN)
        if stop >= 2:
            phase_h0()
        if stop >= 3:
            phase_edges0()
        if stop >= 4:
            phase_agg0()
        if stop >= 5:
            phase_mix("m0", True)
        if stop >= 6:
            phase_out("o0", [ctx_side], KD, A["L0_mix_bo"], XN)
        if stop >= 7:
            phase_norm("na", gain=(A["L0_mix_g1"], A["L0_mix_be1"]), keep=True, eps=1e-12)
        if stop >= 8:
            phase_up("u0", None, COLS["L0_mix_b1"][0])
        if stop >= 9:
            phase_down("d0", None, A["L0_mix_b2"])
        if stop >= 10:
            phase_norm("nb", gain=(A["L0_mix_g2"], A["L0_mix_be2"]), add=XR, keep=True, turn=False, eps=1e-12)
        if stop >= 11:
            phase_norm("n1", keep_sum=True)
        if stop >= 12:
            phase_route()
        if stop >= 13:
            phase_moe()
            recycle()
        if stop >= 14:
            phase_norm("n2", tok=tokB, store_src=XR, rms=160)
        if stop >= 15:
            phase_gat_in()
        if stop >= 16:
            phase_mix("m1", False)
        if stop >= 17:
            phase_gat()
        if stop >= 18:
            phase_out("o1", [ctx_side, gat_side], KD + 2, A["L1_mix_b_proj"], XR)
        if stop >= 19:
            phase_norm("n3")
            phase_binarize()
            phase_up("u1", lambda m: w1T[:, :, m * 128:(m + 1) * 128], COLS["L1_ffn_b1"][0])
        if stop >= 20:
            phase_down("d1", lambda c: w2T[:, :, c * 512:(c + 1) * 512], A["L1_ffn_b2"], dram=out)
        if stop < 20:
            with nc.Block() as block:
                @block.sync
                def _(sp):
                    for i in range(2):
                        if fulls[i]:
                            sp.wait_ge(w_full[i], fulls[i][-1])


def kernel(**inputs):
    import numpy as _np
    import concourse.bacc as _bacc
    from concourse import mybir as _mybir
    from concourse.bass_utils import run_bass_kernel_spmd as _run

    nc = _bacc.Bacc("TRN2", target_bir_lowering=False, num_devices=1)
    given = {name: _np.asarray(a) for name, a in inputs.items()}
    given["L1_gnn_att_row"] = given["L1_gnn_att"].reshape(-1)
    arrays, aps = {}, {}
    for name, a in given.items():
        if name in COLS:
            a = a.reshape(-1, 128).T
        a = _np.ascontiguousarray(a)
        arrays[f"in_{name}"] = a
        aps[name] = nc.dram_tensor(f"in_{name}", a.shape, _mybir.dt.from_np(a.dtype), kind="ExternalInput").ap()
    out = nc.dram_tensor("out", (N, D), F32, kind="ExternalOutput").ap()
    build(nc, aps, out)
    return _run(nc, [arrays], core_ids=[0]).results[0]["out"]
```
